# Optimizing a Trainium2 kernel written in Bass

```python
import numpy as np
import jax
import jax.numpy as jnp

def _softmax(x, axis=-1):
    return jax.nn.softmax(x, axis=axis)

def _gelu(x):
    return jax.nn.gelu(x, approximate=True)

def _silu(x):
    return jax.nn.silu(x)

def _sigmoid(x):
    return jax.nn.sigmoid(x)

def _layernorm(x, axis=-1, eps=1e-05):
    m = jnp.mean(x, axis=axis, keepdims=True)
    v = jnp.var(x, axis=axis, keepdims=True)
    return (x - m) / jnp.sqrt(v + eps)

def _scatter_add(tgt, idx, src, axis=0):
    return tgt.at[idx].add(src)

def _segment_sum(src, seg, n):
    return jax.ops.segment_sum(src, seg, n)
kernel_name = 'mk_flamingo_gated_d2_seqx_r8_3b1b01'

def setup_inputs(seed: int=0):
    np.random.seed(seed)
    _w = jnp.asarray

    def _rec_inputs():
        import jax
        import jax.numpy as jnp
        _rk = jax.random.key(seed)
        x = -0.0003929 + 0.9999 * jax.random.normal(jax.random.fold_in(_rk, 1), (16, 64, 512), jnp.float32)
        _lenS = 64 - jax.random.randint(jax.random.fold_in(_rk, 7), (16,), 0, max(1, 64 // 4) + 1, jnp.int32)
        _lenS2 = 64 - jax.random.randint(jax.random.fold_in(_rk, 8), (16,), 0, max(1, 64 // 4) + 1, jnp.int32)
        _ctx_4096P = jax.random.normal(jax.random.fold_in(_rk, 11), (16, 16, 512), jnp.float32)
        _ctx_4096c = jax.random.dirichlet(jax.random.fold_in(_rk, 511), 0.3 * jnp.ones((16,), jnp.float32), (16, 64))
        _ctx_4096t = jnp.einsum('bsk,bkd->bsd', _ctx_4096c, _ctx_4096P)
        _ctx_4096t = _ctx_4096t * jax.lax.rsqrt(jnp.mean(jnp.square(_ctx_4096t)) + 1e-12) * 0.953939
        ctx_4096 = 2.81802e-05 + 1.00001 * (_ctx_4096t + 0.3 * jax.random.normal(jax.random.fold_in(_rk, 611), (16, 64, 512), jnp.float32))
        pos_BxS2 = jnp.broadcast_to(jnp.arange(64, dtype=jnp.int32), (16, 64))
        _validS = jnp.arange(64)[None, :] < _lenS[:, None]
        _validS2 = jnp.arange(64)[None, :] < _lenS2[:, None]
        _causal = jnp.tril(jnp.ones((64, 64), dtype=bool))
        mask_BxSxS2_ik0 = jnp.where(jnp.broadcast_to(_validS2[:, None, :], (16, 64, 64)), 0, 1).astype(jnp.int32)
        mask_BxSxS2_ff0 = jnp.where(jnp.ones((16, 64, 64), dtype=bool), 0.0, -1000000000.0).astype(jnp.float32)
        _g = jax.random.normal(jax.random.fold_in(_rk, 9001), (2, 2), jnp.float32)
        _g = jnp.sign(_g) * jnp.maximum(jnp.abs(_g), 1.0) + (_g == 0) * 1.0
        g_xattn = _g[0]
        g_ffn = _g[1]
        return (x, ctx_4096, pos_BxS2, mask_BxSxS2_ik0, mask_BxSxS2_ff0, g_xattn, g_ffn)
    x, ctx_4096, pos_BxS2, mask_BxSxS2_ik0, mask_BxSxS2_ff0, g_xattn, g_ffn = _rec_inputs()

    def _L0_xattn_setup():
        import jax, jax.numpy as jnp
        import numpy as np
        B, S, E = (2, 256, 512)
        H, KVH, D = (32, 8, 128)
        GROUPS = H // KVH
        MAX_POS = 512
        ROPE_THETA = 10000.0

        def _rope_tables(max_pos, dim, theta):
            inv_freq = 1.0 / theta ** (jnp.arange(0, dim, 2, dtype=jnp.float32) / dim)
            t = jnp.arange(max_pos, dtype=jnp.float32)
            freqs = jnp.einsum('i,j->ij', t, inv_freq)
            emb = jnp.concatenate([freqs, freqs], axis=-1)
            return (jnp.cos(emb), jnp.sin(emb))

        def _rotate_half(x):
            x1, x2 = (x[..., :x.shape[-1] // 2], x[..., x.shape[-1] // 2:])
            return jnp.concatenate([-x2, x1], axis=-1)
        key = jax.random.key(seed)
        ks = jax.random.split(key, 8)
        scale_w = 1.0 / np.sqrt(E)
        query = jax.random.normal(ks[0], (B, S, E), dtype=jnp.float32)
        k_in = jax.random.normal(ks[1], (B, S, E), dtype=jnp.float32)
        v_in = jax.random.normal(ks[2], (B, S, E), dtype=jnp.float32)
        position_ids = jnp.broadcast_to(jnp.arange(S, dtype=jnp.int64), (B, S))
        src_mask = jnp.tril(jnp.ones((S, S), dtype=jnp.int32))
        src_mask = jnp.broadcast_to(src_mask, (B, S, S))
        Wq = jax.random.normal(ks[3], (E, H * D), dtype=jnp.float32) * scale_w
        Wk = jax.random.normal(ks[4], (E, KVH * D), dtype=jnp.float32) * scale_w
        Wv = jax.random.normal(ks[5], (E, KVH * D), dtype=jnp.float32) * scale_w
        Wo = jax.random.normal(ks[6], (H * D, E), dtype=jnp.float32) * scale_w
        return {'query': query, 'key': k_in, 'value': v_in, 'position_ids': position_ids, 'src_mask': src_mask, 'Wq': Wq, 'Wk': Wk, 'Wv': Wv, 'Wo': Wo}
    _L0_xattn_all = _L0_xattn_setup()
    _L0_xattn_in = {k: v for k, v in _L0_xattn_all.items() if k in ('Wq', 'Wk', 'Wv', 'Wo')}
    del _L0_xattn_all

    def _L0_ffn_setup():
        import jax, jax.numpy as jnp
        import numpy as np
        ALPHA = 32
        R = 16
        SCALING = ALPHA / R
        key = jax.random.key(seed)
        k1, k2, k3, k4 = jax.random.split(key, 4)
        B_, S, D = (4, 256, 512)
        H, r, O = (8, R, 512)
        x = jax.random.normal(k1, (B_, S, D), dtype=jnp.float32)
        A = jax.random.normal(k2, (H, r, D), dtype=jnp.float32) * 0.02
        Bm = jax.random.normal(k3, (H, O, r), dtype=jnp.float32) * 0.02
        Wr = jax.random.normal(k4, (H, D), dtype=jnp.float32) * 0.02
        br = jnp.zeros((H,), dtype=jnp.float32)
        return {'x': x, 'A': A, 'B': Bm, 'Wr': Wr, 'br': br}
    _L0_ffn_all = _L0_ffn_setup()
    _L0_ffn_in = {k: v for k, v in _L0_ffn_all.items() if k in ('A', 'B', 'Wr', 'br')}
    del _L0_ffn_all

    def _L1_xattn_setup():
        import jax, jax.numpy as jnp
        import numpy as np
        BS, SEQ, D_MODEL = (4, 128, 512)
        N_Q_HEADS, N_KV_HEADS, D_K, D_V = (32, 8, 128, 128)
        ROPE_BASE = 10000.0

        def _rotate_half(x):
            x1, x2 = jnp.split(x, 2, axis=-1)
            return jnp.concatenate([-x2, x1], axis=-1)

        def _apply_rope(x, pos0):
            d = x.shape[-1]
            seq = x.shape[2]
            inv_freq = 1.0 / ROPE_BASE ** (jnp.arange(0, d, 2, dtype=jnp.float32) / d)
            pos = (pos0 + jnp.arange(seq)).astype(jnp.float32)
            ang = pos[:, None] * inv_freq[None, :]
            cos = jnp.concatenate([jnp.cos(ang), jnp.cos(ang)], axis=-1)
            sin = jnp.concatenate([jnp.sin(ang), jnp.sin(ang)], axis=-1)
            return x * cos[None, None] + _rotate_half(x) * sin[None, None]
        key = jax.random.key(seed)
        ks = jax.random.split(key, 8)
        w_scale = 0.02
        return {'query': jax.random.normal(ks[0], (BS, SEQ, D_MODEL), dtype=jnp.float32), 'key': jax.random.normal(ks[1], (BS, SEQ, D_MODEL), dtype=jnp.float32), 'value': jax.random.normal(ks[2], (BS, SEQ, D_MODEL), dtype=jnp.float32), 'mask': jnp.zeros((BS, SEQ, SEQ), dtype=jnp.float32), 'wq': jax.random.normal(ks[3], (D_MODEL, N_Q_HEADS * D_K), dtype=jnp.float32) * w_scale, 'wk': jax.random.normal(ks[4], (D_MODEL, N_KV_HEADS * D_K), dtype=jnp.float32) * w_scale, 'wv': jax.random.normal(ks[5], (D_MODEL, N_KV_HEADS * D_V), dtype=jnp.float32) * w_scale, 'wo': jax.random.normal(ks[6], (N_Q_HEADS * D_V, D_MODEL), dtype=jnp.float32) * w_scale, 'curr_seq_pos': 0}
    _L1_xattn_all = _L1_xattn_setup()
    _L1_xattn_in = {k: v for k, v in _L1_xattn_all.items() if k in ('wq', 'wk', 'wv', 'wo')}
    del _L1_xattn_all

    def _L1_ffn_setup():
        import jax, jax.numpy as jnp
        import numpy as np
        H, FF = (512, 1792)
        B, S = (4, 256)
        key = jax.random.key(seed)
        ks = jax.random.split(key, 7)
        x = jax.random.normal(ks[0], (B, S, H), dtype=jnp.float32)
        gate_t = jax.random.randint(ks[1], (FF, H), -1, 2, dtype=jnp.int32)
        up_t = jax.random.randint(ks[2], (FF, H), -1, 2, dtype=jnp.int32)
        down_t = jax.random.randint(ks[3], (H, FF), -1, 2, dtype=jnp.int32)
        gate_s = jax.random.uniform(ks[4], (FF,), jnp.float32, 0.01, 0.1)
        up_s = jax.random.uniform(ks[5], (FF,), jnp.float32, 0.01, 0.1)
        down_s = jax.random.uniform(ks[6], (H,), jnp.float32, 0.01, 0.1)
        return {'x': x, 'gate_t': gate_t, 'up_t': up_t, 'down_t': down_t, 'gate_s': gate_s, 'up_s': up_s, 'down_s': down_s}
    _L1_ffn_all = _L1_ffn_setup()
    _L1_ffn_in = {k: v for k, v in _L1_ffn_all.items() if k in ('gate_t', 'up_t', 'down_t', 'gate_s', 'up_s', 'down_s')}
    del _L1_ffn_all
    return {'x': x, 'ctx_4096': ctx_4096, 'pos_BxS2': pos_BxS2, 'mask_BxSxS2_ik0': mask_BxSxS2_ik0, 'mask_BxSxS2_ff0': mask_BxSxS2_ff0, 'g_xattn': g_xattn, 'g_ffn': g_ffn, 'L0_xattn_Wq': _L0_xattn_in['Wq'], 'L0_xattn_Wk': _L0_xattn_in['Wk'], 'L0_xattn_Wv': _L0_xattn_in['Wv'], 'L0_xattn_Wo': _L0_xattn_in['Wo'], 'L0_ffn_A': _L0_ffn_in['A'], 'L0_ffn_B': _L0_ffn_in['B'], 'L0_ffn_Wr': _L0_ffn_in['Wr'], 'L0_ffn_br': _L0_ffn_in['br'], 'L1_xattn_wq': _L1_xattn_in['wq'], 'L1_xattn_wk': _L1_xattn_in['wk'], 'L1_xattn_wv': _L1_xattn_in['wv'], 'L1_xattn_wo': _L1_xattn_in['wo'], 'L1_ffn_gate_t': _L1_ffn_in['gate_t'], 'L1_ffn_up_t': _L1_ffn_in['up_t'], 'L1_ffn_down_t': _L1_ffn_in['down_t'], 'L1_ffn_gate_s': _L1_ffn_in['gate_s'], 'L1_ffn_up_s': _L1_ffn_in['up_s'], 'L1_ffn_down_s': _L1_ffn_in['down_s']}

def reference(x, ctx_4096, pos_BxS2, mask_BxSxS2_ik0, mask_BxSxS2_ff0, g_xattn, g_ffn, L0_xattn_Wq, L0_xattn_Wk, L0_xattn_Wv, L0_xattn_Wo, L0_ffn_A, L0_ffn_B, L0_ffn_Wr, L0_ffn_br, L1_xattn_wq, L1_xattn_wk, L1_xattn_wv, L1_xattn_wo, L1_ffn_gate_t, L1_ffn_up_t, L1_ffn_down_t, L1_ffn_gate_s, L1_ffn_up_s, L1_ffn_down_s):
    import jax
    import jax.numpy as jnp

    def _L0_xattn_ref(query, key, value, position_ids, src_mask, Wq, Wk, Wv, Wo):
        import jax, jax.numpy as jnp
        import numpy as np
        B, S, E = (2, 256, 512)
        H, KVH, D = (32, 8, 128)
        GROUPS = H // KVH
        MAX_POS = 512
        ROPE_THETA = 10000.0

        def _rope_tables(max_pos, dim, theta):
            inv_freq = 1.0 / theta ** (jnp.arange(0, dim, 2, dtype=jnp.float32) / dim)
            t = jnp.arange(max_pos, dtype=jnp.float32)
            freqs = jnp.einsum('i,j->ij', t, inv_freq)
            emb = jnp.concatenate([freqs, freqs], axis=-1)
            return (jnp.cos(emb), jnp.sin(emb))

        def _rotate_half(x):
            x1, x2 = (x[..., :x.shape[-1] // 2], x[..., x.shape[-1] // 2:])
            return jnp.concatenate([-x2, x1], axis=-1)
        nb, q_len, _ = query.shape
        q = (query @ Wq).reshape(nb, q_len, H, D).transpose(0, 2, 1, 3)
        k = (key @ Wk).reshape(nb, q_len, KVH, D).transpose(0, 2, 1, 3)
        v = (value @ Wv).reshape(nb, q_len, KVH, D).transpose(0, 2, 1, 3)
        cos_t, sin_t = _rope_tables(MAX_POS, D, ROPE_THETA)
        cos = cos_t[position_ids][:, None]
        sin = sin_t[position_ids][:, None]
        q = q * cos + _rotate_half(q) * sin
        k = k * cos + _rotate_half(k) * sin
        k = jnp.repeat(k, GROUPS, axis=1)
        v = jnp.repeat(v, GROUPS, axis=1)
        scores = jnp.einsum('bhqd,bhkd->bhqk', q, k) / jnp.sqrt(jnp.float32(D))
        mask = src_mask[:, None]
        scores = jnp.where(mask == 0, jnp.float32(-1000000000.0), scores)
        attn = jax.nn.softmax(scores, axis=-1)
        x = jnp.einsum('bhqk,bhkd->bhqd', attn, v)
        x = x.transpose(0, 2, 1, 3).reshape(nb, q_len, H * D)
        return x @ Wo

    def _L0_ffn_ref(x, A, B, Wr, br):
        import jax, jax.numpy as jnp
        import numpy as np
        ALPHA = 32
        R = 16
        SCALING = ALPHA / R
        H = A.shape[0]
        router_logits = jnp.einsum('bsd,hd->bsh', x, Wr) + br
        scores = H * jax.nn.softmax(router_logits, axis=-1)
        low = jnp.einsum('bsd,hrd->bshr', x, A)
        out = jnp.einsum('bshr,hor,bsh->bso', low, B, scores)
        return SCALING * out

    def _L1_xattn_ref(query, key, value, mask, wq, wk, wv, wo, curr_seq_pos):
        import jax, jax.numpy as jnp
        import numpy as np
        BS, SEQ, D_MODEL = (4, 128, 512)
        N_Q_HEADS, N_KV_HEADS, D_K, D_V = (32, 8, 128, 128)
        ROPE_BASE = 10000.0

        def _rotate_half(x):
            x1, x2 = jnp.split(x, 2, axis=-1)
            return jnp.concatenate([-x2, x1], axis=-1)

        def _apply_rope(x, pos0):
            d = x.shape[-1]
            seq = x.shape[2]
            inv_freq = 1.0 / ROPE_BASE ** (jnp.arange(0, d, 2, dtype=jnp.float32) / d)
            pos = (pos0 + jnp.arange(seq)).astype(jnp.float32)
            ang = pos[:, None] * inv_freq[None, :]
            cos = jnp.concatenate([jnp.cos(ang), jnp.cos(ang)], axis=-1)
            sin = jnp.concatenate([jnp.sin(ang), jnp.sin(ang)], axis=-1)
            return x * cos[None, None] + _rotate_half(x) * sin[None, None]
        bs, sq, _ = query.shape
        n_groups = N_Q_HEADS // N_KV_HEADS
        q = (query @ wq).reshape(bs, sq, N_Q_HEADS, D_K).transpose((0, 2, 1, 3))
        sk = key.shape[1]
        k = (key @ wk).reshape(bs, sk, N_KV_HEADS, 1, D_K)
        k = jnp.repeat(k, n_groups, axis=3).reshape(bs, sk, N_Q_HEADS, D_K).transpose((0, 2, 1, 3))
        v = (value @ wv).reshape(bs, sk, N_KV_HEADS, 1, D_V)
        v = jnp.repeat(v, n_groups, axis=3).reshape(bs, sk, N_Q_HEADS, D_V).transpose((0, 2, 1, 3))
        scale = jnp.sqrt(jnp.float32(D_K))
        q = _apply_rope(q, curr_seq_pos)
        k = _apply_rope(k, curr_seq_pos)
        raw = jnp.einsum('bhqd,bhkd->bhqk', q, k) / scale
        masked = raw + mask[:bs, None, curr_seq_pos:curr_seq_pos + sq, :sk]
        attn = jax.nn.softmax(masked, axis=-1)
        out = jnp.einsum('bhqk,bhkd->bhqd', attn, v)
        out = out.transpose((0, 2, 1, 3)).reshape(bs, sq, N_Q_HEADS * D_V)
        return out @ wo

    def _L1_ffn_ref(x, gate_t, up_t, down_t, gate_s, up_s, down_s):
        import jax, jax.numpy as jnp
        import numpy as np
        H, FF = (512, 1792)
        B, S = (4, 256)
        Bb, Ss, Hh = x.shape
        x_flat = x.reshape(Bb * Ss, Hh)
        gate_w = gate_t.astype(jnp.float32) * gate_s[:, None]
        up_w = up_t.astype(jnp.float32) * up_s[:, None]
        down_w = down_t.astype(jnp.float32) * down_s[:, None]
        gate_out = x_flat @ gate_w.T
        up_out = x_flat @ up_w.T
        hidden = jax.nn.silu(gate_out) * up_out
        out_flat = hidden @ down_w.T
        return out_flat.reshape(Bb, Ss, -1)
    x = x + jnp.tanh(g_xattn[0]) * _L0_xattn_ref(_layernorm(x, axis=-1), ctx_4096, ctx_4096, pos_BxS2, mask_BxSxS2_ik0, L0_xattn_Wq, L0_xattn_Wk, L0_xattn_Wv, L0_xattn_Wo)
    x = x + jnp.tanh(g_ffn[0]) * _L0_ffn_ref(_layernorm(x, axis=-1), L0_ffn_A, L0_ffn_B, L0_ffn_Wr, L0_ffn_br)
    x = x + jnp.tanh(g_xattn[1]) * _L1_xattn_ref(_layernorm(x, axis=-1), ctx_4096, ctx_4096, mask_BxSxS2_ff0, L1_xattn_wq, L1_xattn_wk, L1_xattn_wv, L1_xattn_wo, 0)
    x = x + jnp.tanh(g_ffn[1]) * _L1_ffn_ref(_layernorm(x, axis=-1), L1_ffn_gate_t, L1_ffn_up_t, L1_ffn_down_t, L1_ffn_gate_s, L1_ffn_up_s, L1_ffn_down_s)
    return x

_drawn_inputs = setup_inputs


def setup_inputs(seed=0):
    import zlib

    import numpy as np

    out = dict(_drawn_inputs(seed))
    spreads = {'g_ffn': (-1.0, 0.2), 'L0_ffn_br': (0.0, 0.408)}
    factors = {'L1_xattn_wq': 3.853, 'L1_xattn_wk': 3.905}
    for name, (base, spread) in spreads.items():
        noise = np.random.default_rng([zlib.crc32(name.encode()), seed]).standard_normal(out[name].shape)
        drawn = base * np.exp(spread * noise) if base else spread * noise
        out[name] = jnp.asarray(drawn.astype(out[name].dtype))
    for name, factor in factors.items():
        out[name] = (out[name] * factor).astype(out[name].dtype)
    return out
```

```python
from contextlib import ExitStack

import concourse.bass as bass
from concourse import mybir

P = 128
F32 = mybir.dt.float32
F32R = mybir.dt.float32r
I32 = mybir.dt.int32
U8 = mybir.dt.uint8
ALU = mybir.AluOpType
ACT = mybir.ActivationFunctionType
AX_X = mybir.AxisListType.X

BATCH, SEQ, DM = 16, 64, 512
TOK = BATCH * SEQ
NT = TOK // P
KC = DM // P
HALF = TOK // 2
D = 128
NG, HPG = 8, 4
SCALE = float(D) ** -0.5
MAX_POS = 512
EPS = 1e-5
FF = 1792
FFT = FF // P
NFP = FFT // 2
RH, RR = 8, 16


class Group:

    def __init__(self, added, register=None):
        self.added, self.register = added, register

    def __add__(self, n):
        return Group(self.added + n, self.register)

    def valid(self):
        return self.register is not None or 0 <= self.added < NG

    def number(self, per_group, c):
        c += self.added * per_group
        return c if self.register is None else self.register * per_group + c

    def count(self, per_group, c):
        assert self.register is None or (1 + self.added) * per_group + c > 0
        return self.number(per_group, c)


def wait_count(eng, sem, g, per_group, c):
    value = g.count(per_group, c)
    if not isinstance(value, int) or value > 0:
        eng.wait_ge(sem, value)


def back(g, t):
    return (g, t - 1) if t else (g + -1, NT - 1)


def ahead(g, t):
    return (g, t + 1) if t < NT - 1 else (g + 1, 0)


PROJ = {
    2: [("q", 0, 0)],
    3: [("q", 1, 0), ("v", 0, None)],
    4: [("q", 2, 0), ("k", 0, 0)],
    5: [("q", 3, 0), ("v", 1, None)],
    6: [("q", 0, 1)],
    7: [("q", 1, 1), ("v", 2, None)],
    0: [("q", 2, 1), ("k", 0, 1)],
    1: [("q", 3, 1), ("v", 3, None)],
}
STEPS = [2, 3, 4, 5, 6, 7, 0, 1]
UNITS = [u for t in STEPS for u in PROJ[t]]
ROPES = [u for u in UNITS if u[0] != "v"]
NU, NR = len(UNITS), len(ROPES)
FIRST_HALF_ROPES = sum(u[2] == 0 for u in ROPES)
SPLIT_Q = {7: (2, 0), 0: (1, 1), 1: (1, 2), 2: (1, 3)}
PASSES = ((0, 0), (0, 1), (1, 0))


def proj_group(g, t):
    return g + 1 if t >= 2 else g


class Chip:

    def __init__(self, nc, ctx):
        self.nc, self.ctx = nc, ctx

    def sb(self, name, shape, dt=F32):
        return self.ctx.enter_context(self.nc.sbuf_tensor(name, shape, dt))

    def bank(self, name):
        return self.ctx.enter_context(self.nc.psum_tensor(name, [P, 512], F32))

    def sem(self, name):
        return self.ctx.enter_context(self.nc.semaphore(name))


def load_phase(nc, sems, ctx_in, x_in, pos_in, tab_in, tab1_in, gx_in, gf_in, x_res, ctxT, ctx_parts, cos0, sin0,
               rope1, gates, ident):
    with ExitStack() as c:
        m = Chip(nc, c)
        ctx_nat = m.sb("ctx_nat", [P, NT, DM])
        pos_i = m.sb("pos_i", [P, TOK], I32)
        posf = m.sb("posf", [P, TOK])
        wrap = m.sb("wrap", [P, TOK])
        rowid_i = m.sb("rowid_i", [P, MAX_POS // P], I32)
        rowid = m.sb("rowid", [P, MAX_POS // P])
        onehot = m.sb("onehot", [P, MAX_POS // P, TOK], F32R)
        tab = m.sb("tab", [P, MAX_POS // P, 2, D])
        tab_hi = m.sb("tab_hi", [P, MAX_POS // P, 2, D], F32R)
        tab_lo = m.sb("tab_lo", [P, MAX_POS // P, 2, D], F32R)
        gate_raw = m.sb("gate_raw", [P, 4])
        tr = [m.bank(f"ld_tr{i}") for i in range(4)]
        tb = [m.bank(f"ld_tb{i}") for i in range(4)]
        x_in_s, ctx_loaded, pos_loaded, tab_loaded, rope_loaded, gate_loaded = (
            sems("ld_" + n) for n in ("x", "ctx", "pos", "tab", "rope", "gate"))
        ident_zero, ident_ready, rowid_ready = (sems("ld_" + n) for n in ("id0", "id1", "rowid"))
        ctx_tr, ctx_raw, ctx_hi, ctx_lo = (sems("ld_" + n) for n in ("ctx_tr", "ctx_raw", "ctx_hi", "ctx_lo"))
        tab_hi_ready, tab_lo_ready, pos_step, onehot_ready, tab_mm, gate_done = (
            sems("ld_" + n) for n in ("tab_hi", "tab_lo", "pos_step", "onehot", "tab_mm", "gates"))
        block = c.enter_context(nc.Block())

        @block.sync
        def _(sp):
            for t in range(NT):
                sp.dma_start(ctx_nat[:, t, :], ctx_in[t * P:(t + 1) * P, :]).then_inc(ctx_loaded[t], 16)
            for t in range(NT):
                sp.dma_start(x_res[:, t, :], x_in[t * P:(t + 1) * P, :]).then_inc(x_in_s, 16)
            sp.dma_start(rope1[:], tab1_in).then_inc(rope_loaded, 16)
            sp.wait_ge(x_in_s, 16 * NT)
            sp.wait_ge(rope_loaded, 16)

        @block.scalar
        def _(act):
            act.dma_start(pos_i[:], pos_in).then_inc(pos_loaded, 16)
            act.dma_start(tab[:], tab_in).then_inc(tab_loaded, 16)
            act.dma_start(gate_raw[:, 0:2], gx_in).then_inc(gate_loaded, 16)
            act.dma_start(gate_raw[:, 2:4], gf_in).then_inc(gate_loaded, 16)
            act.wait_ge(gate_loaded, 32)
            nc.scalar.activation(gates[:], gate_raw[:], ACT.Tanh).then_inc(gate_done, 1)
            for t in range(NT):
                act.wait_ge(ctx_tr, t + 1)
                raw = ctxT[:, :, t * P:(t + 1) * P]
                nc.scalar.activation(raw, tr[t % 4][:].rearrange("p (c n) -> p c n", c=KC), ACT.Copy).then_inc(ctx_raw, 1)
                act.wait_ge(ctx_raw, t + 1)
                nc.scalar.activation(ctx_parts[0][:, :, t * P:(t + 1) * P], raw, ACT.Copy).then_inc(ctx_hi, 1)

        @block.gpsimd
        def _(pool):
            nc.gpsimd.memset(ident[:], 0.0).then_inc(ident_zero, 1)
            pool.wait_ge(ident_zero, 1)
            nc.gpsimd.affine_select(out=ident[:], in_=ident[:], compare_op=ALU.not_equal, fill=1.0, base=0,
                                    pattern=[[-1, P]], channel_multiplier=1).then_inc(ident_ready, 1)
            nc.gpsimd.iota(rowid_i[:], pattern=[[P, MAX_POS // P]], base=0, channel_multiplier=1).then_inc(rowid_ready, 1)

        @block.vector
        def _(dve):
            dve.wait_ge(rowid_ready, 1)
            nc.vector.tensor_copy(rowid[:], rowid_i[:]).then_inc(pos_step, 1)
            dve.wait_ge(pos_loaded, 16)
            nc.vector.tensor_copy(posf[:], pos_i[:]).then_inc(pos_step, 1)
            dve.wait_ge(pos_step, 2)
            nc.vector.tensor_scalar(wrap[:], posf[:], 0.0, float(MAX_POS), ALU.is_lt, ALU.mult).then_inc(pos_step, 1)
            dve.wait_ge(pos_step, 3)
            nc.vector.tensor_tensor(posf[:], posf[:], wrap[:], ALU.add).then_inc(pos_step, 1)
            dve.wait_ge(pos_step, 4)
            nc.vector.tensor_scalar(wrap[:], posf[:], 0.0, float(MAX_POS - 1), ALU.max, ALU.min).then_inc(pos_step, 1)
            dve.wait_ge(pos_step, 5)
            for q in range(MAX_POS // P):
                nc.vector.tensor_scalar(onehot[:, q, :], wrap[:], rowid[:, q:q + 1], None, ALU.is_equal).then_inc(onehot_ready, 1)
            dve.wait_ge(tab_loaded, 16)
            nc.vector.tensor_copy(tab_hi[:], tab[:]).then_inc(tab_hi_ready, 1)
            dve.wait_ge(tab_hi_ready, 1)
            nc.vector.tensor_tensor(tab_lo[:], tab[:], tab_hi[:].bitcast(F32), ALU.subtract).then_inc(tab_lo_ready, 1)
            for t in range(NT):
                dve.wait_ge(ctx_hi, t + 1)
                nc.vector.tensor_tensor(ctx_parts[1][:, :, t * P:(t + 1) * P], ctxT[:, :, t * P:(t + 1) * P],
                                        ctx_parts[0][:, :, t * P:(t + 1) * P].bitcast(F32), ALU.subtract).then_inc(ctx_lo, 1)
            for n, dest in enumerate((cos0, sin0)):
                for h in range(2):
                    dve.wait_ge(tab_mm, 2 * n + h + 1)
                    nc.vector.tensor_copy(dest[:, h * HALF:(h + 1) * HALF], tb[2 * n + h][:]).then_inc(pos_step, 1)

        @block.tensor
        def _(pe):
            pe.wait_ge(ident_ready, 1)
            for t in range(NT):
                pe.wait_ge(ctx_loaded[t], 16)
                if t >= 4:
                    pe.wait_ge(ctx_raw, t - 3)
                for k in range(KC):
                    last = nc.tensor.transpose(tr[t % 4][:, k * P:(k + 1) * P], ctx_nat[:, t, k * P:(k + 1) * P], ident[:])
                last.then_inc(ctx_tr, 1)
            pe.wait_ge(onehot_ready, MAX_POS // P)
            pe.wait_ge(tab_lo_ready, 1)
            for n in range(2):
                for h in range(2):
                    steps = [(q, part) for q in range(MAX_POS // P) for part in (tab_hi, tab_lo)]
                    for i, (q, part) in enumerate(steps):
                        last = nc.tensor.matmul(tb[2 * n + h][:], part[:, q, n, :], onehot[:, q, h * HALF:(h + 1) * HALF],
                                                start=(i == 0), stop=(i == len(steps) - 1))
                    last.then_inc(tab_mm, 1)


def norm_phase(nc, sems, name, x_res, parts, raw, ident):
    with ExitStack() as c:
        m = Chip(nc, c)
        stats = m.sb(name + "stats", [P, NT, 6])
        mv = m.sb(name + "mv", [P, NT, 2])
        var_eps = m.sb(name + "var_eps", [P, NT])
        power = m.sb(name + "power", [P, NT])
        rstd = m.sb(name + "rstd", [P, NT])
        xn = m.sb(name + "xn", [P, 2, DM])
        tr = [m.bank(f"{name}tr{i}") for i in range(4)]
        stats_done, aggr_done, eps_done, power_ready, rstd_ready, xn_ready, tr_done, hi_ready, lo_ready = (
            sems(name + n) for n in ("stats", "aggr", "eps", "power", "rstd", "xn", "tr", "hi", "lo"))
        block = c.enter_context(nc.Block())

        @block.vector
        def _(dve):
            for t in range(NT):
                nc.vector.bn_stats(stats[:, t, :], x_res[:, t, :]).then_inc(stats_done, 1)
                dve.wait_ge(stats_done, t + 1)
                nc.vector.bn_aggr(mv[:, t, :], stats[:, t, :]).then_inc(aggr_done, 1)
            dve.wait_ge(aggr_done, NT)
            nc.vector.tensor_scalar(var_eps[:], mv[:, :, 1], EPS, None, ALU.add).then_inc(eps_done, 1)
            dve.wait_ge(rstd_ready, 1)

            def low_part(t):
                dve.wait_ge(hi_ready, t + 1)
                nc.vector.tensor_tensor(parts[1][:, :, t * P:(t + 1) * P], tr[t % 4][:].rearrange("p (c n) -> p c n", c=KC),
                                        parts[0][:, :, t * P:(t + 1) * P].bitcast(F32), ALU.subtract).then_inc(lo_ready, 1)

            for t in range(NT):
                if t >= 2:
                    dve.wait_ge(tr_done, t - 1)
                nc.vector.tensor_scalar(xn[:, t % 2, :], x_res[:, t, :], mv[:, t, 0:1], rstd[:, t:t + 1],
                                        ALU.subtract, ALU.mult).then_inc(xn_ready, 1)
                if t >= 1 and raw is None:
                    low_part(t - 1)
            if raw is None:
                low_part(NT - 1)

        @block.gpsimd
        def _(pool):
            nc.gpsimd.memset(power[:], -0.5).then_inc(power_ready, 1)
            pool.wait_ge(power_ready, 1)
            pool.wait_ge(eps_done, 1)
            nc.gpsimd.tensor_tensor(rstd[:], var_eps[:], power[:], ALU.pow).then_inc(rstd_ready, 1)

        @block.tensor
        def _(pe):
            for t in range(NT):
                pe.wait_ge(xn_ready, t + 1)
                if t >= 4:
                    pe.wait_ge(hi_ready if raw is not None else lo_ready, t - 3)
                for k in range(KC):
                    last = nc.tensor.transpose(tr[t % 4][:, k * P:(k + 1) * P], xn[:, t % 2, k * P:(k + 1) * P], ident[:])
                last.then_inc(tr_done, 1)

        @block.scalar
        def _(act):
            for t in range(NT):
                act.wait_ge(tr_done, t + 1)
                dest = parts[0] if raw is None else raw
                nc.scalar.activation(dest[:, :, t * P:(t + 1) * P], tr[t % 4][:].rearrange("p (c n) -> p c n", c=KC),
                                     ACT.Copy).then_inc(hi_ready, 1)


def attention_phase(nc, sems, name, wq, wk, wv, wo, mask_in, masked, cos, sin, gate, x_res, xn_parts, ctxT, ctx_parts, ident):
    with ExitStack() as c:
        m = Chip(nc, c)
        qT = m.sb(name + "qT", [P, BATCH, HPG, SEQ])
        kT = m.sb(name + "kT", [P, BATCH, SEQ])
        v = m.sb(name + "v", [P, NT, D])
        wq_raw = m.sb(name + "wq_raw", [P, 2, KC, D])
        wq_parts = [m.sb(f"{name}wq_{n}", [P, HPG, KC, D], F32R) for n in ("hi", "lo")]
        wk_raw = m.sb(name + "wk_raw", [P, KC, D])
        wk_parts = [m.sb(f"{name}wk_{n}", [P, KC, D], F32R) for n in ("hi", "lo")]
        wv_sb = m.sb(name + "wv_sb", [P, KC, D])
        wo_raw = m.sb(name + "wo_raw", [P, HPG, DM])
        wo_parts = [m.sb(f"{name}wo_{n}", [P, HPG, DM], F32R) for n in ("hi", "lo")]
        rot = m.sb(name + "rot", [P, 2, HALF])
        qcos = m.sb(name + "qcos", [P, HALF])
        sc = m.sb(name + "sc", [P, 256])
        prob = m.sb(name + "prob", [P, 2, 256])
        probT = m.sb(name + "probT", [P, 2, 256])
        oT_parts = [m.sb(f"{name}oT_{n}", [P, 2, HPG, 2, SEQ], F32R) for n in ("hi", "lo")]
        mx, total, inv = (m.sb(name + n, [P, 4]) for n in ("mx", "total", "inv"))
        if masked:
            x_mask = m.sb(name + "mask_i", [P, BATCH // 4, SEQ], I32)
            hidden, shown = (m.sb(name + n, [P, BATCH, SEQ], U8) for n in ("hidden", "shown"))
        else:
            x_mask = m.sb(name + "mask", [P, BATCH, SEQ])
        proj_bank = [m.bank(f"{name}proj{i}") for i in range(2)]
        s_bank, t_bank, o_bank = (m.bank(name + n) for n in ("s", "t", "o"))
        pv_bank = [m.bank(f"{name}pv{i}") for i in range(2)]

        wq_loaded = [sems(f"{name}wq_loaded{i}") for i in range(2)]
        wk_loaded, wv_loaded, wo_loaded, mask_loaded = (sems(name + n) for n in ("wk_loaded", "wv_loaded", "wo_loaded", "mask_loaded"))
        wq_hi, wq_lo, wk_hi, wk_lo, wo_hi, wo_lo_pool, wo_lo_dve = (
            sems(name + n) for n in ("wq_hi", "wq_lo", "wk_hi", "wk_lo", "wo_hi", "wo_lo_pool", "wo_lo_dve"))
        proj_done, s_done, t_done, pv_done, o_done = (sems(name + n) for n in ("proj_done", "s_done", "t_done", "pv_done", "o_done"))
        rot_ready, sin_done, cos_done, rope_done, v_ready = (
            sems(name + n) for n in ("rot_ready", "sin_done", "cos_done", "rope_done", "v_ready"))
        s_read, s_masked, mx_ready, shifted, exp_ready, total_ready, inv_ready, prob_ready = (
            sems(name + n) for n in ("s_read", "s_masked", "mx", "shifted", "exp", "total", "inv", "prob"))
        probT_ready, oT_hi, oT_lo, acc_done, mask_ready = (
            sems(name + n) for n in ("probT", "oT_hi", "oT_lo", "acc_done", "mask_ready"))

        wq_v = wq.rearrange("(c p) n -> p c n", p=P)
        wk_v = wk.rearrange("(c p) n -> p c n", p=P)
        wv_v = wv.rearrange("(c p) n -> p c n", p=P)

        def heads_of(unit):
            kind, h, half = unit
            b = slice(half * (BATCH // 2), (half + 1) * (BATCH // 2))
            return qT[:, b, h, :] if kind == "q" else kT[:, b, :]

        def by_batch(ap):
            return ap.rearrange("p (b s) -> p b s", s=SEQ)

        block = c.enter_context(nc.Block())

        @block.sync
        def _(sp):
            def load_wq(g, h):
                if g.valid():
                    wait_count(sp, wq_lo, g, HPG, h - 1)
                    sp.dma_start(wq_raw[:, h % 2], wq_v[:, :, bass.ds(g.number(HPG * D, h * D), D)]).then_inc(wq_loaded[h % 2], 16)

            def load_wk(g):
                if g.valid():
                    wait_count(sp, wk_lo, g, 1, 0)
                    sp.dma_start(wk_raw[:], wk_v[:, :, bass.ds(g.number(D, 0), D)]).then_inc(wk_loaded, 16)

            def load_wo(g):
                if g.valid():
                    wait_count(sp, wo_lo_pool, g, 2, 0)
                    wait_count(sp, wo_lo_dve, g, 2, 0)
                    for h in range(HPG):
                        sp.dma_start(wo_raw[:, h], wo[bass.ds(g.number(HPG * D, h * D), D), :]).then_inc(wo_loaded, 16)

            def step(g, t):
                if t == 2:
                    if (g + 1).valid():
                        wait_count(sp, proj_done, g, NU, NU)
                        sp.dma_start(wv_sb[:], wv_v[:, :, bass.ds((g + 1).number(D, 0), D)]).then_inc(wv_loaded, 16)
                    load_wq(g + 2, 0)
                    load_wq(g + 2, 1)
                elif t == 4:
                    load_wk(g + 2)
                elif t == 0:
                    load_wq(g + 1, 2)
                elif t == 1:
                    load_wq(g + 1, 3)
                    load_wo(g + 1)

            load_wq(Group(0), 0)
            load_wq(Group(0), 1)
            load_wk(Group(0))
            if masked:
                for q in range(4):
                    if q:
                        sp.wait_ge(mask_ready, 2 * q)
                    for half in range(2):
                        sp.dma_start(x_mask[half * SEQ:(half + 1) * SEQ], mask_in[4 * q:4 * q + 4].rearrange("b q k -> q b k"))\
                          .then_inc(mask_loaded, 16)
            else:
                for half in range(2):
                    sp.dma_start(x_mask[half * SEQ:(half + 1) * SEQ], mask_in.rearrange("b q k -> q b k")).then_inc(mask_loaded, 16)
            load_wq(Group(0), 2)
            load_wq(Group(0), 3)
            load_wo(Group(0))
            run_steps(sp, step)

        @block.tensor
        def _(pe):
            def project(g, t, which):
                if len(PROJ[t]) <= which or not proj_group(g, t).valid():
                    return
                g = proj_group(g, t)
                kind, h, half = PROJ[t][which]
                j = UNITS.index(PROJ[t][which])
                before, gb = (UNITS[j - 2], g) if j >= 2 else (UNITS[j - 2], g + -1)
                if before[0] == "v":
                    wait_count(pe, v_ready, gb, NT // 2, before[1] + 1)
                else:
                    wait_count(pe, cos_done, gb, NR, ROPES.index(before) + 1)
                out = proj_bank[j % 2]
                if kind == "v":
                    wait_count(pe, wv_loaded, g, 16, 16)
                    for i in range(2):
                        tile = 2 * h + i
                        for k in range(KC):
                            last = nc.tensor.matmul(out[:, i * D:(i + 1) * D], ctxT[:, k, tile * P:(tile + 1) * P], wv_sb[:, k, :],
                                                    start=(k == 0), stop=(k == KC - 1))
                else:
                    if kind == "q":
                        wait_count(pe, wq_lo, g, HPG, h + 1)
                        weights, moving = [w[:, h] for w in wq_parts], xn_parts
                    else:
                        wait_count(pe, wk_lo, g, 1, 1)
                        weights, moving = [w[:] for w in wk_parts], ctx_parts
                    for k in range(KC):
                        for n, (a, b) in enumerate(PASSES):
                            last = nc.tensor.matmul(out[:], weights[a][:, k, :], moving[b][:, k, half * HALF:(half + 1) * HALF],
                                                    start=(k == 0 and n == 0), stop=(k == KC - 1 and n == 2))
                last.then_inc(proj_done, 1)

            def scores(g, t):
                if not g.valid():
                    return
                wait_count(pe, rope_done, g, NR, NR if t >= NT // 2 else FIRST_HALF_ROPES)
                wait_count(pe, s_read, g, NT, t)
                for pair in range(HPG // 2):
                    for b2 in range(2):
                        b = 2 * t + b2
                        last = nc.tensor.matmul(s_bank[:, (2 * pair + b2) * SEQ:(2 * pair + b2 + 1) * SEQ],
                                                qT[:, b, 2 * pair:2 * pair + 2, :].rearrange("p h s -> p (h s)"), kT[:, b, :],
                                                start=True, stop=True)
                last.then_inc(s_done, 1)

            def transpose_probs(g, t):
                if not g.valid():
                    return
                wait_count(pe, prob_ready, g, NT, t + 1)
                wait_count(pe, probT_ready, g, NT, t)
                for pair in range(HPG // 2):
                    last = nc.tensor.transpose(t_bank[:, pair * P:(pair + 1) * P], prob[:, t % 2, pair * P:(pair + 1) * P], ident[:])
                last.then_inc(t_done, 1)

            def probs_values(g, t):
                if not g.valid():
                    return
                wait_count(pe, probT_ready, g, NT, t + 1)
                wait_count(pe, v_ready, g, NT // 2, t // 2 + 1)
                wait_count(pe, oT_lo, g, 2 * NT, 2 * t)
                for b2 in range(2):
                    rows = slice(b2 * SEQ, (b2 + 1) * SEQ)
                    last = nc.tensor.matmul(pv_bank[b2][:, 0:256], v[rows, t, :], probT[rows, t % 2, :], start=True, stop=True)
                last.then_inc(pv_done, 1)

            def output(g, t):
                if not g.valid():
                    return
                wait_count(pe, oT_lo, g, 2 * NT, 2 * t + 2)
                wait_count(pe, wo_lo_pool, g, 2, 2)
                wait_count(pe, wo_lo_dve, g, 2, 2)
                wait_count(pe, acc_done, g, NT, t)
                for h in range(HPG):
                    for n, (a, b) in enumerate(PASSES):
                        last = nc.tensor.matmul(o_bank[:], oT_parts[a][:, t % 2, h].rearrange("p b s -> p (b s)"), wo_parts[b][:, h, :],
                                                start=(h == 0 and n == 0), stop=(h == HPG - 1 and n == 2))
                last.then_inc(o_done, 1)

            def step(g, t):
                scores(*ahead(g, t))
                transpose_probs(g, t)
                project(g, t, 0)
                output(*back(g, t))
                probs_values(g, t)
                project(g, t, 1)

            run_steps(pe, step)

        @block.scalar
        def _(act):
            def rotate_or_copy(g, t, which):
                if len(PROJ[t]) <= which or not proj_group(g, t).valid():
                    return
                g = proj_group(g, t)
                unit = PROJ[t][which]
                bank = proj_bank[UNITS.index(unit) % 2]
                wait_count(act, proj_done, g, NU, UNITS.index(unit) + 1)
                if unit[0] == "v":
                    i = unit[1]
                    wait_count(act, pv_done, g + -1, NT, 2 * i + 2)
                    nc.scalar.activation(v[:, 2 * i:2 * i + 2, :], bank[:, 0:2 * D].rearrange("p (t d) -> p t d", d=D),
                                         ACT.Copy).then_inc(v_ready, 1)
                else:
                    r = ROPES.index(unit)
                    gb = g if r >= 2 else g + -1
                    wait_count(act, rope_done, gb, NR, r - 1 if r >= 2 else NR + r - 1)
                    nc.scalar.activation(rot[0:64, r % 2, :], bank[64:128, :], ACT.Copy).then_inc(rot_ready, 1)
                    nc.scalar.activation(rot[64:128, r % 2, :], bank[0:64, :], ACT.Copy).then_inc(rot_ready, 1)

            def exponentials(g, t):
                if not g.valid():
                    return
                wait_count(act, shifted, g, NT, t + 1)
                nc.scalar.activation(prob[:, t % 2, :], sc[:], ACT.Exp).then_inc(exp_ready, 1)

            def probs_out(g, t):
                if not g.valid():
                    return
                wait_count(act, t_done, g, NT, t + 1)
                nc.scalar.activation(probT[:, t % 2, :], t_bank[:, 0:256], ACT.Copy).then_inc(probT_ready, 1)

            def heads_high(g, t):
                if not g.valid():
                    return
                wait_count(act, pv_done, g, NT, t + 1)
                for b2 in range(2):
                    nc.scalar.activation(oT_parts[0][:, t % 2, :, b2, :], by_batch(pv_bank[b2][:, 0:256]), ACT.Copy).then_inc(oT_hi, 1)

            def split_wq(g, h):
                if not g.valid():
                    return
                wait_count(act, wq_loaded[h % 2], g, 32, 16 * (h // 2) + 16)
                wait_count(act, proj_done, g + -1, NU, UNITS.index(("q", h, 1)) + 1)
                nc.scalar.activation(wq_parts[0][:, h], wq_raw[:, h % 2], ACT.Copy).then_inc(wq_hi, 1)

            def split_wk(g):
                if not g.valid():
                    return
                wait_count(act, wk_loaded, g, 16, 16)
                wait_count(act, proj_done, g + -1, NU, UNITS.index(("k", 0, 1)) + 1)
                nc.scalar.activation(wk_parts[0][:], wk_raw[:], ACT.Copy).then_inc(wk_hi, 1)

            def split_wo(g):
                if not g.valid():
                    return
                wait_count(act, wo_loaded, g, 16 * HPG, 16 * HPG)
                wait_count(act, o_done, g, NT, 0)
                for h in (0, 2, 1, 3):
                    nc.scalar.activation(wo_parts[0][:, h], wo_raw[:, h], ACT.Copy).then_inc(wo_hi, 1)

            def step(g, t):
                gb, tb = back(g, t)
                heads_high(gb, tb)
                rotate_or_copy(gb, tb, 1)
                probs_out(g, t)
                exponentials(*ahead(g, t))
                rotate_or_copy(g, t, 0)
                if t in SPLIT_Q:
                    split_wq(g + SPLIT_Q[t][0], SPLIT_Q[t][1])
                if t == 3:
                    split_wk(g + 1)
                if t == 0:
                    split_wo(g)

            for h in range(3):
                split_wq(Group(0), h)
            run_steps(act, step)

        @block.gpsimd
        def _(pool):
            def times_sin(g, t, which):
                if len(PROJ[t]) <= which or PROJ[t][which][0] == "v" or not proj_group(g, t).valid():
                    return
                g = proj_group(g, t)
                unit = PROJ[t][which]
                r = ROPES.index(unit)
                wait_count(pool, rot_ready, g, 2 * NR, 2 * r + 2)
                nc.gpsimd.tensor_tensor(by_batch(rot[:, r % 2, :]), by_batch(rot[:, r % 2, :]), sin(unit[2]), ALU.mult).then_inc(sin_done, 1)

            def low_wq(g, h):
                if g.valid():
                    wait_count(pool, wq_hi, g, HPG, h + 1)
                    nc.gpsimd.tensor_tensor(wq_parts[1][:, h], wq_raw[:, h % 2], wq_parts[0][:, h].bitcast(F32),
                                            ALU.subtract).then_inc(wq_lo, 1)

            def low_wk(g):
                if g.valid():
                    wait_count(pool, wk_hi, g, 1, 1)
                    nc.gpsimd.tensor_tensor(wk_parts[1][:], wk_raw[:], wk_parts[0][:].bitcast(F32), ALU.subtract).then_inc(wk_lo, 1)

            def low_wo(g):
                if g.valid():
                    for i, h in enumerate((0, 1)):
                        wait_count(pool, wo_hi, g, HPG, 2 * i + 1)
                        nc.gpsimd.tensor_tensor(wo_parts[1][:, h], wo_raw[:, h], wo_parts[0][:, h].bitcast(F32),
                                                ALU.subtract).then_inc(wo_lo_pool, 1)

            def step(g, t):
                gb, tb = back(g, t)
                times_sin(gb, tb, 1)
                times_sin(g, t, 0)
                if t in SPLIT_Q:
                    low_wq(g + SPLIT_Q[t][0], SPLIT_Q[t][1])
                if t == 3:
                    low_wk(g + 1)
                if t == 0:
                    low_wo(g)

            for h in range(3):
                low_wq(Group(0), h)
            run_steps(pool, step)

        @block.vector
        def _(dve):
            if masked:
                for q in range(4):
                    dve.wait_ge(mask_loaded, 32 * (q + 1))
                    nc.vector.tensor_scalar(hidden[:, 4 * q:4 * q + 4, :], x_mask[:], 0, None, ALU.is_equal).then_inc(mask_ready, 1)
                    nc.vector.tensor_scalar(shown[:, 4 * q:4 * q + 4, :], x_mask[:], 0, None, ALU.not_equal).then_inc(mask_ready, 1)
                dve.wait_ge(mask_ready, 8)
            else:
                dve.wait_ge(mask_loaded, 32)

            def rotary(g, t, which):
                if len(PROJ[t]) <= which or PROJ[t][which][0] == "v" or not proj_group(g, t).valid():
                    return
                g = proj_group(g, t)
                unit = PROJ[t][which]
                r = ROPES.index(unit)
                bank = proj_bank[UNITS.index(unit) % 2]
                wait_count(dve, rot_ready, g, 2 * NR, 2 * r + 2)
                wait_count(dve, rope_done, g, NR, r)
                nc.vector.tensor_tensor(by_batch(qcos[:]), by_batch(bank[:]), cos(unit[2]), ALU.mult).then_inc(cos_done, 1)
                wait_count(dve, cos_done, g, NR, r + 1)
                wait_count(dve, sin_done, g, NR, r + 1)
                wait_count(dve, s_done, g + -1, NT, NT // 2 * (unit[2] + 1))
                nc.vector.tensor_tensor(heads_of(unit), by_batch(qcos[:]), by_batch(rot[:, r % 2, :]), ALU.add).then_inc(rope_done, 1)

            def softmax(g, t):
                if not g.valid():
                    return
                wait_count(dve, s_done, g, NT, t + 1)
                wait_count(dve, exp_ready, g, NT, t)
                b = slice(2 * t, 2 * t + 2)
                both_pairs = [P, 2, 2 * SEQ]
                pairs = sc[:].rearrange("p (a n) -> p a n", a=2)
                bank = s_bank[:, 0:256].rearrange("p (a n) -> p a n", a=2)

                def for_tile(mask):
                    return mask[:, b, :].rearrange("p b k -> p (b k)").unsqueeze(1).to_broadcast(both_pairs)

                if masked:
                    nc.vector.scalar_tensor_tensor(out=pairs, in0=bank, scalar=SCALE, in1=for_tile(shown),
                                                   op0=ALU.mult, op1=ALU.mult).then_inc(s_read, 1)
                    wait_count(dve, s_read, g, NT, t + 1)
                    nc.vector.scalar_tensor_tensor(out=pairs, in0=for_tile(hidden), scalar=-1e9, in1=pairs,
                                                   op0=ALU.mult, op1=ALU.add).then_inc(s_masked, 1)
                    wait_count(dve, s_masked, g, NT, t + 1)
                else:
                    nc.vector.scalar_tensor_tensor(out=pairs, in0=bank, scalar=SCALE, in1=for_tile(x_mask),
                                                   op0=ALU.mult, op1=ALU.add).then_inc(s_read, 1)
                    wait_count(dve, s_read, g, NT, t + 1)
                rows = [P, 4, SEQ]
                sc4 = by_batch(sc[:])
                pr4 = by_batch(prob[:, t % 2, :])
                nc.vector.reduce_max(mx[:], sc4, AX_X).then_inc(mx_ready, 1)
                wait_count(dve, mx_ready, g, NT, t + 1)
                nc.vector.tensor_tensor(sc4, sc4, mx[:].unsqueeze(2).to_broadcast(rows), ALU.subtract).then_inc(shifted, 1)
                wait_count(dve, exp_ready, g, NT, t + 1)
                nc.vector.reduce_sum(total[:], pr4, AX_X).then_inc(total_ready, 1)
                wait_count(dve, total_ready, g, NT, t + 1)
                nc.vector.reciprocal(inv[:], total[:]).then_inc(inv_ready, 1)
                wait_count(dve, inv_ready, g, NT, t + 1)
                nc.vector.tensor_tensor(pr4, pr4, inv[:].unsqueeze(2).to_broadcast(rows), ALU.mult).then_inc(prob_ready, 1)

            def heads_low(g, t):
                if not g.valid():
                    return
                for b2 in range(2):
                    wait_count(dve, oT_hi, g, 2 * NT, 2 * t + b2 + 1)
                    nc.vector.tensor_tensor(oT_parts[1][:, t % 2, :, b2, :], by_batch(pv_bank[b2][:, 0:256]),
                                            oT_parts[0][:, t % 2, :, b2, :].bitcast(F32), ALU.subtract).then_inc(oT_lo, 1)

            def accumulate(g, t):
                if not g.valid():
                    return
                wait_count(dve, o_done, g, NT, t + 1)
                nc.vector.scalar_tensor_tensor(out=x_res[:, t, :], in0=o_bank[:], scalar=gate, in1=x_res[:, t, :],
                                               op0=ALU.mult, op1=ALU.add).then_inc(acc_done, 1)

            def low_wo(g):
                if g.valid():
                    for i, h in enumerate((2, 3)):
                        wait_count(dve, wo_hi, g, HPG, 2 * i + 2)
                        nc.vector.tensor_tensor(wo_parts[1][:, h], wo_raw[:, h], wo_parts[0][:, h].bitcast(F32),
                                                ALU.subtract).then_inc(wo_lo_dve, 1)

            def step(g, t):
                gb, tb = back(g, t)
                heads_low(gb, tb)
                rotary(gb, tb, 1)
                softmax(*ahead(g, t))
                rotary(g, t, 0)
                accumulate(gb, tb)
                if t == 0:
                    low_wo(g)

            run_steps(dve, step)



def run_steps(eng, step):
    def body(g):
        for t in STEPS:
            step(g if t >= 2 else g + 1, t)

    body(Group(-1))
    body(Group(0))
    with eng.Fori(1, NG - 2) as g:
        body(Group(0, g))
    body(Group(NG - 2))
    body(Group(NG - 1))


def low_rank_phase(nc, sems, a_in, b_in, wr_in, br_in, x_res, xnT, gates, ident):
    RD = RH * RR
    with ExitStack() as c:
        m = Chip(nc, c)
        a_nat = m.sb("lr_a", [P, DM])
        wr_nat = m.sb("lr_wr", [RH, DM])
        b_nat = m.sb("lr_b", [P, KC, RH, RR])
        br = m.sb("lr_br", [P, RH])
        awT = m.sb("lr_awT", [P, KC, RD + RH])
        bT = m.sb("lr_bT", [P, DM])
        low = m.sb("lr_low", [P, NT, RD + RH])
        logit, shifted, expd, score = (m.sb("lr_" + n, [P, NT, RH]) for n in ("logit", "shifted", "expd", "score"))
        mx, total, inv = (m.sb("lr_" + n, [P, NT]) for n in ("mx", "total", "inv"))
        lowS = m.sb("lr_lowS", [P, NT, RD])
        lowT = m.sb("lr_lowT", [P, 2, P])
        gate = m.sb("lr_gate", [P, 1])
        tr = [m.bank(f"lr_tr{i}") for i in range(2)]
        lo_bank = [m.bank(f"lr_lo{i}") for i in range(2)]
        lt_bank = [m.bank(f"lr_lt{i}") for i in range(2)]
        o_bank = [m.bank(f"lr_o{i}") for i in range(2)]
        a_loaded, b_loaded, wt_tr, wt_out, low_mm, low_out, chain, lowS_ready, lt_tr, lt_out, o_done, acc_done, gate_ready = (
            sems("lr_" + n) for n in ("a", "b", "wt_tr", "wt_out", "low_mm", "low_out", "chain", "lowS", "lt_tr", "lt_out", "o_done",
                                      "acc", "gate"))
        block = c.enter_context(nc.Block())

        @block.sync
        def _(sp):
            sp.dma_start(a_nat[:], a_in.rearrange("h r d -> (h r) d")).then_inc(a_loaded, 16)
            sp.dma_start(wr_nat[:], wr_in).then_inc(a_loaded, 16)
            sp.dma_start(br[:], br_in.unsqueeze(0).to_broadcast([P, RH])).then_inc(a_loaded, 16)
            for e in range(RH):
                sp.dma_start(b_nat[:, :, e, :], b_in[e].rearrange("(c p) r -> p c r", p=P)).then_inc(b_loaded, 16)

        @block.tensor
        def _(pe):
            pe.wait_ge(a_loaded, 48)
            for k in range(KC):
                nc.tensor.transpose(tr[0][:, k * P:(k + 1) * P], a_nat[:, k * P:(k + 1) * P], ident[:])
            for k in range(KC):
                last = nc.tensor.transpose(tr[1][:, k * RH:(k + 1) * RH], wr_nat[:, k * P:(k + 1) * P], ident[0:RH, 0:RH])
            last.then_inc(wt_tr, 1)
            pe.wait_ge(wt_out, 2)
            for t in range(NT):
                if t >= 2:
                    pe.wait_ge(low_out, t - 1)
                for k in range(KC):
                    last = nc.tensor.matmul(lo_bank[t % 2][:, 0:RD + RH], xnT[:, k, t * P:(t + 1) * P], awT[:, k, :],
                                            start=(k == 0), stop=(k == KC - 1))
                last.then_inc(low_mm, 1)
            pe.wait_ge(b_loaded, 16 * RH)
            for k in range(KC):
                last = nc.tensor.transpose(tr[0][:, k * P:(k + 1) * P], b_nat[:, k].rearrange("p h r -> p (h r)"), ident[:])
            last.then_inc(wt_tr, 1)
            pe.wait_ge(lowS_ready, 1)
            for t in range(NT + 1):
                if t < NT:
                    if t >= 2:
                        pe.wait_ge(lt_out, t - 1)
                    nc.tensor.transpose(lt_bank[t % 2][:, 0:P], lowS[:, t, :], ident[:]).then_inc(lt_tr, 1)
                if t >= 1:
                    u = t - 1
                    pe.wait_ge(lt_out, u + 1)
                    if u == 0:
                        pe.wait_ge(wt_out, 3)
                    if u >= 2:
                        pe.wait_ge(acc_done, u - 1)
                    nc.tensor.matmul(o_bank[u % 2][:], lowT[:, u % 2, :], bT[:], start=True, stop=True).then_inc(o_done, 1)

        @block.scalar
        def _(act):
            act.wait_ge(wt_tr, 1)
            nc.scalar.activation(awT[:, :, 0:RD], tr[0][:].rearrange("p (c n) -> p c n", c=KC), ACT.Copy).then_inc(wt_out, 1)
            nc.scalar.activation(awT[:, :, RD:RD + RH], tr[1][:, 0:KC * RH].rearrange("p (c n) -> p c n", c=KC), ACT.Copy).then_inc(wt_out, 1)
            for t in range(NT):
                act.wait_ge(low_mm, t + 1)
                nc.scalar.activation(low[:, t, :], lo_bank[t % 2][:, 0:RD + RH], ACT.Copy).then_inc(low_out, 1)
            act.wait_ge(wt_tr, 2)
            nc.scalar.activation(bT[:], tr[0][:], ACT.Copy).then_inc(wt_out, 1)
            act.wait_ge(chain, 3)
            nc.scalar.activation(expd[:], shifted[:], ACT.Exp).then_inc(chain, 1)
            for t in range(NT):
                act.wait_ge(lt_tr, t + 1)
                if t >= 2:
                    act.wait_ge(o_done, t - 1)
                nc.scalar.activation(lowT[:, t % 2, :], lt_bank[t % 2][:, 0:P], ACT.Copy).then_inc(lt_out, 1)

        @block.vector
        def _(dve):
            nc.vector.tensor_scalar(gate[:], gates[:, 2:3], float(2 * RH), None, ALU.mult).then_inc(gate_ready, 1)
            dve.wait_ge(a_loaded, 48)
            dve.wait_ge(low_out, NT)
            tile = [P, NT, RH]
            nc.vector.tensor_tensor(logit[:], low[:, :, RD:RD + RH], br[:].unsqueeze(1).to_broadcast(tile), ALU.add).then_inc(chain, 1)
            dve.wait_ge(chain, 1)
            nc.vector.reduce_max(mx[:], logit[:], AX_X).then_inc(chain, 1)
            dve.wait_ge(chain, 2)
            nc.vector.tensor_tensor(shifted[:], logit[:], mx[:].unsqueeze(2).to_broadcast(tile), ALU.subtract).then_inc(chain, 1)
            dve.wait_ge(chain, 4)
            nc.vector.reduce_sum(total[:], expd[:], AX_X).then_inc(chain, 1)
            dve.wait_ge(chain, 5)
            nc.vector.reciprocal(inv[:], total[:]).then_inc(chain, 1)
            dve.wait_ge(chain, 6)
            nc.vector.tensor_tensor(score[:], expd[:], inv[:].unsqueeze(2).to_broadcast(tile), ALU.mult).then_inc(chain, 1)
            dve.wait_ge(chain, 7)
            nc.vector.tensor_tensor(lowS[:].rearrange("p t (h r) -> p t h r", r=RR), low[:, :, 0:RD].rearrange("p t (h r) -> p t h r", r=RR),
                                    score[:].unsqueeze(3).to_broadcast([P, NT, RH, RR]), ALU.mult).then_inc(lowS_ready, 1)
            dve.wait_ge(gate_ready, 1)
            for t in range(NT):
                dve.wait_ge(o_done, t + 1)
                nc.vector.scalar_tensor_tensor(out=x_res[:, t, :], in0=o_bank[t % 2][:], scalar=gate[:, 0:1], in1=x_res[:, t, :],
                                               op0=ALU.mult, op1=ALU.add).then_inc(acc_done, 1)


def ternary_phase(nc, sems, gate_in, up_in, down_in, gate_s_in, up_s_in, down_s_in, x_res, xn_parts, gates, out, ident):
    with ExitStack() as c:
        m = Chip(nc, c)
        nat_i = m.sb("nat_i", [P, 3, 2 * DM], I32)
        nat = m.sb("nat", [P, 3, 2 * DM])
        w_parts = [[m.sb(f"{w}T_{n}", [P, 2, DM], F32R) for n in ("hi", "lo")] for w in ("gate", "up", "down")]
        hid_parts = [m.sb(f"hid_{n}", [P, 2, TOK], F32R) for n in ("hi", "lo")]
        silu = m.sb("silu", [P, 2, HALF])
        hid = m.sb("hid", [P, 2, HALF])
        acc = m.sb("acc", [P, NT, DM])
        scales_nat = m.sb("scales_nat", [FFT, 2, P])
        scales = m.sb("ff_scales", [P, 2, FFT])
        pair_scale = m.sb("pair_scale", [P, 2])
        down_s = m.sb("down_s", [P, DM])
        down_sg = m.sb("down_sg", [P, DM])
        tr = [m.bank(f"ff_tr{i}") for i in range(2)]
        g_bank = [m.bank(f"ff_g{i}") for i in range(2)]
        u_bank = [m.bank(f"ff_u{i}") for i in range(2)]
        d_bank = [m.bank(f"ff_d{i}") for i in range(2)]
        loaded = [sems(f"ff_loaded{i}") for i in range(3)]
        scales_loaded, scales_tr, scales_ready, down_s_loaded, pair_scale_ready = (
            sems("ff_" + n) for n in ("scales", "scales_tr", "scales_ready", "down_s", "pair_scale"))
        cast, tr_done, w_hi, w_lo, prod_done, silu_ready, hid_ready, h_hi, h_lo, d_done, acc_done, setup, final, written = (
            sems("ff_" + n) for n in ("cast", "tr", "w_hi", "w_lo", "prod", "silu", "hid", "h_hi", "h_lo", "d", "acc", "setup",
                                      "final", "written"))
        gate_v = gate_in.rearrange("(f p) d -> p f d", p=P)
        up_v = up_in.rearrange("(f p) d -> p f d", p=P)
        down_v = down_in.rearrange("(c p) f -> p c f", p=P)

        TR = [(0, 0), (1, 0), (0, 1), (1, 1), (2, 0), (2, 1)]
        UNITS_FF = [(0, 0), (1, 0), (0, 1), (1, 1)]
        block = c.enter_context(nc.Block())

        class Pair(Group):
            def valid(self):
                return self.register is not None or 0 <= self.added < NFP

        def run_pairs(eng, iteration):
            iteration(Pair(0))
            with eng.Fori(1, NFP - 1) as i:
                iteration(Pair(0, i))
            iteration(Pair(NFP - 1))

        def nxt(i, n=1):
            return Pair(i.added + n, i.register)

        @block.sync
        def _(sp):
            def load(i):
                if not i.valid():
                    return
                wait_count(sp, cast, i, 3, 0)
                for n, view in enumerate((gate_v, up_v)):
                    sp.dma_start(nat_i[:, n].rearrange("p (f d) -> p f d", f=2), view[:, bass.ds(i.number(2, 0), 2), :]).then_inc(loaded[n], 16)
                sp.dma_start(nat_i[:, 2].rearrange("p (c f) -> p c f", c=KC), down_v[:, :, bass.ds(i.number(2 * P, 0), 2 * P)]).then_inc(loaded[2], 16)

            load(Pair(0))
            sp.dma_start(scales_nat[:, 0, :], gate_s_in.rearrange("(f p) -> f p", p=P)).then_inc(scales_loaded, 16)
            sp.dma_start(scales_nat[:, 1, :], up_s_in.rearrange("(f p) -> f p", p=P)).then_inc(scales_loaded, 16)
            sp.dma_start(down_s[:], down_s_in.unsqueeze(0).to_broadcast([P, DM])).then_inc(down_s_loaded, 16)
            load(Pair(1))
            with sp.Fori(1, NFP - 1) as i:
                load(Pair(1, i))
            for t in range(NT):
                sp.wait_ge(final, 2 * t + 2)
                sp.dma_start(out[t * P:(t + 1) * P, :], x_res[:, t, :]).then_inc(written, 16)
            sp.wait_ge(written, 16 * NT)

        @block.tensor
        def _(pe):
            def transpose(i, n):
                if not i.valid():
                    return
                w, f = TR[n]
                wait_count(pe, cast, i, 3, w + 1)
                wait_count(pe, w_lo, i, len(TR), n - 1)
                for k in range(KC):
                    if w < 2:
                        src = nat[:, w, f * DM + k * P:f * DM + (k + 1) * P]
                    else:
                        src = nat[:, w, k * 2 * P + f * P:k * 2 * P + (f + 1) * P]
                    last = nc.tensor.transpose(tr[n % 2][:, k * P:(k + 1) * P], src, ident[:])
                last.then_inc(tr_done, 1)

            def products(i, n):
                f, half = UNITS_FF[n]
                wait_count(pe, w_lo, i, len(TR), 2 * f + 2)
                wait_count(pe, hid_ready, i, 4, n - 1)
                for w, bank in ((0, g_bank), (1, u_bank)):
                    for k in range(KC):
                        for q, (a, b) in enumerate(PASSES):
                            last = nc.tensor.matmul(bank[n % 2][:], w_parts[w][a][:, f, k * P:(k + 1) * P],
                                                    xn_parts[b][:, k, half * HALF:(half + 1) * HALF],
                                                    start=(k == 0 and q == 0), stop=(k == KC - 1 and q == 2))
                last.then_inc(prod_done, 1)

            def down(i, half):
                if not i.valid():
                    return
                wait_count(pe, w_lo, i, len(TR), 6)
                wait_count(pe, h_lo, i, 4, 2 * half + 2)
                for t in range(NT // 2 * half, NT // 2 * (half + 1)):
                    wait_count(pe, acc_done, i, NT, t - 1)
                    for f in range(2):
                        for q, (a, b) in enumerate(PASSES):
                            last = nc.tensor.matmul(d_bank[t % 2][:], hid_parts[a][:, f, t * P:(t + 1) * P], w_parts[2][b][:, f, :],
                                                    start=(f == 0 and q == 0), stop=(f == 1 and q == 2))
                    last.then_inc(d_done, 1)

            def iteration(i):
                transpose(i, 2)
                transpose(i, 3)
                products(i, 0)
                down(nxt(i, -1), 1)
                transpose(i, 4)
                transpose(i, 5)
                products(i, 1)
                products(i, 2)
                last = i.register is None and i.added == NFP - 1
                if not last:
                    transpose(nxt(i), 0)
                    transpose(nxt(i), 1)
                down(i, 0)
                products(i, 3)

            pe.wait_ge(scales_loaded, 32)
            for n in range(2):
                last = nc.tensor.transpose(d_bank[0][:, n * FFT:(n + 1) * FFT], scales_nat[:, n, :], ident[0:FFT, 0:FFT])
            last.then_inc(scales_tr, 1)
            transpose(Pair(0), 0)
            transpose(Pair(0), 1)
            run_pairs(pe, iteration)
            down(Pair(NFP - 1), 1)

        @block.scalar
        def _(act):
            def high_part(i, n):
                if not i.valid():
                    return
                w, f = TR[n]
                wait_count(act, tr_done, i, len(TR), n + 1)
                nc.scalar.activation(w_parts[w][0][:, f, :], tr[n % 2][:], ACT.Copy).then_inc(w_hi, 1)

            def silu_of(i, n):
                f = UNITS_FF[n][0]
                wait_count(act, pair_scale_ready, i, 1, 1)
                wait_count(act, prod_done, i, 4, n + 1)
                nc.scalar.activation(silu[:, n % 2, :], g_bank[n % 2][:], ACT.Silu, scale=pair_scale[:, f:f + 1]).then_inc(silu_ready, 1)

            def hidden_high(i, n):
                f, half = UNITS_FF[n]
                wait_count(act, hid_ready, i, 4, n + 1)
                wait_count(act, d_done, i, NT, NT // 2 * (half + 1) - NT)
                nc.scalar.activation(hid_parts[0][:, f, half * HALF:(half + 1) * HALF], hid[:, n % 2, :], ACT.Copy).then_inc(h_hi, 1)

            def iteration(i):
                nc.scalar.activation(pair_scale[:], scales[:, 0, bass.ds(i.number(2, 0), 2)], ACT.Copy).then_inc(pair_scale_ready, 1)
                high_part(i, 2)
                high_part(i, 3)
                silu_of(i, 0)
                hidden_high(i, 0)
                high_part(i, 4)
                high_part(i, 5)
                silu_of(i, 1)
                hidden_high(i, 1)
                silu_of(i, 2)
                hidden_high(i, 2)
                if not (i.register is None and i.added == NFP - 1):
                    high_part(nxt(i), 0)
                    high_part(nxt(i), 1)
                silu_of(i, 3)
                hidden_high(i, 3)

            act.wait_ge(scales_tr, 1)
            nc.scalar.activation(scales[:], d_bank[0][:, 0:2 * FFT].rearrange("p (n f) -> p n f", n=2), ACT.Copy).then_inc(scales_ready, 1)
            act.wait_ge(scales_ready, 1)
            high_part(Pair(0), 0)
            high_part(Pair(0), 1)
            run_pairs(act, iteration)

        @block.vector
        def _(dve):
            def cast_to_float(i, n):
                wait_count(dve, loaded[n], i, 16, 16)
                wait_count(dve, tr_done, i, len(TR), (-2, -2, 0)[n])
                nc.vector.tensor_copy(nat[:, n], nat_i[:, n]).then_inc(cast, 1)

            def low_part(i, n):
                if not i.valid():
                    return
                w, f = TR[n]
                wait_count(dve, w_hi, i, len(TR), n + 1)
                nc.vector.tensor_tensor(w_parts[w][1][:, f, :], tr[n % 2][:], w_parts[w][0][:, f, :].bitcast(F32), ALU.subtract).then_inc(w_lo, 1)

            def hidden(i, n):
                f, half = UNITS_FF[n]
                wait_count(dve, silu_ready, i, 4, n + 1)
                wait_count(dve, h_lo, i, 4, n - 1)
                scale = scales[:, 1, bass.ds(i.number(2, f), 1)]
                nc.vector.scalar_tensor_tensor(out=hid[:, n % 2, :], in0=u_bank[n % 2][:], scalar=scale, in1=silu[:, n % 2, :],
                                               op0=ALU.mult, op1=ALU.mult).then_inc(hid_ready, 1)
                cols = slice(half * HALF, (half + 1) * HALF)
                wait_count(dve, h_hi, i, 4, n + 1)
                nc.vector.tensor_tensor(hid_parts[1][:, f, cols], hid[:, n % 2, :], hid_parts[0][:, f, cols].bitcast(F32),
                                        ALU.subtract).then_inc(h_lo, 1)

            def accumulate(i, half):
                if not i.valid():
                    return
                for t in range(NT // 2 * half, NT // 2 * (half + 1)):
                    wait_count(dve, d_done, i, NT, t + 1)
                    nc.vector.tensor_tensor(acc[:, t, :], d_bank[t % 2][:], acc[:, t, :], ALU.add).then_inc(acc_done, 1)

            def iteration(i):
                last = i.register is None and i.added == NFP - 1
                low_part(i, 2)
                low_part(i, 3)
                if not last:
                    cast_to_float(nxt(i), 0)
                    cast_to_float(nxt(i), 1)
                hidden(i, 0)
                accumulate(nxt(i, -1), 1)
                low_part(i, 4)
                low_part(i, 5)
                if not last:
                    cast_to_float(nxt(i), 2)
                hidden(i, 1)
                hidden(i, 2)
                if not last:
                    low_part(nxt(i), 0)
                    low_part(nxt(i), 1)
                accumulate(i, 0)
                hidden(i, 3)

            for n in range(3):
                cast_to_float(Pair(0), n)
            nc.vector.memset(acc[:], 0.0).then_inc(setup, 1)
            dve.wait_ge(down_s_loaded, 16)
            nc.vector.tensor_scalar(down_sg[:], down_s[:], gates[:, 3:4], None, ALU.mult).then_inc(setup, 1)
            dve.wait_ge(setup, 2)
            dve.wait_ge(scales_ready, 1)
            low_part(Pair(0), 0)
            low_part(Pair(0), 1)
            run_pairs(dve, iteration)
            accumulate(Pair(NFP - 1), 1)
            for t in range(NT):
                dve.wait_ge(acc_done, NT * (NFP - 1) + t + 1)
                nc.vector.tensor_tensor(acc[:, t, :], acc[:, t, :], down_sg[:], ALU.mult).then_inc(final, 1)
                dve.wait_ge(final, 2 * t + 1)
                nc.vector.tensor_tensor(x_res[:, t, :], acc[:, t, :], x_res[:, t, :], ALU.add).then_inc(final, 1)


def flamingo(nc, a, out):
    with ExitStack() as c:
        m = Chip(nc, c)


        in_use = []

        def sems(name):
            if name == "ld_ctx":
                return [sems(f"ld_ctx{t}") for t in range(NT)]
            in_use.append(nc.alloc_semaphore(name=name))
            return in_use[-1]

        def phase_ends():
            nc.clear_and_free_semaphores(in_use)
            in_use.clear()
            nc.all_engine_barrier()

        x_res = m.sb("x_res", [P, NT, DM])
        ctxT = m.sb("ctxT", [P, KC, TOK])
        ctx_parts = [m.sb(f"ctxT_{n}", [P, KC, TOK], F32R) for n in ("hi", "lo")]
        ident = m.sb("ident", [P, P])
        gates = m.sb("gates", [P, 4])
        cos0, sin0 = m.sb("cos0", [P, TOK]), m.sb("sin0", [P, TOK])
        rope1 = m.sb("rope1", [P, 2, SEQ])
        x_in = a["x"].rearrange("b s d -> (b s) d")
        pos_in = a["pos_BxS2"].rearrange("b s -> (b s)").unsqueeze(0).to_broadcast([P, TOK])
        load_phase(nc, sems, a["ctx_4096"].rearrange("b s d -> (b s) d"), x_in, pos_in, a["tables"], a["table1"],
                   a["g_xattn"].unsqueeze(0).to_broadcast([P, 2]), a["g_ffn"].unsqueeze(0).to_broadcast([P, 2]),
                   x_res, ctxT, ctx_parts, cos0, sin0, rope1, gates, ident)
        phase_ends()

        def half_of(table):
            return lambda half: table[:, half * HALF:(half + 1) * HALF].rearrange("p (b s) -> p b s", s=SEQ)

        def every_batch(n):
            return lambda half: rope1[:, n, :].unsqueeze(1).to_broadcast([P, BATCH // 2, SEQ])

        def with_xn(phase):
            with ExitStack() as c2:
                parts = [c2.enter_context(nc.sbuf_tensor(f"{phase}xnT_{n}", [P, KC, TOK], F32R)) for n in ("hi", "lo")]
                norm_phase(nc, sems, phase + "n_", x_res, parts, None, ident)
                phase_ends()
                if phase == "a0_":
                    attention_phase(nc, sems, phase, a["L0_xattn_Wq"], a["L0_xattn_Wk"], a["L0_xattn_Wv"], a["L0_xattn_Wo"],
                                    a["mask_BxSxS2_ik0"], True, half_of(cos0), half_of(sin0), gates[:, 0:1], x_res, parts, ctxT,
                                    ctx_parts, ident)
                elif phase == "a1_":
                    attention_phase(nc, sems, phase, a["L1_xattn_wq"], a["L1_xattn_wk"], a["L1_xattn_wv"], a["L1_xattn_wo"],
                                    a["mask_BxSxS2_ff0"], False, every_batch(0), every_batch(1), gates[:, 1:2], x_res, parts, ctxT,
                                    ctx_parts, ident)
                else:
                    ternary_phase(nc, sems, a["L1_ffn_gate_t"], a["L1_ffn_up_t"], a["L1_ffn_down_t"], a["L1_ffn_gate_s"],
                                  a["L1_ffn_up_s"], a["L1_ffn_down_s"], x_res, parts, gates, out, ident)
                phase_ends()

        with_xn("a0_")
        with ExitStack() as c2:
            xnT = c2.enter_context(nc.sbuf_tensor("f0_xnT", [P, KC, TOK], F32))
            norm_phase(nc, sems, "f0_", x_res, None, xnT, ident)
            phase_ends()
            low_rank_phase(nc, sems, a["L0_ffn_A"], a["L0_ffn_B"], a["L0_ffn_Wr"], a["L0_ffn_br"], x_res, xnT, gates, ident)
            phase_ends()
        with_xn("a1_")
        with_xn("f1_")


def rotary_tables():
    import numpy as np

    inv_freq = (1.0 / 10000.0 ** (np.arange(0, D, 2, dtype=np.float32) / np.float32(D))).astype(np.float32)
    angle = np.arange(MAX_POS, dtype=np.float32)[:, None] * inv_freq[None, :]
    cos, sin = np.cos(angle).astype(np.float32), np.sin(angle).astype(np.float32)
    cos, sin = np.concatenate([cos, cos], 1), np.concatenate([-sin, sin], 1)
    both = np.stack([cos, sin], 1)
    chunks = both.reshape(MAX_POS // P, P, 2, D).transpose(1, 0, 2, 3)
    return np.ascontiguousarray(chunks), np.ascontiguousarray(both[:SEQ].transpose(2, 1, 0))


_INS = ['x', 'ctx_4096', 'pos_BxS2', 'mask_BxSxS2_ik0', 'mask_BxSxS2_ff0', 'g_xattn', 'g_ffn', 'L0_xattn_Wq', 'L0_xattn_Wk',
        'L0_xattn_Wv', 'L0_xattn_Wo', 'L0_ffn_A', 'L0_ffn_B', 'L0_ffn_Wr', 'L0_ffn_br', 'L1_xattn_wq', 'L1_xattn_wk', 'L1_xattn_wv',
        'L1_xattn_wo', 'L1_ffn_gate_t', 'L1_ffn_up_t', 'L1_ffn_down_t', 'L1_ffn_gate_s', 'L1_ffn_up_s', 'L1_ffn_down_s']


def kernel(**inputs):
    import numpy as _np
    import concourse.bacc as _bacc
    from concourse import mybir as _mybir
    from concourse.bass_utils import run_bass_kernel_spmd as _run

    nc = _bacc.Bacc("TRN2", target_bir_lowering=False, num_devices=1)
    arrays = {name: _np.ascontiguousarray(inputs[name]) for name in _INS}
    arrays["tables"], arrays["table1"] = rotary_tables()
    aps = {name: nc.dram_tensor(f"in_{name}", x.shape, _mybir.dt.from_np(x.dtype), kind="ExternalInput").ap() for name, x in arrays.items()}
    out = nc.dram_tensor("out", (TOK, DM), _mybir.dt.float32, kind="ExternalOutput").ap()
    flamingo(nc, aps, out)
    r = _run(nc, [{f"in_{name}": x for name, x in arrays.items()}], core_ids=[0])
    return r.results[0]["out"].reshape(BATCH, SEQ, DM)
```

```python
from contextlib import ExitStack

import concourse.bass as bass
from concourse import mybir

P = 128
F32 = mybir.dt.float32
F32R = mybir.dt.float32r
I32 = mybir.dt.int32
U8 = mybir.dt.uint8
ALU = mybir.AluOpType
ACT = mybir.ActivationFunctionType
AX_X = mybir.AxisListType.X

BATCH, SEQ, DM = 16, 64, 512
TOK = BATCH * SEQ
NT = TOK // P
KC = DM // P
HALF = TOK // 2
D = 128
NG, HPG = 8, 4
SCALE = float(D) ** -0.5
MAX_POS = 512
EPS = 1e-5
FF = 1792
FFT = FF // P
NFP = FFT // 2
RH, RR = 8, 16
LAYERS = 2
PREFETCHED_LOW_RANK = 16 * (3 + RH)
PREFETCHED = PREFETCHED_LOW_RANK + 16 * 4


class Group:

    def __init__(self, added, register=None):
        self.added, self.register = added, register

    def __add__(self, n):
        return Group(self.added + n, self.register)

    def within(self, first, end):
        return self.register is not None or first <= self.added < end

    def number(self, per_group, c):
        c += self.added * per_group
        return c if self.register is None else self.register * per_group + c

    def count(self, per_group, c):
        assert self.register is None or (1 + self.added) * per_group + c > 0
        return self.number(per_group, c)


def wait_count(eng, sem, g, per_group, c):
    value = g.count(per_group, c)
    if not isinstance(value, int) or value > 0:
        eng.wait_ge(sem, value)


def back(g, t):
    return (g, t - 1) if t else (g + -1, NT - 1)


def ahead(g, t):
    return (g, t + 1) if t < NT - 1 else (g + 1, 0)


PROJ = {
    2: [("q", 0, 0)],
    3: [("q", 1, 0)],
    4: [("q", 2, 0), ("k", 0, 0)],
    5: [("q", 3, 0), ("v", 0, 0)],
    6: [("q", 0, 1), ("x", 0, 0)],
    7: [("q", 1, 1), ("v", 0, 1)],
    0: [("q", 2, 1), ("k", 0, 1)],
    1: [("q", 3, 1), ("x", 0, 1)],
}
STEPS = [2, 3, 4, 5, 6, 7, 0, 1]
UNITS = [u for t in STEPS for u in PROJ[t]]
ROPES = [u for u in UNITS if u[0] in "qk"]
NU, NR = len(UNITS), len(ROPES)
FIRST_HALF_ROPES = sum(u[2] == 0 for u in ROPES)
SPLIT_Q = {7: (2, 0), 0: (1, 1), 1: (1, 2), 2: (1, 3)}
PASSES = ((0, 0), (0, 1), (1, 0))


def proj_group(g, t):
    return g + 1 if t >= 2 else g


class Chip:

    def __init__(self, nc, ctx):
        self.nc, self.ctx = nc, ctx

    def sb(self, name, shape, dt=F32):
        return self.ctx.enter_context(self.nc.sbuf_tensor(name, shape, dt))

    def parts(self, name, shape):
        return [self.sb(f"{name}_{n}", shape, F32R) for n in ("hi", "lo")]

    def bank(self, name):
        return self.ctx.enter_context(self.nc.psum_tensor(name, [P, 512], F32))


def by_batch(ap):
    return ap.rearrange("p (b s) -> p b s", s=SEQ)


def by_chunk(ap):
    return ap.rearrange("p (c n) -> p c n", c=KC)


class Norm:

    def __init__(self, nc, sems, m, name, x_res, xn_parts, ring, banks, ident):
        self.nc, self.x_res, self.xn_parts, self.ring, self.banks, self.ident = nc, x_res, xn_parts, ring, banks, ident
        self.stats, self.mv = m.sb(name + "stats", [P, 2, 6]), m.sb(name + "mv", [P, NT, 2])
        self.var_eps, self.power, self.rstd = (m.sb(name + n, [P, NT]) for n in ("var_eps", "power", "rstd"))
        self.stats_done, self.aggr_done, self.eps_done, self.power_ready, self.rstd_ready, self.xn_ready, self.tr_done, self.hi, self.lo = (
            sems(name + n) for n in ("stats", "aggr", "eps", "power", "rstd", "xn", "tr", "hi", "lo"))

    def vector_stats(self, dve, t):
        self.nc.vector.bn_stats(self.stats[:, t % 2, :], self.x_res[:, t, :]).then_inc(self.stats_done, 1)
        dve.wait_ge(self.stats_done, t + 1)
        self.nc.vector.bn_aggr(self.mv[:, t, :], self.stats[:, t % 2, :]).then_inc(self.aggr_done, 1)
        dve.wait_ge(self.aggr_done, t + 1)
        self.nc.vector.tensor_scalar(self.var_eps[:, t:t + 1], self.mv[:, t, 1:2], EPS, None, ALU.add).then_inc(self.eps_done, 1)

    def pool_setup(self, pool):
        self.nc.gpsimd.memset(self.power[:], -0.5).then_inc(self.power_ready, 1)
        pool.wait_ge(self.power_ready, 1)

    def pool_rstd(self, pool, t):
        pool.wait_ge(self.eps_done, t + 1)
        self.nc.gpsimd.tensor_tensor(self.rstd[:, t:t + 1], self.var_eps[:, t:t + 1], self.power[:, t:t + 1], ALU.pow).then_inc(self.rstd_ready, 1)

    def vector_apply(self, dve, t):
        dve.wait_ge(self.rstd_ready, t + 1)
        if t >= 2:
            dve.wait_ge(self.tr_done, t - 1)
        self.nc.vector.tensor_scalar(self.ring[:, t % 2, :], self.x_res[:, t, :], self.mv[:, t, 0:1], self.rstd[:, t:t + 1],
                                     ALU.subtract, ALU.mult).then_inc(self.xn_ready, 1)

    def tensor_transpose(self, pe, t):
        n = len(self.banks)
        pe.wait_ge(self.xn_ready, t + 1)
        if t >= n:
            pe.wait_ge(self.lo, t - n + 1)
        for k in range(KC):
            last = self.nc.tensor.transpose(self.banks[t % n][:, k * P:(k + 1) * P], self.ring[:, t % 2, k * P:(k + 1) * P], self.ident[:])
        last.then_inc(self.tr_done, 1)

    def scalar_high(self, act, t):
        act.wait_ge(self.tr_done, t + 1)
        self.nc.scalar.activation(self.xn_parts[0][:, :, t * P:(t + 1) * P], by_chunk(self.banks[t % len(self.banks)][:]),
                                  ACT.Copy).then_inc(self.hi, 1)

    def vector_low(self, dve, t):
        dve.wait_ge(self.hi, t + 1)
        self.nc.vector.tensor_tensor(self.xn_parts[1][:, :, t * P:(t + 1) * P], by_chunk(self.banks[t % len(self.banks)][:]),
                                     self.xn_parts[0][:, :, t * P:(t + 1) * P].bitcast(F32), ALU.subtract).then_inc(self.lo, 1)


class Weights:

    def __init__(self, nc, m, sem, arrays):
        self.nc, self.arrays = nc, arrays
        self.wq_raw, self.wq = m.sb("wq_raw", [P, 2, KC, D]), m.parts("wq", [P, HPG, KC, D])
        self.wk_raw, self.wk = m.sb("wk_raw", [P, KC, D]), m.parts("wk", [P, KC, D])
        self.wv_raw, self.wv = m.sb("wv_raw", [P, KC, D]), m.parts("wv", [P, KC, D])
        self.wo_raw, self.wo = m.sb("wo_raw", [P, HPG, DM]), m.parts("wo", [P, HPG, DM])
        self.wq_loaded = [sem(f"wq_loaded{i}") for i in range(2)]
        self.wk_loaded, self.wv_loaded, self.wo_loaded = (sem(n) for n in ("wk_loaded", "wv_loaded", "wo_loaded"))
        self.wq_hi, self.wq_lo, self.wk_hi, self.wk_lo, self.wv_hi, self.wv_lo, self.wo_hi, self.wo_lo_pool, self.wo_lo_dve = (
            sem(n) for n in ("wq_hi", "wq_lo", "wk_hi", "wk_lo", "wv_hi", "wv_lo", "wo_hi", "wo_lo_pool", "wo_lo_dve"))

    def source(self, which, g, layer):
        if g.register is None:
            layer = g.added // NG
        return self.arrays[layer][which], g + -NG * layer

    def load_wq(self, sp, g, h, layer):
        w, i = self.source(0, g, layer)
        wait_count(sp, self.wq_lo, g, HPG, h - 1)
        sp.dma_start(self.wq_raw[:, h % 2], w.rearrange("(c p) n -> p c n", p=P)[:, :, bass.ds(i.number(HPG * D, h * D), D)])\
          .then_inc(self.wq_loaded[h % 2], 16)

    def load_wk(self, sp, g, layer):
        w, i = self.source(1, g, layer)
        wait_count(sp, self.wk_lo, g, 1, 0)
        sp.dma_start(self.wk_raw[:], w.rearrange("(c p) n -> p c n", p=P)[:, :, bass.ds(i.number(D, 0), D)]).then_inc(self.wk_loaded, 16)

    def load_wv(self, sp, g, layer):
        w, i = self.source(2, g, layer)
        wait_count(sp, self.wv_lo, g, 1, 0)
        sp.dma_start(self.wv_raw[:], w.rearrange("(c p) n -> p c n", p=P)[:, :, bass.ds(i.number(D, 0), D)]).then_inc(self.wv_loaded, 16)

    def load_wo(self, sp, g, layer):
        w, i = self.source(3, g, layer)
        wait_count(sp, self.wo_lo_pool, g, 2, 0)
        wait_count(sp, self.wo_lo_dve, g, 2, 0)
        sp.dma_start(self.wo_raw[:], w[bass.ds(i.number(HPG * D, 0), HPG * D), :].rearrange("(h p) n -> p h n", p=P)).then_inc(self.wo_loaded, 16)


    def high_wq(self, act, g, h):
        wait_count(act, self.wq_loaded[h % 2], g, 32, 16 * (h // 2) + 16)
        self.nc.scalar.activation(self.wq[0][:, h], self.wq_raw[:, h % 2], ACT.Copy).then_inc(self.wq_hi, 1)

    def high_wk(self, act, g):
        wait_count(act, self.wk_loaded, g, 16, 16)
        self.nc.scalar.activation(self.wk[0][:], self.wk_raw[:], ACT.Copy).then_inc(self.wk_hi, 1)

    def high_wv(self, act, g):
        wait_count(act, self.wv_loaded, g, 16, 16)
        self.nc.scalar.activation(self.wv[0][:], self.wv_raw[:], ACT.Copy).then_inc(self.wv_hi, 1)

    def high_wo(self, act, g):
        wait_count(act, self.wo_loaded, g, 16, 16)
        for h in (0, 2, 1, 3):
            self.nc.scalar.activation(self.wo[0][:, h], self.wo_raw[:, h], ACT.Copy).then_inc(self.wo_hi, 1)

    def low_wq(self, pool, g, h):
        wait_count(pool, self.wq_hi, g, HPG, h + 1)
        self.nc.gpsimd.tensor_tensor(self.wq[1][:, h], self.wq_raw[:, h % 2], self.wq[0][:, h].bitcast(F32), ALU.subtract).then_inc(self.wq_lo, 1)

    def low_wk(self, pool, g):
        wait_count(pool, self.wk_hi, g, 1, 1)
        self.nc.gpsimd.tensor_tensor(self.wk[1][:], self.wk_raw[:], self.wk[0][:].bitcast(F32), ALU.subtract).then_inc(self.wk_lo, 1)

    def low_wv(self, pool, g):
        wait_count(pool, self.wv_hi, g, 1, 1)
        self.nc.gpsimd.tensor_tensor(self.wv[1][:], self.wv_raw[:], self.wv[0][:].bitcast(F32), ALU.subtract).then_inc(self.wv_lo, 1)

    def low_wo_pool(self, pool, g):
        for i, h in enumerate((0, 1)):
            wait_count(pool, self.wo_hi, g, HPG, 2 * i + 1)
            self.nc.gpsimd.tensor_tensor(self.wo[1][:, h], self.wo_raw[:, h], self.wo[0][:, h].bitcast(F32), ALU.subtract).then_inc(self.wo_lo_pool, 1)

    def low_wo_vector(self, dve, g):
        for i, h in enumerate((2, 3)):
            wait_count(dve, self.wo_hi, g, HPG, 2 * i + 2)
            self.nc.vector.tensor_tensor(self.wo[1][:, h], self.wo_raw[:, h], self.wo[0][:, h].bitcast(F32), ALU.subtract).then_inc(self.wo_lo_dve, 1)


def load_phase(nc, sems, w, ctx_in, x_in, pos_in, tab_in, tab1_in, gx_in, gf_in, mask_in, x_res, ctx_parts, xn_parts, tables, rope1,
               x_mask, hidden, shown, gates, ident):
    with ExitStack() as c:
        m = Chip(nc, c)
        ctx_nat = m.sb("ctx_nat", [P, 4, DM])
        ring = m.sb("ld_ring", [P, 2, DM])
        pos_i = m.sb("pos_i", [P, TOK], I32)
        posf = m.sb("posf", [P, TOK])
        wrap = pos_i[:].bitcast(F32)
        rowid_i = m.sb("rowid_i", [P, MAX_POS // P], I32)
        rowid = m.sb("rowid", [P, MAX_POS // P])
        onehot = m.sb("onehot", [P, MAX_POS // P, TOK], F32R)
        tab = m.sb("tab", [P, MAX_POS // P, 2, D])
        tab_parts = m.parts("tab", [P, MAX_POS // P, 2, D])
        gate_raw = m.sb("gate_raw", [P, 4])
        tr = [m.bank(f"ld_tr{i}") for i in range(3)]
        norm = Norm(nc, sems, m, "n0_", x_res, xn_parts, ring, [m.bank(f"ld_nt{i}") for i in range(3)], ident)
        tb = [m.bank(f"ld_tb{i}") for i in range(2)]
        x_loaded = [sems(f"ld_x{t}") for t in range(NT)]
        ctx_loaded = [sems(f"ld_ctx{t}") for t in range(NT)]
        pos_loaded, tab_loaded, rope_loaded, gate_loaded, mask_loaded = (sems("ld_" + n) for n in ("pos", "tab", "rope", "gate", "mask"))
        ident_zero, ident_ready, rowid_ready = (sems("ld_" + n) for n in ("id0", "id1", "rowid"))
        ctx_tr, ctx_hi, ctx_lo = (sems("ld_" + n) for n in ("ctx_tr", "ctx_hi", "ctx_lo"))
        tab_hi_ready, tab_lo_ready, pos_step, onehot_ready, tab_mm, tab_out, gate_done, mask_done = (
            sems("ld_" + n) for n in ("tab_hi", "tab_lo", "pos_step", "onehot", "tab_mm", "tab_out", "gates", "mask_done"))
        first = Group(0)
        block = c.enter_context(nc.Block())

        @block.sync
        def _(sp):
            for t in range(NT):
                sp.dma_start(x_res[:, t, :], x_in[t * P:(t + 1) * P, :]).then_inc(x_loaded[t], 16)
                if t == 1:
                    w.load_wq(sp, first, 0, 0)
                    w.load_wq(sp, first, 1, 0)
            w.load_wk(sp, first, 0)
            w.load_wv(sp, first, 0)
            w.load_wo(sp, first, 0)
            for half in range(2):
                sp.dma_start(x_mask[half * SEQ:(half + 1) * SEQ].bitcast(I32), mask_in.rearrange("b q k -> q b k")).then_inc(mask_loaded, 16)
            w.load_wq(sp, first, 2, 0)
            w.load_wq(sp, first, 3, 0)
            sp.dma_start(rope1[:], tab1_in).then_inc(rope_loaded, 16)
            sp.wait_ge(rope_loaded, 16)

        @block.scalar
        def _(act):
            def load_ctx(t):
                act.dma_start(ctx_nat[:, t % 4, :], ctx_in[t * P:(t + 1) * P, :]).then_inc(ctx_loaded[t], 16)

            for t in range(4):
                load_ctx(t)
                if t == 1:
                    act.dma_start(pos_i[:], pos_in).then_inc(pos_loaded, 16)
                    act.dma_start(tab[:], tab_in).then_inc(tab_loaded, 16)
            act.dma_start(gate_raw[:, 0:2], gx_in).then_inc(gate_loaded, 16)
            act.dma_start(gate_raw[:, 2:4], gf_in).then_inc(gate_loaded, 16)
            for t in range(NT + 2):
                if t < NT:
                    act.wait_ge(ctx_tr, t + 1)
                    nc.scalar.activation(ctx_parts[0][:, :, t * P:(t + 1) * P], by_chunk(tr[t % 3][:]), ACT.Copy).then_inc(ctx_hi, 1)
                    if t + 4 < NT:
                        load_ctx(t + 4)
                if t >= 2:
                    norm.scalar_high(act, t - 2)
                if t in (3, 4, 7, 8):
                    w.high_wq(act, first, (3, 4, 7, 8).index(t))
                if t == 5:
                    w.high_wk(act, first)
                if t == 6:
                    w.high_wv(act, first)
            w.high_wo(act, first)
            act.wait_ge(gate_loaded, 32)
            nc.scalar.activation(gates[:], gate_raw[:], ACT.Tanh).then_inc(gate_done, 1)
            for n in range(2):
                for h in range(2):
                    act.wait_ge(tab_mm, 2 * n + h + 1)
                    nc.scalar.activation(tables[:, n, h * HALF:(h + 1) * HALF], tb[h][:], ACT.Copy).then_inc(tab_out, 1)

        @block.gpsimd
        def _(pool):
            nc.gpsimd.memset(ident[:], 0.0).then_inc(ident_zero, 1)
            pool.wait_ge(ident_zero, 1)
            nc.gpsimd.affine_select(out=ident[:], in_=ident[:], compare_op=ALU.not_equal, fill=1.0, base=0,
                                    pattern=[[-1, P]], channel_multiplier=1).then_inc(ident_ready, 1)
            nc.gpsimd.iota(rowid_i[:], pattern=[[P, MAX_POS // P]], base=0, channel_multiplier=1).then_inc(rowid_ready, 1)
            norm.pool_setup(pool)
            for t in range(NT):
                norm.pool_rstd(pool, t)
                if t in (3, 4):
                    w.low_wq(pool, first, t - 3)
                if t == 5:
                    w.low_wk(pool, first)
                if t == 6:
                    w.low_wv(pool, first)
            w.low_wq(pool, first, 2)
            w.low_wq(pool, first, 3)
            w.low_wo_pool(pool, first)

        @block.vector
        def _(dve):
            def low_ctx(t):
                dve.wait_ge(ctx_hi, t + 1)
                nc.vector.tensor_tensor(ctx_parts[1][:, :, t * P:(t + 1) * P], by_chunk(tr[t % 3][:]),
                                        ctx_parts[0][:, :, t * P:(t + 1) * P].bitcast(F32), ALU.subtract).then_inc(ctx_lo, 1)

            for t in range(NT + 2):
                if t < NT:
                    dve.wait_ge(x_loaded[t], 16)
                    norm.vector_stats(dve, t)
                    low_ctx(t)
                if 1 <= t <= NT:
                    norm.vector_apply(dve, t - 1)
                if t == 3:
                    dve.wait_ge(tab_loaded, 16)
                    nc.vector.tensor_copy(tab_parts[0][:], tab[:]).then_inc(tab_hi_ready, 1)
                    dve.wait_ge(tab_hi_ready, 1)
                    nc.vector.tensor_tensor(tab_parts[1][:], tab[:], tab_parts[0][:].bitcast(F32), ALU.subtract).then_inc(tab_lo_ready, 1)
                    dve.wait_ge(rowid_ready, 1)
                    nc.vector.tensor_copy(rowid[:], rowid_i[:]).then_inc(pos_step, 1)
                    dve.wait_ge(pos_loaded, 16)
                    nc.vector.tensor_copy(posf[:], pos_i[:]).then_inc(pos_step, 1)
                    dve.wait_ge(pos_step, 2)
                    nc.vector.tensor_scalar(wrap, posf[:], 0.0, float(MAX_POS), ALU.is_lt, ALU.mult).then_inc(pos_step, 1)
                    dve.wait_ge(pos_step, 3)
                    nc.vector.tensor_tensor(posf[:], posf[:], wrap, ALU.add).then_inc(pos_step, 1)
                    dve.wait_ge(pos_step, 4)
                    nc.vector.tensor_scalar(wrap, posf[:], 0.0, float(MAX_POS - 1), ALU.max, ALU.min).then_inc(pos_step, 1)
                    dve.wait_ge(pos_step, 5)
                    for q in range(MAX_POS // P):
                        nc.vector.tensor_scalar(onehot[:, q, :], wrap, rowid[:, q:q + 1], None, ALU.is_equal).then_inc(onehot_ready, 1)
                if t >= 2:
                    norm.vector_low(dve, t - 2)
            w.low_wo_vector(dve, first)
            dve.wait_ge(mask_loaded, 32)
            nc.vector.tensor_scalar(hidden[:], x_mask[:].bitcast(I32), 0, None, ALU.is_equal).then_inc(mask_done, 1)
            nc.vector.tensor_scalar(shown[:], x_mask[:].bitcast(I32), 0, None, ALU.not_equal).then_inc(mask_done, 1)

        @block.tensor
        def _(pe):
            pe.wait_ge(ident_ready, 1)
            for t in range(NT + 1):
                if t < NT:
                    pe.wait_ge(ctx_loaded[t], 16)
                    if t >= 3:
                        pe.wait_ge(ctx_lo, t - 2)
                    for k in range(KC):
                        last = nc.tensor.transpose(tr[t % 3][:, k * P:(k + 1) * P], ctx_nat[:, t % 4, k * P:(k + 1) * P], ident[:])
                    last.then_inc(ctx_tr, 1)
                if t >= 1:
                    norm.tensor_transpose(pe, t - 1)
            pe.wait_ge(onehot_ready, MAX_POS // P)
            pe.wait_ge(tab_lo_ready, 1)
            for n in range(2):
                for h in range(2):
                    if n:
                        pe.wait_ge(tab_out, h + 1)
                    steps = [(q, part) for q in range(MAX_POS // P) for part in tab_parts]
                    for i, (q, part) in enumerate(steps):
                        last = nc.tensor.matmul(tb[h][:], part[:, q, n, :], onehot[:, q, h * HALF:(h + 1) * HALF],
                                                start=(i == 0), stop=(i == len(steps) - 1))
                    last.then_inc(tab_mm, 1)


class AttentionSignals:

    def __init__(self, sem):
        self.proj_done, self.s_done, self.t_done, self.pv_done, self.o_done = (
            sem(n) for n in ("proj_done", "s_done", "t_done", "pv_done", "o_done"))
        self.rot_ready, self.sin_done, self.cos_done, self.rope_done, self.vT_ready, self.v_hi, self.v_lo = (
            sem(n) for n in ("rot_ready", "sin_done", "cos_done", "rope_done", "vT_ready", "v_hi", "v_lo"))
        self.s_read, self.s_masked, self.mx_ready, self.shifted, self.exp_ready, self.total_ready, self.inv_ready, self.prob_ready = (
            sem(n) for n in ("s_read", "s_masked", "mx_ready", "shifted", "exp_ready", "total_ready", "inv_ready", "prob_ready"))
        self.probT_hi, self.probT_lo, self.oT_hi, self.oT_lo, self.acc_done = (
            sem(n) for n in ("probT_hi", "probT_lo", "oT_hi", "oT_lo", "acc_done"))


def attention_phase(nc, sems, layer, w, sig, masks, cos, sin, gate, x_res, xn_parts, ctx_parts, prefetch, ident):
    first_group, end_group = layer * NG, (layer + 1) * NG
    with ExitStack() as c:
        m = Chip(nc, c)
        name = f"a{layer}_"
        qT = m.sb(name + "qT", [P, BATCH, HPG, SEQ])
        kT = m.sb(name + "kT", [P, BATCH, SEQ])
        vT = m.sb(name + "vT", [P, HALF])
        v = m.parts(name + "v", [P, NT, D])
        rot = m.sb(name + "rot", [P, 2, HALF])
        qcos = m.sb(name + "qcos", [P, HALF])
        sc = m.sb(name + "sc", [P, 256])
        prob = m.sb(name + "prob", [P, 2, 256])
        probT = m.parts(name + "probT", [P, 2, 256])
        oT = m.parts(name + "oT", [P, 2, HPG, 2, SEQ])
        mx, total, inv = (m.sb(name + n, [P, 4]) for n in ("mx", "total", "inv"))
        proj_bank = [m.bank(f"{name}proj{i}") for i in range(2)]
        s_bank, t_bank, o_bank = (m.bank(name + n) for n in ("s", "t", "o"))
        pv_bank = [m.bank(f"{name}pv{i}") for i in range(2)]
        norm = Norm(nc, sems, m, f"n{layer + 1}_" if layer == 0 else "n3_", x_res, xn_parts, rot, proj_bank, ident)

        def in_layer(g):
            return g.within(first_group, end_group)

        def weights_due(g):
            return g.within(first_group + 1, min(end_group, LAYERS * NG - 1) + 1)

        def norm_step(g, t):
            return -1 if g.register is not None else (g.added - end_group + 1) * NT + t

        def heads_of(unit):
            kind, h, half = unit
            b = slice(half * (BATCH // 2), (half + 1) * (BATCH // 2))
            return qT[:, b, h, :] if kind == "q" else kT[:, b, :]

        def unit_at(g, t, which):
            if len(PROJ[t]) > which and in_layer(proj_group(g, t)):
                return proj_group(g, t), PROJ[t][which]
            return None

        block = c.enter_context(nc.Block())

        def run_steps(eng, step):
            def body(g):
                for t in STEPS:
                    step(g if t >= 2 else g + 1, t)

            body(Group(first_group - 1))
            body(Group(first_group))
            with eng.Fori(first_group + 1, end_group - 2) as g:
                body(Group(0, g))
            body(Group(end_group - 2))
            body(Group(end_group - 1))
            step(Group(end_group), 2)

        @block.sync
        def _(sp):
            def step(g, t):
                if t == 2:
                    for h in range(2):
                        if weights_due(g + 2):
                            w.load_wq(sp, g + 2, h, layer)
                elif t == 3 and weights_due(g + 2):
                    w.load_wv(sp, g + 2, layer)
                elif t == 4 and weights_due(g + 2):
                    w.load_wk(sp, g + 2, layer)
                elif t == 0 and weights_due(g + 1):
                    w.load_wq(sp, g + 1, 2, layer)
                elif t == 1 and weights_due(g + 1):
                    w.load_wq(sp, g + 1, 3, layer)
                    w.load_wo(sp, g + 1, layer)

            if layer == 1:
                prefetch(sp)
            run_steps(sp, step)
            if layer == 0:
                sp.wait_ge(sig.rope_done, end_group * NR)
                prefetch(sp)

        @block.tensor
        def _(pe):
            def project(g, t, which):
                if (found := unit_at(g, t, which)) is None:
                    return
                g, unit = found
                kind, h, half = unit
                j = UNITS.index(unit)
                before, gb = (UNITS[j - 2], g) if j >= 2 else (UNITS[j - 2], g + -1)
                if before[0] == "v":
                    wait_count(pe, sig.vT_ready, gb, 2, before[2] + 1)
                elif before[0] == "x":
                    wait_count(pe, sig.v_lo, gb, 2, before[2] + 1)
                else:
                    wait_count(pe, sig.cos_done, gb, NR, ROPES.index(before) + 1)
                out = proj_bank[j % 2]
                if kind == "x":
                    wait_count(pe, sig.vT_ready, g, 2, half + 1)
                    for i in range(NT // 2):
                        last = nc.tensor.transpose(out[:, i * P:(i + 1) * P], vT[:, i * P:(i + 1) * P], ident[:])
                else:
                    if kind == "q":
                        wait_count(pe, w.wq_lo, g, HPG, h + 1)
                        weights, moving = [part[:, h] for part in w.wq], xn_parts
                    elif kind == "k":
                        wait_count(pe, w.wk_lo, g, 1, 1)
                        weights, moving = [part[:] for part in w.wk], ctx_parts
                    else:
                        wait_count(pe, w.wv_lo, g, 1, 1)
                        weights, moving = [part[:] for part in w.wv], ctx_parts
                    for k in range(KC):
                        for n, (a, b) in enumerate(PASSES):
                            last = nc.tensor.matmul(out[:], weights[a][:, k, :], moving[b][:, k, half * HALF:(half + 1) * HALF],
                                                    start=(k == 0 and n == 0), stop=(k == KC - 1 and n == 2))
                last.then_inc(sig.proj_done, 1)

            def scores(g, t):
                if not in_layer(g):
                    return
                wait_count(pe, sig.rope_done, g, NR, NR if t >= NT // 2 else FIRST_HALF_ROPES)
                wait_count(pe, sig.s_read, g, NT, t)
                for pair in range(HPG // 2):
                    for b2 in range(2):
                        b = 2 * t + b2
                        last = nc.tensor.matmul(s_bank[:, (2 * pair + b2) * SEQ:(2 * pair + b2 + 1) * SEQ],
                                                qT[:, b, 2 * pair:2 * pair + 2, :].rearrange("p h s -> p (h s)"), kT[:, b, :],
                                                start=True, stop=True)
                last.then_inc(sig.s_done, 1)

            def transpose_probs(g, t):
                if not in_layer(g):
                    return
                wait_count(pe, sig.prob_ready, g, NT, t + 1)
                wait_count(pe, sig.probT_lo, g, NT, t)
                for pair in range(HPG // 2):
                    last = nc.tensor.transpose(t_bank[:, pair * P:(pair + 1) * P], prob[:, t % 2, pair * P:(pair + 1) * P], ident[:])
                last.then_inc(sig.t_done, 1)

            def probs_values(g, t):
                if not in_layer(g):
                    return
                wait_count(pe, sig.probT_lo, g, NT, t + 1)
                wait_count(pe, sig.v_lo, g, 2, t // (NT // 2) + 1)
                wait_count(pe, sig.oT_lo, g, 2 * NT, 2 * t)
                for b2 in range(2):
                    rows = slice(b2 * SEQ, (b2 + 1) * SEQ)
                    for n, (a, b) in enumerate(PASSES):
                        last = nc.tensor.matmul(pv_bank[b2][:, 0:256], v[a][rows, t, :], probT[b][rows, t % 2, :], start=(n == 0), stop=(n == 2))
                last.then_inc(sig.pv_done, 1)

            def output(g, t):
                if not in_layer(g):
                    return
                wait_count(pe, sig.oT_lo, g, 2 * NT, 2 * t + 2)
                wait_count(pe, w.wo_lo_pool, g, 2, 2)
                wait_count(pe, w.wo_lo_dve, g, 2, 2)
                wait_count(pe, sig.acc_done, g, NT, t)
                for h in range(HPG):
                    for n, (a, b) in enumerate(PASSES):
                        last = nc.tensor.matmul(o_bank[:], oT[a][:, t % 2, h].rearrange("p b s -> p (b s)"), w.wo[b][:, h, :],
                                                start=(h == 0 and n == 0), stop=(h == HPG - 1 and n == 2))
                last.then_inc(sig.o_done, 1)

            def step(g, t):
                scores(*ahead(g, t))
                transpose_probs(g, t)
                project(g, t, 0)
                output(*back(g, t))
                probs_values(g, t)
                project(g, t, 1)
                n = norm_step(g, t)
                if n == 2:
                    pe.wait_ge(sig.v_lo, 2 * end_group)
                    pe.wait_ge(sig.cos_done, NR * end_group)
                if 2 <= n < NT + 2:
                    norm.tensor_transpose(pe, n - 2)

            run_steps(pe, step)

        @block.scalar
        def _(act):
            def rotate_or_copy(g, t, which):
                if (found := unit_at(g, t, which)) is None:
                    return
                g, unit = found
                kind, _, half = unit
                bank = proj_bank[UNITS.index(unit) % 2]
                wait_count(act, sig.proj_done, g, NU, UNITS.index(unit) + 1)
                if kind == "v":
                    nc.scalar.activation(vT[:], bank[:], ACT.Copy).then_inc(sig.vT_ready, 1)
                elif kind == "x":
                    wait_count(act, sig.pv_done, g + -1, NT, NT // 2 * (half + 1))
                    tiles = slice(NT // 2 * half, NT // 2 * (half + 1))
                    nc.scalar.activation(v[0][:, tiles, :], bank[:].rearrange("p (t d) -> p t d", d=D), ACT.Copy).then_inc(sig.v_hi, 1)
                else:
                    r = ROPES.index(unit)
                    wait_count(act, sig.rope_done, g, NR, r - 1)
                    nc.scalar.activation(rot[0:64, r % 2, :], bank[64:128, :], ACT.Copy).then_inc(sig.rot_ready, 1)
                    nc.scalar.activation(rot[64:128, r % 2, :], bank[0:64, :], ACT.Copy).then_inc(sig.rot_ready, 1)

            def exponentials(g, t):
                if not in_layer(g):
                    return
                wait_count(act, sig.shifted, g, NT, t + 1)
                nc.scalar.activation(prob[:, t % 2, :], sc[:], ACT.Exp).then_inc(sig.exp_ready, 1)

            def probs_high(g, t):
                if not in_layer(g):
                    return
                wait_count(act, sig.t_done, g, NT, t + 1)
                nc.scalar.activation(probT[0][:, t % 2, :], t_bank[:, 0:256], ACT.Copy).then_inc(sig.probT_hi, 1)

            def heads_high(g, t):
                if not in_layer(g):
                    return
                wait_count(act, sig.pv_done, g, NT, t + 1)
                for b2 in range(2):
                    nc.scalar.activation(oT[0][:, t % 2, :, b2, :], by_batch(pv_bank[b2][:, 0:256]), ACT.Copy).then_inc(sig.oT_hi, 1)

            def split_wq(g, h):
                if weights_due(g):
                    wait_count(act, sig.proj_done, g + -1, NU, UNITS.index(("q", h, 1)) + 1)
                    w.high_wq(act, g, h)

            def split_k_or_v(g, kind):
                if weights_due(g):
                    wait_count(act, sig.proj_done, g + -1, NU, UNITS.index((kind, 0, 1)) + 1)
                    (w.high_wk if kind == "k" else w.high_wv)(act, g)

            def split_wo(g):
                if weights_due(g):
                    wait_count(act, sig.o_done, g, NT, 0)
                    w.high_wo(act, g)

            def step(g, t):
                n = norm_step(g, t)
                gb, tb = back(g, t)
                heads_high(gb, tb)
                rotate_or_copy(gb, tb, 1)
                if 3 <= n < NT + 3:
                    norm.scalar_high(act, n - 3)
                probs_high(g, t)
                exponentials(*ahead(g, t))
                rotate_or_copy(g, t, 0)
                if t in SPLIT_Q:
                    split_wq(g + SPLIT_Q[t][0], SPLIT_Q[t][1])
                if t == 2:
                    split_k_or_v(g + 1, "v")
                if t == 3:
                    split_k_or_v(g + 1, "k")
                if t == 0:
                    split_wo(g)

            run_steps(act, step)

        @block.gpsimd
        def _(pool):
            def times_sin(g, t, which):
                if (found := unit_at(g, t, which)) is None or found[1][0] not in "qk":
                    return
                g, unit = found
                r = ROPES.index(unit)
                wait_count(pool, sig.rot_ready, g, 2 * NR, 2 * r + 2)
                nc.gpsimd.tensor_tensor(by_batch(rot[:, r % 2, :]), by_batch(rot[:, r % 2, :]), sin(unit[2]), ALU.mult).then_inc(sig.sin_done, 1)

            def step(g, t):
                gb, tb = back(g, t)
                times_sin(gb, tb, 1)
                times_sin(g, t, 0)
                if t in SPLIT_Q and weights_due(g + SPLIT_Q[t][0]):
                    w.low_wq(pool, g + SPLIT_Q[t][0], SPLIT_Q[t][1])
                if t == 2 and weights_due(g + 1):
                    w.low_wv(pool, g + 1)
                if t == 3 and weights_due(g + 1):
                    w.low_wk(pool, g + 1)
                if t == 0 and weights_due(g):
                    w.low_wo_pool(pool, g)
                n = norm_step(g, t)
                if 1 <= n < NT + 1:
                    norm.pool_rstd(pool, n - 1)

            norm.pool_setup(pool)
            run_steps(pool, step)

        @block.vector
        def _(dve):
            def rotary_or_low(g, t, which):
                if (found := unit_at(g, t, which)) is None:
                    return
                g, unit = found
                kind, _, half = unit
                bank = proj_bank[UNITS.index(unit) % 2]
                if kind == "x":
                    wait_count(dve, sig.v_hi, g, 2, half + 1)
                    tiles = slice(NT // 2 * half, NT // 2 * (half + 1))
                    nc.vector.tensor_tensor(v[1][:, tiles, :], bank[:].rearrange("p (t d) -> p t d", d=D), v[0][:, tiles, :].bitcast(F32),
                                            ALU.subtract).then_inc(sig.v_lo, 1)
                if kind not in "qk":
                    return
                r = ROPES.index(unit)
                wait_count(dve, sig.rot_ready, g, 2 * NR, 2 * r + 2)
                wait_count(dve, sig.rope_done, g, NR, r)
                nc.vector.tensor_tensor(by_batch(qcos[:]), by_batch(bank[:]), cos(half), ALU.mult).then_inc(sig.cos_done, 1)
                wait_count(dve, sig.cos_done, g, NR, r + 1)
                wait_count(dve, sig.sin_done, g, NR, r + 1)
                wait_count(dve, sig.s_done, g + -1, NT, NT // 2 * (half + 1))
                nc.vector.tensor_tensor(heads_of(unit), by_batch(qcos[:]), by_batch(rot[:, r % 2, :]), ALU.add).then_inc(sig.rope_done, 1)

            def softmax(g, t):
                if not in_layer(g):
                    return
                b = slice(2 * t, 2 * t + 2)
                both_pairs = [P, 2, 2 * SEQ]
                pairs = sc[:].rearrange("p (a n) -> p a n", a=2)
                bank = s_bank[:, 0:256].rearrange("p (a n) -> p a n", a=2)

                def for_tile(mask):
                    return mask[:, b, :].rearrange("p b k -> p (b k)").unsqueeze(1).to_broadcast(both_pairs)

                wait_count(dve, sig.exp_ready, g, NT, t)
                wait_count(dve, sig.s_done, g, NT, t + 1)
                if len(masks) == 2:
                    nc.vector.scalar_tensor_tensor(out=pairs, in0=bank, scalar=SCALE, in1=for_tile(masks[0]),
                                                   op0=ALU.mult, op1=ALU.mult).then_inc(sig.s_read, 1)
                    wait_count(dve, sig.s_read, g, NT, t + 1)
                    nc.vector.scalar_tensor_tensor(out=pairs, in0=for_tile(masks[1]), scalar=-1e9, in1=pairs,
                                                   op0=ALU.mult, op1=ALU.add).then_inc(sig.s_masked, 1)
                    wait_count(dve, sig.s_masked, g, NT, t + 1)
                else:
                    nc.vector.scalar_tensor_tensor(out=pairs, in0=bank, scalar=SCALE, in1=for_tile(masks[0]),
                                                   op0=ALU.mult, op1=ALU.add).then_inc(sig.s_read, 1)
                    wait_count(dve, sig.s_read, g, NT, t + 1)
                rows = [P, 4, SEQ]
                sc4 = by_batch(sc[:])
                pr4 = by_batch(prob[:, t % 2, :])
                nc.vector.reduce_max(mx[:], sc4, AX_X).then_inc(sig.mx_ready, 1)
                wait_count(dve, sig.mx_ready, g, NT, t + 1)
                nc.vector.tensor_tensor(sc4, sc4, mx[:].unsqueeze(2).to_broadcast(rows), ALU.subtract).then_inc(sig.shifted, 1)
                wait_count(dve, sig.exp_ready, g, NT, t + 1)
                nc.vector.reduce_sum(total[:], pr4, AX_X).then_inc(sig.total_ready, 1)
                wait_count(dve, sig.total_ready, g, NT, t + 1)
                nc.vector.reciprocal(inv[:], total[:]).then_inc(sig.inv_ready, 1)
                wait_count(dve, sig.inv_ready, g, NT, t + 1)
                nc.vector.tensor_tensor(pr4, pr4, inv[:].unsqueeze(2).to_broadcast(rows), ALU.mult).then_inc(sig.prob_ready, 1)

            def probs_low(g, t):
                if not in_layer(g):
                    return
                wait_count(dve, sig.probT_hi, g, NT, t + 1)
                nc.vector.tensor_tensor(probT[1][:, t % 2, :], t_bank[:, 0:256], probT[0][:, t % 2, :].bitcast(F32), ALU.subtract)\
                  .then_inc(sig.probT_lo, 1)

            def heads_low(g, t):
                if not in_layer(g):
                    return
                for b2 in range(2):
                    wait_count(dve, sig.oT_hi, g, 2 * NT, 2 * t + b2 + 1)
                    nc.vector.tensor_tensor(oT[1][:, t % 2, :, b2, :], by_batch(pv_bank[b2][:, 0:256]),
                                            oT[0][:, t % 2, :, b2, :].bitcast(F32), ALU.subtract).then_inc(sig.oT_lo, 1)

            def accumulate(g, t):
                if not in_layer(g):
                    return
                wait_count(dve, sig.o_done, g, NT, t + 1)
                nc.vector.scalar_tensor_tensor(out=x_res[:, t, :], in0=o_bank[:], scalar=gate, in1=x_res[:, t, :],
                                               op0=ALU.mult, op1=ALU.add).then_inc(sig.acc_done, 1)

            def step(g, t):
                n = norm_step(g, t)
                gb, tb = back(g, t)
                heads_low(gb, tb)
                rotary_or_low(gb, tb, 1)
                if 2 <= n < NT + 2:
                    norm.vector_apply(dve, n - 2)
                probs_low(g, t)
                softmax(*ahead(g, t))
                rotary_or_low(g, t, 0)
                if 3 <= n < NT + 3:
                    norm.vector_low(dve, n - 3)
                accumulate(gb, tb)
                if 1 <= n < NT + 1:
                    wait_count(dve, sig.acc_done, gb, NT, tb + 1)
                    norm.vector_stats(dve, n - 1)
                if t == 0 and weights_due(g):
                    w.low_wo_vector(dve, g)

            run_steps(dve, step)


def low_rank_phase(nc, sems, a_nat, wr_nat, b_nat, br, prefetched, mask_in, x_mask, x_res, xn_parts, gates, ident):
    RD = RH * RR
    HT = NT // 2
    with ExitStack() as c:
        m = Chip(nc, c)
        awT = m.parts("lr_awT", [P, KC, RD + RH])
        bT = m.sb("lr_bT", [P, DM])
        low = m.sb("lr_low", [P, NT, RD + RH])
        logit, shifted, expd, score = (m.sb("lr_" + n, [P, NT, RH]) for n in ("logit", "shifted", "expd", "score"))
        mx, total, inv = (m.sb("lr_" + n, [P, NT]) for n in ("mx", "total", "inv"))
        lowS = m.sb("lr_lowS", [P, NT, RD])
        lowT = m.sb("lr_lowT", [P, 2, P])
        gate = m.sb("lr_gate", [P, 1])
        ring = m.sb("lr_ring", [P, 2, DM])
        tr = [m.bank(f"lr_tr{i}") for i in range(2)]
        lo_bank = [m.bank(f"lr_lo{i}") for i in range(2)]
        lt_bank = [m.bank(f"lr_lt{i}") for i in range(2)]
        o_bank = [m.bank(f"lr_o{i}") for i in range(2)]
        norm = Norm(nc, sems, m, "n2_", x_res, xn_parts, ring, tr, ident)
        wt_tr, wt_hi, wt_lo, bT_ready, low_mm, low_out, chain, exp_done, lowS_ready, lt_tr, lt_out, o_done, acc_done, gate_ready, mask_loaded = (
            sems("lr_" + n) for n in ("wt_tr", "wt_hi", "wt_lo", "bT", "low_mm", "low_out", "chain", "exp", "lowS", "lt_tr", "lt_out", "o_done",
                                      "acc", "gate", "mask"))
        block = c.enter_context(nc.Block())

        def by_rows(bank, n):
            return bank[:, 0:KC * n].rearrange("p (c n) -> p c n", c=KC)

        WT = [(by_rows(tr[0], RD), slice(0, RD)), (by_rows(tr[1], RH), slice(RD, RD + RH))]

        def exponentials(act, half):
            tiles = slice(half * HT, (half + 1) * HT)
            act.wait_ge(chain, 6 * half + 3)
            nc.scalar.activation(expd[:, tiles], shifted[:, tiles], ACT.Exp).then_inc(exp_done, 1)

        @block.sync
        def _(sp):
            for half in range(2):
                sp.dma_start(x_mask[half * SEQ:(half + 1) * SEQ], mask_in.rearrange("b q k -> q b k")).then_inc(mask_loaded, 16)
            sp.wait_ge(mask_loaded, 32)

        @block.tensor
        def _(pe):
            pe.wait_ge(prefetched, PREFETCHED_LOW_RANK)
            for k in range(KC):
                nc.tensor.transpose(tr[0][:, k * P:(k + 1) * P], a_nat[:, k * P:(k + 1) * P], ident[:])
            for k in range(KC):
                last = nc.tensor.transpose(tr[1][:, k * RH:(k + 1) * RH], wr_nat[:, k * P:(k + 1) * P], ident[0:RH, 0:RH])
            last.then_inc(wt_tr, 1)
            for k in range(KC):
                last = nc.tensor.transpose(o_bank[0][:, k * P:(k + 1) * P], b_nat[:, k * RD:(k + 1) * RD], ident[:])
            last.then_inc(wt_tr, 1)
            pe.wait_ge(wt_lo, 2)
            for t in range(NT):
                if t >= 2:
                    pe.wait_ge(low_out, t - 1)
                for k in range(KC):
                    for n, (a, b) in enumerate(PASSES):
                        last = nc.tensor.matmul(lo_bank[t % 2][:, 0:RD + RH], xn_parts[a][:, k, t * P:(t + 1) * P], awT[b][:, k, :],
                                                start=(k == 0 and n == 0), stop=(k == KC - 1 and n == 2))
                last.then_inc(low_mm, 1)
            for t in range(NT + 3):
                if t < NT:
                    pe.wait_ge(lowS_ready, t // HT + 1)
                    if t >= 2:
                        pe.wait_ge(lt_out, t - 1)
                    nc.tensor.transpose(lt_bank[t % 2][:, 0:P], lowS[:, t, :], ident[:]).then_inc(lt_tr, 1)
                if 1 <= t <= NT:
                    u = t - 1
                    pe.wait_ge(lt_out, u + 1)
                    if u == 0:
                        pe.wait_ge(bT_ready, 1)
                    if u >= 2:
                        pe.wait_ge(acc_done, u - 1)
                    nc.tensor.matmul(o_bank[u % 2][:], lowT[:, u % 2, :], bT[:], start=True, stop=True).then_inc(o_done, 1)
                if t >= 3:
                    norm.tensor_transpose(pe, t - 3)

        @block.scalar
        def _(act):
            act.wait_ge(wt_tr, 1)
            for bank, cols in WT:
                nc.scalar.activation(awT[0][:, :, cols], bank, ACT.Copy).then_inc(wt_hi, 1)
            act.wait_ge(wt_tr, 2)
            nc.scalar.activation(bT[:], o_bank[0][:], ACT.Copy).then_inc(bT_ready, 1)
            for t in range(NT):
                act.wait_ge(low_mm, t + 1)
                nc.scalar.activation(low[:, t, :], lo_bank[t % 2][:, 0:RD + RH], ACT.Copy).then_inc(low_out, 1)
                if t == HT + 1:
                    exponentials(act, 0)
            exponentials(act, 1)
            for t in range(NT + 3):
                if t < NT:
                    act.wait_ge(lt_tr, t + 1)
                    if t >= 2:
                        act.wait_ge(o_done, t - 1)
                    nc.scalar.activation(lowT[:, t % 2, :], lt_bank[t % 2][:, 0:P], ACT.Copy).then_inc(lt_out, 1)
                if t >= 3:
                    norm.scalar_high(act, t - 3)

        @block.gpsimd
        def _(pool):
            norm.pool_setup(pool)
            for t in range(NT):
                norm.pool_rstd(pool, t)

        @block.vector
        def _(dve):
            nc.vector.tensor_scalar(gate[:], gates[:, 2:3], float(2 * RH), None, ALU.mult).then_inc(gate_ready, 1)
            for n, (bank, cols) in enumerate(WT):
                dve.wait_ge(wt_hi, n + 1)
                nc.vector.tensor_tensor(awT[1][:, :, cols], bank, awT[0][:, :, cols].bitcast(F32), ALU.subtract).then_inc(wt_lo, 1)
            for half in range(2):
                tiles = slice(half * HT, (half + 1) * HT)
                block_shape = [P, HT, RH]
                dve.wait_ge(low_out, HT * (half + 1))
                nc.vector.tensor_tensor(logit[:, tiles], low[:, tiles, RD:RD + RH], br.unsqueeze(1).to_broadcast(block_shape), ALU.add)\
                  .then_inc(chain, 1)
                dve.wait_ge(chain, 6 * half + 1)
                nc.vector.reduce_max(mx[:, tiles], logit[:, tiles], AX_X).then_inc(chain, 1)
                dve.wait_ge(chain, 6 * half + 2)
                nc.vector.tensor_tensor(shifted[:, tiles], logit[:, tiles], mx[:, tiles].unsqueeze(2).to_broadcast(block_shape), ALU.subtract)\
                  .then_inc(chain, 1)
                dve.wait_ge(exp_done, half + 1)
                nc.vector.reduce_sum(total[:, tiles], expd[:, tiles], AX_X).then_inc(chain, 1)
                dve.wait_ge(chain, 6 * half + 4)
                nc.vector.reciprocal(inv[:, tiles], total[:, tiles]).then_inc(chain, 1)
                dve.wait_ge(chain, 6 * half + 5)
                nc.vector.tensor_tensor(score[:, tiles], expd[:, tiles], inv[:, tiles].unsqueeze(2).to_broadcast(block_shape), ALU.mult)\
                  .then_inc(chain, 1)
                dve.wait_ge(chain, 6 * half + 6)
                nc.vector.tensor_tensor(lowS[:, tiles].rearrange("p t (h r) -> p t h r", r=RR),
                                        low[:, tiles, 0:RD].rearrange("p t (h r) -> p t h r", r=RR),
                                        score[:, tiles].unsqueeze(3).to_broadcast([P, HT, RH, RR]), ALU.mult).then_inc(lowS_ready, 1)
            dve.wait_ge(gate_ready, 1)
            for t in range(NT + 2):
                if t < NT:
                    dve.wait_ge(o_done, t + 1)
                    nc.vector.scalar_tensor_tensor(out=x_res[:, t, :], in0=o_bank[t % 2][:], scalar=gate[:, 0:1], in1=x_res[:, t, :],
                                                   op0=ALU.mult, op1=ALU.add).then_inc(acc_done, 1)
                if 1 <= t <= NT:
                    norm.vector_apply(dve, t - 1)
                if t < NT:
                    dve.wait_ge(acc_done, t + 1)
                    norm.vector_stats(dve, t)
                if t >= 2:
                    norm.vector_low(dve, t - 2)


def ternary_phase(nc, sems, gate_in, up_in, down_in, down_s_in, first_pair, scales_nat, prefetched, x_res, xn_parts, gates, out, ident):
    with ExitStack() as c:
        m = Chip(nc, c)
        nat_i = m.sb("nat_i", [P, 3, 2 * DM], I32)
        nat = m.sb("nat", [P, 3, 2 * DM])
        w_parts = [[m.sb(f"{w}T_{n}", [P, 2, DM], F32R) for n in ("hi", "lo")] for w in ("gate", "up", "down")]
        hid_parts = [m.sb(f"hid_{n}", [P, 2, TOK], F32R) for n in ("hi", "lo")]
        silu = m.sb("silu", [P, 2, HALF])
        hid = m.sb("hid", [P, 2, HALF])
        acc = m.sb("acc", [P, NT, DM])
        scales = m.sb("ff_scales", [P, 2, FFT])
        pair_scale = m.sb("pair_scale", [P, 2])
        down_s = m.sb("down_s", [P, DM])
        down_sg = m.sb("down_sg", [P, DM])
        tr = [m.bank(f"ff_tr{i}") for i in range(2)]
        g_bank = [m.bank(f"ff_g{i}") for i in range(2)]
        u_bank = [m.bank(f"ff_u{i}") for i in range(2)]
        d_bank = [m.bank(f"ff_d{i}") for i in range(2)]
        loaded = [sems(f"ff_loaded{i}") for i in range(3)]
        scales_tr, scales_ready, down_s_loaded, pair_scale_ready = (
            sems("ff_" + n) for n in ("scales_tr", "scales_ready", "down_s", "pair_scale"))
        cast, tr_done, w_hi, w_lo, prod_done, silu_ready, hid_ready, h_hi, h_lo, d_done, acc_done, setup, final, written = (
            sems("ff_" + n) for n in ("cast", "tr", "w_hi", "w_lo", "prod", "silu", "hid", "h_hi", "h_lo", "d", "acc", "setup",
                                      "final", "written"))
        gate_v = gate_in.rearrange("(f p) d -> p f d", p=P)
        up_v = up_in.rearrange("(f p) d -> p f d", p=P)
        down_v = down_in.rearrange("(c p) f -> p c f", p=P)

        TR = [(0, 0), (1, 0), (0, 1), (1, 1), (2, 0), (2, 1)]
        UNITS_FF = [(0, 0), (1, 0), (0, 1), (1, 1)]
        block = c.enter_context(nc.Block())

        class Pair(Group):
            def valid(self):
                return self.register is not None or 0 <= self.added < NFP

        def run_pairs(eng, iteration):
            iteration(Pair(0))
            with eng.Fori(1, NFP - 1) as i:
                iteration(Pair(0, i))
            iteration(Pair(NFP - 1))

        def nxt(i, n=1):
            return Pair(i.added + n, i.register)

        @block.sync
        def _(sp):
            def load(i):
                if not i.valid():
                    return
                wait_count(sp, cast, i, 3, 0)
                for n, view in enumerate((gate_v, up_v)):
                    if i.register is not None or i.added > 0:
                        sp.dma_start(nat_i[:, n].rearrange("p (f d) -> p f d", f=2), view[:, bass.ds(i.number(2, 0), 2), :])\
                          .then_inc(loaded[n], 16)
                sp.dma_start(nat_i[:, 2].rearrange("p (c f) -> p c f", c=KC), down_v[:, :, bass.ds(i.number(2 * P, 0), 2 * P)]).then_inc(loaded[2], 16)

            load(Pair(0))
            sp.dma_start(down_s[:], down_s_in.unsqueeze(0).to_broadcast([P, DM])).then_inc(down_s_loaded, 16)
            load(Pair(1))
            with sp.Fori(1, NFP - 1) as i:
                load(Pair(1, i))
            for t in range(NT):
                sp.wait_ge(final, 2 * t + 2)
                sp.dma_start(out[t * P:(t + 1) * P, :], x_res[:, t, :]).then_inc(written, 16)
            sp.wait_ge(written, 16 * NT)

        @block.tensor
        def _(pe):
            def transpose(i, n):
                if not i.valid():
                    return
                w, f = TR[n]
                wait_count(pe, cast, i, 3, w + 1)
                wait_count(pe, w_lo, i, len(TR), n - 1)
                for k in range(KC):
                    if w < 2:
                        src = nat[:, w, f * DM + k * P:f * DM + (k + 1) * P]
                    else:
                        src = nat[:, w, k * 2 * P + f * P:k * 2 * P + (f + 1) * P]
                    last = nc.tensor.transpose(tr[n % 2][:, k * P:(k + 1) * P], src, ident[:])
                last.then_inc(tr_done, 1)

            def products(i, n):
                f, half = UNITS_FF[n]
                wait_count(pe, w_lo, i, len(TR), 2 * f + 2)
                wait_count(pe, hid_ready, i, 4, n - 1)
                for w, bank in ((0, g_bank), (1, u_bank)):
                    for k in range(KC):
                        for q, (a, b) in enumerate(PASSES):
                            last = nc.tensor.matmul(bank[n % 2][:], w_parts[w][a][:, f, k * P:(k + 1) * P],
                                                    xn_parts[b][:, k, half * HALF:(half + 1) * HALF],
                                                    start=(k == 0 and q == 0), stop=(k == KC - 1 and q == 2))
                last.then_inc(prod_done, 1)

            def down(i, half):
                if not i.valid():
                    return
                wait_count(pe, w_lo, i, len(TR), 6)
                wait_count(pe, h_lo, i, 4, 2 * half + 2)
                for t in range(NT // 2 * half, NT // 2 * (half + 1)):
                    wait_count(pe, acc_done, i, NT, t - 1)
                    for f in range(2):
                        for q, (a, b) in enumerate(PASSES):
                            last = nc.tensor.matmul(d_bank[t % 2][:], hid_parts[a][:, f, t * P:(t + 1) * P], w_parts[2][b][:, f, :],
                                                    start=(f == 0 and q == 0), stop=(f == 1 and q == 2))
                    last.then_inc(d_done, 1)

            def iteration(i):
                transpose(i, 2)
                transpose(i, 3)
                products(i, 0)
                down(nxt(i, -1), 1)
                transpose(i, 4)
                transpose(i, 5)
                products(i, 1)
                products(i, 2)
                last = i.register is None and i.added == NFP - 1
                if not last:
                    transpose(nxt(i), 0)
                    transpose(nxt(i), 1)
                down(i, 0)
                products(i, 3)

            pe.wait_ge(prefetched, PREFETCHED)
            for n in range(2):
                last = nc.tensor.transpose(d_bank[0][:, n * FFT:(n + 1) * FFT], scales_nat[:, n, :], ident[0:FFT, 0:FFT])
            last.then_inc(scales_tr, 1)
            transpose(Pair(0), 0)
            transpose(Pair(0), 1)
            run_pairs(pe, iteration)
            down(Pair(NFP - 1), 1)

        @block.scalar
        def _(act):
            def high_part(i, n):
                if not i.valid():
                    return
                w, f = TR[n]
                wait_count(act, tr_done, i, len(TR), n + 1)
                nc.scalar.activation(w_parts[w][0][:, f, :], tr[n % 2][:], ACT.Copy).then_inc(w_hi, 1)

            def silu_of(i, n):
                f = UNITS_FF[n][0]
                wait_count(act, pair_scale_ready, i, 1, 1)
                wait_count(act, prod_done, i, 4, n + 1)
                nc.scalar.activation(silu[:, n % 2, :], g_bank[n % 2][:], ACT.Silu, scale=pair_scale[:, f:f + 1]).then_inc(silu_ready, 1)

            def hidden_high(i, n):
                f, half = UNITS_FF[n]
                wait_count(act, hid_ready, i, 4, n + 1)
                wait_count(act, d_done, i, NT, NT // 2 * (half + 1) - NT)
                nc.scalar.activation(hid_parts[0][:, f, half * HALF:(half + 1) * HALF], hid[:, n % 2, :], ACT.Copy).then_inc(h_hi, 1)

            def iteration(i):
                nc.scalar.activation(pair_scale[:], scales[:, 0, bass.ds(i.number(2, 0), 2)], ACT.Copy).then_inc(pair_scale_ready, 1)
                high_part(i, 2)
                high_part(i, 3)
                silu_of(i, 0)
                hidden_high(i, 0)
                high_part(i, 4)
                high_part(i, 5)
                silu_of(i, 1)
                hidden_high(i, 1)
                silu_of(i, 2)
                hidden_high(i, 2)
                if not (i.register is None and i.added == NFP - 1):
                    high_part(nxt(i), 0)
                    high_part(nxt(i), 1)
                silu_of(i, 3)
                hidden_high(i, 3)

            act.wait_ge(scales_tr, 1)
            nc.scalar.activation(scales[:], d_bank[0][:, 0:2 * FFT].rearrange("p (n f) -> p n f", n=2), ACT.Copy).then_inc(scales_ready, 1)
            act.wait_ge(scales_ready, 1)
            high_part(Pair(0), 0)
            high_part(Pair(0), 1)
            run_pairs(act, iteration)

        @block.vector
        def _(dve):
            def cast_to_float(i, n):
                wait_count(dve, loaded[n], i, 16, 16 if n == 2 else 0)
                wait_count(dve, tr_done, i, len(TR), (-2, -2, 0)[n])
                first = n < 2 and i.register is None and i.added == 0
                nc.vector.tensor_copy(nat[:, n], first_pair[n] if first else nat_i[:, n]).then_inc(cast, 1)

            def low_part(i, n):
                if not i.valid():
                    return
                w, f = TR[n]
                wait_count(dve, w_hi, i, len(TR), n + 1)
                nc.vector.tensor_tensor(w_parts[w][1][:, f, :], tr[n % 2][:], w_parts[w][0][:, f, :].bitcast(F32), ALU.subtract).then_inc(w_lo, 1)

            def hidden(i, n):
                hidden_product(i, n)
                hidden_low(i, n)

            def hidden_product(i, n):
                f, half = UNITS_FF[n]
                wait_count(dve, silu_ready, i, 4, n + 1)
                wait_count(dve, h_lo, i, 4, n - 1)
                scale = scales[:, 1, bass.ds(i.number(2, f), 1)]
                nc.vector.scalar_tensor_tensor(out=hid[:, n % 2, :], in0=u_bank[n % 2][:], scalar=scale, in1=silu[:, n % 2, :],
                                               op0=ALU.mult, op1=ALU.mult).then_inc(hid_ready, 1)

            def hidden_low(i, n):
                f, half = UNITS_FF[n]
                cols = slice(half * HALF, (half + 1) * HALF)
                wait_count(dve, h_hi, i, 4, n + 1)
                nc.vector.tensor_tensor(hid_parts[1][:, f, cols], hid[:, n % 2, :], hid_parts[0][:, f, cols].bitcast(F32),
                                        ALU.subtract).then_inc(h_lo, 1)

            def accumulate(i, t):
                if not i.valid():
                    return
                wait_count(dve, d_done, i, NT, t + 1)
                nc.vector.tensor_tensor(acc[:, t, :], d_bank[t % 2][:], acc[:, t, :], ALU.add).then_inc(acc_done, 1)
                if i.register is None and i.added == NFP - 1:
                    dve.wait_ge(acc_done, NT * (NFP - 1) + t + 1)
                    nc.vector.tensor_tensor(acc[:, t, :], acc[:, t, :], down_sg[:], ALU.mult).then_inc(final, 1)
                    dve.wait_ge(final, 2 * t + 1)
                    nc.vector.tensor_tensor(x_res[:, t, :], acc[:, t, :], x_res[:, t, :], ALU.add).then_inc(final, 1)

            def iteration(i):
                last = i.register is None and i.added == NFP - 1
                low_part(i, 2)
                low_part(i, 3)
                if not last:
                    cast_to_float(nxt(i), 0)
                    cast_to_float(nxt(i), 1)
                hidden_product(i, 0)
                accumulate(nxt(i, -1), 4)
                hidden_low(i, 0)
                for t in range(5, NT):
                    accumulate(nxt(i, -1), t)
                low_part(i, 4)
                low_part(i, 5)
                if not last:
                    cast_to_float(nxt(i), 2)
                hidden(i, 1)
                hidden(i, 2)
                accumulate(i, 0)
                if not last:
                    low_part(nxt(i), 0)
                accumulate(i, 1)
                if not last:
                    low_part(nxt(i), 1)
                accumulate(i, 2)
                accumulate(i, 3)
                hidden(i, 3)

            dve.wait_ge(prefetched, PREFETCHED)
            for n in range(2):
                cast_to_float(Pair(0), n)
            nc.vector.memset(acc[:], 0.0).then_inc(setup, 1)
            dve.wait_ge(scales_ready, 1)
            low_part(Pair(0), 0)
            low_part(Pair(0), 1)
            cast_to_float(Pair(0), 2)
            dve.wait_ge(down_s_loaded, 16)
            nc.vector.tensor_scalar(down_sg[:], down_s[:], gates[:, 3:4], None, ALU.mult).then_inc(setup, 1)
            dve.wait_ge(setup, 2)
            run_pairs(dve, iteration)
            for t in range(4, NT):
                accumulate(Pair(NFP - 1), t)


def flamingo(nc, a, out):
    with ExitStack() as c:
        m = Chip(nc, c)
        in_use, lasting = [], []

        def sems(name):
            in_use.append(nc.alloc_semaphore(name=name))
            return in_use[-1]

        def lasting_sem(name):
            lasting.append(nc.alloc_semaphore(name=name))
            return lasting[-1]

        def phase_ends():
            nc.clear_and_free_semaphores(in_use)
            in_use.clear()
            nc.all_engine_barrier()

        x_res = m.sb("x_res", [P, NT, DM])
        ctx_parts = m.parts("ctxT", [P, KC, TOK])
        xn_parts = m.parts("xnT", [P, KC, TOK])
        tables = m.sb("tables", [P, 2, TOK])
        rope1 = m.sb("rope1", [P, 2, SEQ])
        ident = m.sb("ident", [P, P])
        gates = m.sb("gates", [P, 4])
        scales_nat = m.sb("scales_nat", [FFT, 2, P])
        prefetched = lasting_sem("prefetched")
        a_nat, wr_nat = tables[:, 0, 0:DM], tables[0:RH, 0, DM:2 * DM]
        b_nat, br = tables[:, 1, 0:DM], tables[:, 1, DM:DM + RH]
        gate_in, up_in, down_in = (a[f"L1_ffn_{n}_t"] for n in ("gate", "up", "down"))

        def prefetch_low_rank(sp):
            sp.dma_start(a_nat, a["L0_ffn_A"].rearrange("h r d -> (h r) d")).then_inc(prefetched, 16)
            sp.dma_start(wr_nat, a["L0_ffn_Wr"]).then_inc(prefetched, 16)
            sp.dma_start(br, a["L0_ffn_br"].unsqueeze(0).to_broadcast([P, RH])).then_inc(prefetched, 16)
            b_rows = b_nat.rearrange("p (c h r) -> p c h r", c=KC, h=RH)
            for e in range(RH):
                sp.dma_start(b_rows[:, :, e, :], a["L0_ffn_B"][e].rearrange("(c p) r -> p c r", p=P)).then_inc(prefetched, 16)

        def prefetch_ternary(sp):
            for n, w_in in enumerate((gate_in, up_in)):
                sp.dma_start(tables[:, n, :].bitcast(I32).rearrange("p (f d) -> p f d", f=2), w_in[0:2 * P, :].rearrange("(f p) d -> p f d", p=P))\
                  .then_inc(prefetched, 16)
            for n, name in enumerate(("gate", "up")):
                sp.dma_start(scales_nat[:, n, :], a[f"L1_ffn_{name}_s"].rearrange("(f p) -> f p", p=P)).then_inc(prefetched, 16)

        def half_of(n):
            return lambda half: tables[:, n, half * HALF:(half + 1) * HALF].rearrange("p (b s) -> p b s", s=SEQ)

        def every_batch(n):
            return lambda half: rope1[:, n, :].unsqueeze(1).to_broadcast([P, BATCH // 2, SEQ])

        with ExitStack() as during_attention:
            m2 = Chip(nc, during_attention)
            x_mask = m2.sb("mask", [P, BATCH, SEQ])
            hidden, shown = (m2.sb(n, [P, BATCH, SEQ], U8) for n in ("hidden", "shown"))
            w = Weights(nc, m2, lasting_sem, [[a[f"L0_xattn_W{n}"] for n in "qkvo"], [a[f"L1_xattn_w{n}"] for n in "qkvo"]])
            sig = AttentionSignals(lasting_sem)
            load_phase(nc, sems, w, a["ctx_4096"].rearrange("b s d -> (b s) d"), a["x"].rearrange("b s d -> (b s) d"),
                       a["pos_BxS2"].rearrange("b s -> (b s)").unsqueeze(0).to_broadcast([P, TOK]), a["tables"], a["table1"],
                       a["g_xattn"].unsqueeze(0).to_broadcast([P, 2]), a["g_ffn"].unsqueeze(0).to_broadcast([P, 2]),
                       a["mask_BxSxS2_ik0"], x_res, ctx_parts, xn_parts, tables, rope1, x_mask, hidden, shown, gates, ident)
            phase_ends()
            attention_phase(nc, sems, 0, w, sig, (shown, hidden), half_of(0), half_of(1), gates[:, 0:1], x_res, xn_parts, ctx_parts,
                            prefetch_low_rank, ident)
            phase_ends()
            low_rank_phase(nc, sems, a_nat, wr_nat, b_nat, br, prefetched, a["mask_BxSxS2_ff0"], x_mask, x_res, xn_parts, gates, ident)
            phase_ends()
            attention_phase(nc, sems, 1, w, sig, (x_mask,), every_batch(0), every_batch(1), gates[:, 1:2], x_res, xn_parts, ctx_parts,
                            prefetch_ternary, ident)
            phase_ends()
        ternary_phase(nc, sems, gate_in, up_in, down_in, a["L1_ffn_down_s"], [tables[:, n, :].bitcast(I32) for n in range(2)], scales_nat,
                      prefetched, x_res, xn_parts, gates, out, ident)
        in_use.extend(lasting)
        phase_ends()


def rotary_tables():
    import numpy as np

    inv_freq = (1.0 / 10000.0 ** (np.arange(0, D, 2, dtype=np.float32) / np.float32(D))).astype(np.float32)
    angle = np.arange(MAX_POS, dtype=np.float32)[:, None] * inv_freq[None, :]
    cos, sin = np.cos(angle).astype(np.float32), np.sin(angle).astype(np.float32)
    cos, sin = np.concatenate([cos, cos], 1), np.concatenate([-sin, sin], 1)
    both = np.stack([cos, sin], 1)
    chunks = both.reshape(MAX_POS // P, P, 2, D).transpose(1, 0, 2, 3)
    return np.ascontiguousarray(chunks), np.ascontiguousarray(both[:SEQ].transpose(2, 1, 0))


_INS = ['x', 'ctx_4096', 'pos_BxS2', 'mask_BxSxS2_ik0', 'mask_BxSxS2_ff0', 'g_xattn', 'g_ffn', 'L0_xattn_Wq', 'L0_xattn_Wk',
        'L0_xattn_Wv', 'L0_xattn_Wo', 'L0_ffn_A', 'L0_ffn_B', 'L0_ffn_Wr', 'L0_ffn_br', 'L1_xattn_wq', 'L1_xattn_wk', 'L1_xattn_wv',
        'L1_xattn_wo', 'L1_ffn_gate_t', 'L1_ffn_up_t', 'L1_ffn_down_t', 'L1_ffn_gate_s', 'L1_ffn_up_s', 'L1_ffn_down_s']


def kernel(**inputs):
    import numpy as _np
    import concourse.bacc as _bacc
    from concourse import mybir as _mybir
    from concourse.bass_utils import run_bass_kernel_spmd as _run

    nc = _bacc.Bacc("TRN2", target_bir_lowering=False, num_devices=1)
    arrays = {name: _np.ascontiguousarray(inputs[name]) for name in _INS}
    arrays["tables"], arrays["table1"] = rotary_tables()
    aps = {name: nc.dram_tensor(f"in_{name}", x.shape, _mybir.dt.from_np(x.dtype), kind="ExternalInput").ap() for name, x in arrays.items()}
    out = nc.dram_tensor("out", (TOK, DM), _mybir.dt.float32, kind="ExternalOutput").ap()
    flamingo(nc, aps, out)
    r = _run(nc, [{f"in_{name}": x for name, x in arrays.items()}], core_ids=[0])
    return r.results[0]["out"].reshape(BATCH, SEQ, DM)
```

```python
from contextlib import ExitStack

import concourse.bass as bass
from concourse import mybir

P = 128
F32 = mybir.dt.float32
F32R = mybir.dt.float32r
I32 = mybir.dt.int32
U8 = mybir.dt.uint8
ALU = mybir.AluOpType
ACT = mybir.ActivationFunctionType
AX_X = mybir.AxisListType.X

BATCH, SEQ, DM = 16, 64, 512
TOK = BATCH * SEQ
NT = TOK // P
KC = DM // P
HALF = TOK // 2
D = 128
NG, HPG = 8, 4
SCALE = float(D) ** -0.5
MAX_POS = 512
EPS = 1e-5
FF = 1792
FFT = FF // P
NFP = FFT // 2
RH, RR = 8, 16
LAYERS = 2
EXACT_IN_HIGH_PART = 2048.0
PREFETCHED_LOW_RANK = 16 * (3 + RH)
PREFETCHED = PREFETCHED_LOW_RANK + 16 * 2


class Group:

    def __init__(self, added, register=None, least=1):
        self.added, self.register, self.least = added, register, least

    def __add__(self, n):
        return Group(self.added + n, self.register, self.least)

    def within(self, first, end):
        return self.register is not None or first <= self.added < end

    def number(self, per_group, c):
        c += self.added * per_group
        return c if self.register is None else self.register * per_group + c

    def count(self, per_group, c):
        assert self.register is None or (self.least + self.added) * per_group + c > 0
        return self.number(per_group, c)


def wait_count(eng, sem, g, per_group, c):
    value = g.count(per_group, c)
    if not isinstance(value, int) or value > 0:
        eng.wait_ge(sem, value)


def back(g, t):
    return (g, t - 1) if t else (g + -1, NT - 1)


def ahead(g, t):
    return (g, t + 1) if t < NT - 1 else (g + 1, 0)


PROJ = {
    2: [("q", 0, 0)],
    3: [("q", 1, 0)],
    4: [("q", 2, 0), ("k", 0, 0)],
    5: [("q", 3, 0), ("v", 0, 0)],
    6: [("q", 0, 1), ("x", 0, 0)],
    7: [("q", 1, 1), ("v", 0, 1)],
    0: [("q", 2, 1), ("k", 0, 1)],
    1: [("q", 3, 1), ("x", 0, 1)],
}
STEPS = [2, 3, 4, 5, 6, 7, 0, 1]
UNITS = [u for t in STEPS for u in PROJ[t]]
ROPES = [u for u in UNITS if u[0] in "qk"]
NU, NR = len(UNITS), len(ROPES)
FIRST_HALF_ROPES = sum(u[2] == 0 for u in ROPES)
SPLIT_Q = {7: (2, 0), 0: (1, 1), 1: (1, 2), 2: (1, 3)}
PASSES = ((0, 0), (0, 1), (1, 0))


def proj_group(g, t):
    return g + 1 if t >= 2 else g


class Chip:

    def __init__(self, nc, ctx):
        self.nc, self.ctx = nc, ctx

    def sb(self, name, shape, dt=F32):
        return self.ctx.enter_context(self.nc.sbuf_tensor(name, shape, dt))

    def parts(self, name, shape):
        return [self.sb(f"{name}_{n}", shape, F32R) for n in ("hi", "lo")]

    def bank(self, name):
        return self.ctx.enter_context(self.nc.psum_tensor(name, [P, 512], F32))


def by_batch(ap):
    return ap.rearrange("p (b s) -> p b s", s=SEQ)


def by_chunk(ap):
    return ap.rearrange("p (c n) -> p c n", c=KC)


class Norm:

    def __init__(self, nc, sems, m, name, x_res, xn_parts, ring, banks, ident):
        self.nc, self.x_res, self.xn_parts, self.ring, self.banks, self.ident = nc, x_res, xn_parts, ring, banks, ident
        self.stats, self.mv = m.sb(name + "stats", [P, 2, 6]), m.sb(name + "mv", [P, NT, 2])
        self.var_eps, self.minus_mean, self.power, self.rstd, self.shift = (
            m.sb(name + n, [P, NT]) for n in ("var_eps", "minus_mean", "power", "rstd", "shift"))
        self.stats_done, self.aggr_done, self.eps_done, self.power_ready, self.rstd_ready, self.xn_ready, self.tr_done, self.hi, self.lo = (
            sems(name + n) for n in ("stats", "aggr", "eps", "power", "rstd", "xn", "tr", "hi", "lo"))

    def vector_stats(self, dve, t, low=None):
        self.nc.vector.bn_stats(self.stats[:, t % 2, :], self.x_res[:, t, :]).then_inc(self.stats_done, 1)
        if low is not None and low >= 0:
            self.vector_low(dve, low)
        self.vector_aggregate(dve, t)
        self.vector_variance(dve, t)

    def vector_aggregate(self, dve, t):
        dve.wait_ge(self.stats_done, t + 1)
        self.nc.vector.bn_aggr(self.mv[:, t, :], self.stats[:, t % 2, :]).then_inc(self.aggr_done, 1)

    def vector_variance(self, dve, t):
        dve.wait_ge(self.aggr_done, t + 1)
        self.nc.vector.tensor_scalar(self.var_eps[:, t:t + 1], self.mv[:, t, 1:2], EPS, None, ALU.add).then_inc(self.eps_done, 1)
        self.nc.vector.tensor_scalar(self.minus_mean[:, t:t + 1], self.mv[:, t, 0:1], -1.0, None, ALU.mult).then_inc(self.eps_done, 1)

    def pool_setup(self, pool):
        self.nc.gpsimd.memset(self.power[:], -0.5).then_inc(self.power_ready, 1)
        pool.wait_ge(self.power_ready, 1)

    def pool_rstd(self, pool, t):
        pool.wait_ge(self.eps_done, 2 * t + 2)
        self.nc.gpsimd.tensor_tensor(self.rstd[:, t:t + 1], self.var_eps[:, t:t + 1], self.power[:, t:t + 1], ALU.pow).then_inc(self.rstd_ready, 1)
        pool.wait_ge(self.rstd_ready, 2 * t + 1)
        self.nc.gpsimd.tensor_tensor(self.shift[:, t:t + 1], self.minus_mean[:, t:t + 1], self.rstd[:, t:t + 1], ALU.mult).then_inc(self.rstd_ready, 1)

    def scalar_apply(self, act, t):
        act.wait_ge(self.rstd_ready, 2 * t + 2)
        if t >= 2:
            act.wait_ge(self.tr_done, t - 1)
        self.nc.scalar.activation(self.ring[:, t % 2, :], self.x_res[:, t, :], ACT.Identity, bias=self.shift[:, t:t + 1],
                                  scale=self.rstd[:, t:t + 1]).then_inc(self.xn_ready, 1)

    def tensor_transpose(self, pe, t):
        n = len(self.banks)
        pe.wait_ge(self.xn_ready, t + 1)
        if t >= n:
            pe.wait_ge(self.lo, t - n + 1)
        for k in range(KC):
            last = self.nc.tensor.transpose(self.banks[t % n][:, k * P:(k + 1) * P], self.ring[:, t % 2, k * P:(k + 1) * P], self.ident[:])
        last.then_inc(self.tr_done, 1)

    def scalar_high(self, act, t):
        act.wait_ge(self.tr_done, t + 1)
        self.nc.scalar.activation(self.xn_parts[0][:, :, t * P:(t + 1) * P], by_chunk(self.banks[t % len(self.banks)][:]),
                                  ACT.Copy).then_inc(self.hi, 1)

    def vector_low(self, dve, t):
        dve.wait_ge(self.hi, t + 1)
        self.nc.vector.tensor_tensor(self.xn_parts[1][:, :, t * P:(t + 1) * P], by_chunk(self.banks[t % len(self.banks)][:]),
                                     self.xn_parts[0][:, :, t * P:(t + 1) * P].bitcast(F32), ALU.subtract).then_inc(self.lo, 1)


class Weights:

    def __init__(self, nc, m, sem, arrays):
        self.nc, self.arrays = nc, arrays
        self.wq_raw, self.wq = m.sb("wq_raw", [P, 2, KC, D]), m.parts("wq", [P, HPG, KC, D])
        self.wk_raw, self.wk = m.sb("wk_raw", [P, KC, D]), m.parts("wk", [P, KC, D])
        self.wv_raw, self.wv = m.sb("wv_raw", [P, KC, D]), m.parts("wv", [P, KC, D])
        self.wo_raw, self.wo = m.sb("wo_raw", [P, HPG, DM]), m.parts("wo", [P, HPG, DM])
        self.wq_loaded = [sem(f"wq_loaded{i}") for i in range(2)]
        self.wk_loaded, self.wv_loaded, self.wo_loaded = (sem(n) for n in ("wk_loaded", "wv_loaded", "wo_loaded"))
        self.wq_hi, self.wq_lo, self.wk_hi, self.wk_lo, self.wv_hi, self.wv_lo, self.wo_hi, self.wo_lo_pool, self.wo_lo_dve = (
            sem(n) for n in ("wq_hi", "wq_lo", "wk_hi", "wk_lo", "wv_hi", "wv_lo", "wo_hi", "wo_lo_pool", "wo_lo_dve"))

    def source(self, which, g, layer):
        if g.register is None:
            layer = g.added // NG
        return self.arrays[layer][which], g + -NG * layer

    def load_wq(self, sp, g, h, layer):
        w, i = self.source(0, g, layer)
        wait_count(sp, self.wq_lo, g, HPG, h - 1)
        sp.dma_start(self.wq_raw[:, h % 2], w.rearrange("(c p) n -> p c n", p=P)[:, :, bass.ds(i.number(HPG * D, h * D), D)])\
          .then_inc(self.wq_loaded[h % 2], 16)

    def load_wk(self, sp, g, layer):
        w, i = self.source(1, g, layer)
        wait_count(sp, self.wk_lo, g, 1, 0)
        sp.dma_start(self.wk_raw[:], w.rearrange("(c p) n -> p c n", p=P)[:, :, bass.ds(i.number(D, 0), D)]).then_inc(self.wk_loaded, 16)

    def load_wv(self, sp, g, layer):
        w, i = self.source(2, g, layer)
        wait_count(sp, self.wv_lo, g, 1, 0)
        sp.dma_start(self.wv_raw[:], w.rearrange("(c p) n -> p c n", p=P)[:, :, bass.ds(i.number(D, 0), D)]).then_inc(self.wv_loaded, 16)

    def load_wo(self, sp, g, layer):
        w, i = self.source(3, g, layer)
        wait_count(sp, self.wo_lo_pool, g, 2, 0)
        wait_count(sp, self.wo_lo_dve, g, 2, 0)
        sp.dma_start(self.wo_raw[:], w[bass.ds(i.number(HPG * D, 0), HPG * D), :].rearrange("(h p) n -> p h n", p=P)).then_inc(self.wo_loaded, 16)


    def high_wq(self, act, g, h):
        wait_count(act, self.wq_loaded[h % 2], g, 32, 16 * (h // 2) + 16)
        self.nc.scalar.activation(self.wq[0][:, h], self.wq_raw[:, h % 2], ACT.Copy).then_inc(self.wq_hi, 1)

    def high_wk(self, act, g):
        wait_count(act, self.wk_loaded, g, 16, 16)
        self.nc.scalar.activation(self.wk[0][:], self.wk_raw[:], ACT.Copy).then_inc(self.wk_hi, 1)

    def high_wv(self, act, g):
        wait_count(act, self.wv_loaded, g, 16, 16)
        self.nc.scalar.activation(self.wv[0][:], self.wv_raw[:], ACT.Copy).then_inc(self.wv_hi, 1)

    def high_wo(self, act, g):
        wait_count(act, self.wo_loaded, g, 16, 16)
        for h in (0, 2, 1, 3):
            self.nc.scalar.activation(self.wo[0][:, h], self.wo_raw[:, h], ACT.Copy).then_inc(self.wo_hi, 1)

    def low_wq(self, pool, g, h):
        wait_count(pool, self.wq_hi, g, HPG, h + 1)
        self.nc.gpsimd.tensor_tensor(self.wq[1][:, h], self.wq_raw[:, h % 2], self.wq[0][:, h].bitcast(F32), ALU.subtract).then_inc(self.wq_lo, 1)

    def low_wk(self, pool, g):
        wait_count(pool, self.wk_hi, g, 1, 1)
        self.nc.gpsimd.tensor_tensor(self.wk[1][:], self.wk_raw[:], self.wk[0][:].bitcast(F32), ALU.subtract).then_inc(self.wk_lo, 1)

    def low_wv(self, pool, g):
        wait_count(pool, self.wv_hi, g, 1, 1)
        self.nc.gpsimd.tensor_tensor(self.wv[1][:], self.wv_raw[:], self.wv[0][:].bitcast(F32), ALU.subtract).then_inc(self.wv_lo, 1)

    def low_wo_pool(self, pool, g):
        for i, h in enumerate((0, 1)):
            wait_count(pool, self.wo_hi, g, HPG, 2 * i + 1)
            self.nc.gpsimd.tensor_tensor(self.wo[1][:, h], self.wo_raw[:, h], self.wo[0][:, h].bitcast(F32), ALU.subtract).then_inc(self.wo_lo_pool, 1)

    def low_wo_vector(self, dve, g):
        for i, h in enumerate((2, 3)):
            wait_count(dve, self.wo_hi, g, HPG, 2 * i + 2)
            self.nc.vector.tensor_tensor(self.wo[1][:, h], self.wo_raw[:, h], self.wo[0][:, h].bitcast(F32), ALU.subtract).then_inc(self.wo_lo_dve, 1)


def load_phase(nc, sems, w, ctx_in, x_in, pos_in, tab_in, tab1_in, gx_in, gf_in, mask_in, x_res, ctx_parts, xn_parts, tables, rope1,
               x_mask, hidden, shown, gates, ident):
    with ExitStack() as c:
        m = Chip(nc, c)
        CTX_SLOTS = 6
        ctx_nat = m.sb("ctx_nat", [P, CTX_SLOTS, DM])
        ring = m.sb("ld_ring", [P, 2, DM])
        pos_i = m.sb("pos_i", [P, TOK], I32)
        posf = m.sb("posf", [P, TOK])
        wrap = pos_i[:].bitcast(F32)
        rowid_i = m.sb("rowid_i", [P, MAX_POS // P], I32)
        rowid = m.sb("rowid", [P, MAX_POS // P])
        onehot = m.sb("onehot", [P, MAX_POS // P, TOK], F32R)
        tab = m.sb("tab", [P, MAX_POS // P, 2, D])
        tab_parts = m.parts("tab", [P, MAX_POS // P, 2, D])
        gate_raw = m.sb("gate_raw", [P, 4])
        tr = [m.bank(f"ld_tr{i}") for i in range(3)]
        norm = Norm(nc, sems, m, "n0_", x_res, xn_parts, ring, [m.bank(f"ld_nt{i}") for i in range(3)], ident)
        tb = [m.bank(f"ld_tb{i}") for i in range(2)]
        x_loaded = [sems(f"ld_x{t}") for t in range(NT)]
        ctx_loaded = [sems(f"ld_ctx{t}") for t in range(NT)]
        pos_loaded, tab_loaded, rope_loaded, gate_loaded, mask_loaded = (sems("ld_" + n) for n in ("pos", "tab", "rope", "gate", "mask"))
        ident_zero, ident_ready, rowid_ready = (sems("ld_" + n) for n in ("id0", "id1", "rowid"))
        ctx_tr, ctx_hi, ctx_lo = (sems("ld_" + n) for n in ("ctx_tr", "ctx_hi", "ctx_lo"))
        tab_hi_ready, tab_lo_ready, pos_step, onehot_ready, tab_mm, tab_out, gate_done, mask_done = (
            sems("ld_" + n) for n in ("tab_hi", "tab_lo", "pos_step", "onehot", "tab_mm", "tab_out", "gates", "mask_done"))
        first = Group(0)
        block = c.enter_context(nc.Block())

        @block.sync
        def _(sp):
            sp.dma_start(pos_i[:], pos_in).then_inc(pos_loaded, 16)
            for t in range(NT):
                sp.dma_start(x_res[:, t, :], x_in[t * P:(t + 1) * P, :]).then_inc(x_loaded[t], 16)
                if t >= 2:
                    if t >= CTX_SLOTS:
                        sp.wait_ge(ctx_tr, t - CTX_SLOTS + 1)
                    sp.dma_start(ctx_nat[:, t % CTX_SLOTS, :], ctx_in[t * P:(t + 1) * P, :]).then_inc(ctx_loaded[t], 16)
                if t == 3:
                    sp.dma_start(tab[:], tab_in).then_inc(tab_loaded, 16)
            w.load_wq(sp, first, 0, 0)
            w.load_wq(sp, first, 1, 0)
            w.load_wk(sp, first, 0)
            w.load_wv(sp, first, 0)
            for half in range(2):
                sp.dma_start(x_mask[half * SEQ:(half + 1) * SEQ].bitcast(I32), mask_in.rearrange("b q k -> q b k")).then_inc(mask_loaded, 16)
            w.load_wo(sp, first, 0)
            w.load_wq(sp, first, 2, 0)
            sp.dma_start(rope1[:], tab1_in).then_inc(rope_loaded, 16)
            sp.wait_ge(rope_loaded, 16)

        @block.scalar
        def _(act):
            def table_out(n):
                act.wait_ge(tab_mm, n + 1)
                nc.scalar.activation(tables[:, n // 2, n % 2 * HALF:(n % 2 + 1) * HALF], tb[n % 2][:], ACT.Copy).then_inc(tab_out, 1)

            for t in range(2):
                act.dma_start(ctx_nat[:, t % CTX_SLOTS, :], ctx_in[t * P:(t + 1) * P, :]).then_inc(ctx_loaded[t], 16)
            act.dma_start(gate_raw[:, 0:2], gx_in).then_inc(gate_loaded, 16)
            act.dma_start(gate_raw[:, 2:4], gf_in).then_inc(gate_loaded, 16)
            norm.scalar_apply(act, 0)
            for t in range(NT + 2):
                if t < NT:
                    act.wait_ge(ctx_tr, t + 1)
                    nc.scalar.activation(ctx_parts[0][:, :, t * P:(t + 1) * P], by_chunk(tr[t % 3][:]), ACT.Copy).then_inc(ctx_hi, 1)
                if t == 3:
                    act.wait_ge(tab_loaded, 16)
                    nc.scalar.activation(tab_parts[0][:], tab[:], ACT.Copy).then_inc(tab_hi_ready, 1)
                if t >= 2:
                    norm.scalar_high(act, t - 2)
                if t + 1 < NT:
                    norm.scalar_apply(act, t + 1)
                if t == 6:
                    w.high_wq(act, first, 0)
                if t >= 6:
                    table_out(t - 6)
            act.wait_ge(gate_loaded, 32)
            nc.scalar.activation(gates[:], gate_raw[:], ACT.Tanh).then_inc(gate_done, 1)

        @block.gpsimd
        def _(pool):
            nc.gpsimd.memset(ident[:], 0.0).then_inc(ident_zero, 1)
            pool.wait_ge(ident_zero, 1)
            nc.gpsimd.affine_select(out=ident[:], in_=ident[:], compare_op=ALU.not_equal, fill=1.0, base=0,
                                    pattern=[[-1, P]], channel_multiplier=1).then_inc(ident_ready, 1)
            nc.gpsimd.iota(rowid_i[:], pattern=[[P, MAX_POS // P]], base=0, channel_multiplier=1).then_inc(rowid_ready, 1)
            norm.pool_setup(pool)
            for t in range(NT):
                norm.pool_rstd(pool, t)
                if t == 4:
                    pool.wait_ge(tab_hi_ready, 1)
                    nc.gpsimd.tensor_tensor(tab_parts[1][:], tab[:], tab_parts[0][:].bitcast(F32), ALU.subtract).then_inc(tab_lo_ready, 1)
            w.low_wq(pool, first, 0)

        @block.vector
        def _(dve):
            def low_ctx(t):
                dve.wait_ge(ctx_hi, t + 1)
                nc.vector.tensor_tensor(ctx_parts[1][:, :, t * P:(t + 1) * P], by_chunk(tr[t % 3][:]),
                                        ctx_parts[0][:, :, t * P:(t + 1) * P].bitcast(F32), ALU.subtract).then_inc(ctx_lo, 1)

            dve.wait_ge(rowid_ready, 1)
            nc.vector.tensor_copy(rowid[:], rowid_i[:]).then_inc(pos_step, 1)
            dve.wait_ge(pos_loaded, 16)
            nc.vector.tensor_copy(posf[:], pos_i[:]).then_inc(pos_step, 1)
            dve.wait_ge(pos_step, 2)
            nc.vector.tensor_scalar(wrap, posf[:], 0.0, float(MAX_POS), ALU.is_lt, ALU.mult).then_inc(pos_step, 1)
            dve.wait_ge(x_loaded[0], 16)
            norm.vector_stats(dve, 0)
            dve.wait_ge(pos_step, 3)
            nc.vector.tensor_tensor(posf[:], posf[:], wrap, ALU.add).then_inc(pos_step, 1)
            dve.wait_ge(pos_step, 4)
            nc.vector.tensor_scalar(wrap, posf[:], 0.0, float(MAX_POS - 1), ALU.max, ALU.min).then_inc(pos_step, 1)
            dve.wait_ge(x_loaded[1], 16)
            norm.vector_stats(dve, 1)
            dve.wait_ge(pos_step, 5)
            for q in range(MAX_POS // P):
                nc.vector.tensor_scalar(onehot[:, q, :], wrap, rowid[:, q:q + 1], None, ALU.is_equal).then_inc(onehot_ready, 1)
            for t in range(NT + 2):
                if t < NT:
                    low_ctx(t)
                if t + 2 < NT:
                    dve.wait_ge(x_loaded[t + 2], 16)
                    norm.vector_stats(dve, t + 2, t - 2)
                else:
                    norm.vector_low(dve, t - 2)
            dve.wait_ge(mask_loaded, 32)
            nc.vector.tensor_scalar(hidden[:], x_mask[:].bitcast(I32), 0, None, ALU.is_equal).then_inc(mask_done, 1)
            nc.vector.tensor_scalar(shown[:], x_mask[:].bitcast(I32), 0, None, ALU.not_equal).then_inc(mask_done, 1)

        @block.tensor
        def _(pe):
            def rotary_table(pe, n):
                table, h = n // 2, n % 2
                if n == 0:
                    pe.wait_ge(onehot_ready, MAX_POS // P)
                    pe.wait_ge(tab_lo_ready, 1)
                if table:
                    pe.wait_ge(tab_out, h + 1)
                steps = [(q, part) for q in range(MAX_POS // P) for part in tab_parts]
                for i, (q, part) in enumerate(steps):
                    last = nc.tensor.matmul(tb[h][:], part[:, q, table, :], onehot[:, q, h * HALF:(h + 1) * HALF],
                                            start=(i == 0), stop=(i == len(steps) - 1))
                last.then_inc(tab_mm, 1)

            pe.wait_ge(ident_ready, 1)
            for t in range(NT + 1):
                if t < NT:
                    pe.wait_ge(ctx_loaded[t], 16)
                    if t >= 3:
                        pe.wait_ge(ctx_lo, t - 2)
                    for k in range(KC):
                        last = nc.tensor.transpose(tr[t % 3][:, k * P:(k + 1) * P], ctx_nat[:, t % CTX_SLOTS, k * P:(k + 1) * P], ident[:])
                    last.then_inc(ctx_tr, 1)
                if t >= 1:
                    norm.tensor_transpose(pe, t - 1)
                if t >= 5:
                    rotary_table(pe, t - 5)


class AttentionSignals:

    def __init__(self, sem):
        self.proj_done, self.s_done, self.t_done, self.pv_done, self.o_done = (
            sem(n) for n in ("proj_done", "s_done", "t_done", "pv_done", "o_done"))
        self.rot_ready, self.sin_done, self.cos_done, self.rope_done, self.vT_ready, self.v_hi, self.v_lo = (
            sem(n) for n in ("rot_ready", "sin_done", "cos_done", "rope_done", "vT_ready", "v_hi", "v_lo"))
        self.s_read, self.s_masked, self.mx_ready, self.shifted, self.exp_ready, self.total_ready, self.inv_ready, self.prob_ready = (
            sem(n) for n in ("s_read", "s_masked", "mx_ready", "shifted", "exp_ready", "total_ready", "inv_ready", "prob_ready"))
        self.probT_hi, self.probT_lo, self.oT_hi, self.oT_lo, self.acc_done = (
            sem(n) for n in ("probT_hi", "probT_lo", "oT_hi", "oT_lo", "acc_done"))


class TernaryRange:
    DOWN, GATE, UP = range(3)
    GROUPS = NFP
    LOADS = {2: (DOWN, UP), 6: (GATE,)}
    LOOKS = {4: ((DOWN, 0),), 5: ((DOWN, 1), (UP, 0)), 7: ((UP, 1), (GATE, 0)), 0: ((GATE, 1),)}
    ORDER = sum(LOOKS.values(), ())
    PER_GROUP = len(ORDER)

    def __init__(self, nc, sem, first_group, places, largest, gate_in, up_in, down_in):
        self.nc, self.first_group, self.places, self.largest = nc, first_group, places, largest
        self.views = (down_in.rearrange("(c p) f -> p c f", p=P), gate_in.rearrange("(f p) d -> p f d", p=P), up_in.rearrange("(f p) d -> p f d", p=P))
        self.loaded = [sem(f"range_{n}_loaded") for n in ("down", "gate", "up")]
        self.looked, self.folded = sem("range_looked"), sem("range_folded")

    def due(self, g):
        return g.within(self.first_group, self.first_group + self.GROUPS)

    def load(self, sp, g, t):
        if t not in self.LOADS or not self.due(g):
            return
        n = g + -self.first_group
        pair = n + 1 if n.register is not None else Group((n.added + 1) % NFP)
        for which in self.LOADS[t]:
            if which == self.GATE:
                wait_count(sp, self.looked, n, self.PER_GROUP, self.ORDER.index((self.DOWN, 1)) + 1)
            else:
                wait_count(sp, self.looked, n, self.PER_GROUP, 0)
            view = self.views[which]
            if which == self.DOWN:
                place, src = self.places[0].rearrange("p (c f) -> p c f", c=KC), view[:, :, bass.ds(pair.number(2 * P, 0), 2 * P)]
            else:
                place, src = self.places[which - self.GATE].rearrange("p (f d) -> p f d", f=2), view[:, bass.ds(pair.number(2, 0), 2), :]
            sp.dma_start(place, src).then_inc(self.loaded[which], 16)

    def look(self, dve, g, t):
        if t < 2:
            g = g + -1
        if t not in self.LOOKS or not self.due(g):
            return
        n = g + -self.first_group
        for which, half in self.LOOKS[t]:
            c = self.ORDER.index((which, half))
            wait_count(dve, self.loaded[which], n, 16, 16)
            src = self.places[which == self.UP][:, half * HALF:(half + 1) * HALF]
            self.nc.vector.tensor_reduce(self.largest[:, 1, c:c + 1], src, AX_X, ALU.max, apply_absolute_value=True).then_inc(self.looked, 1)
        if c == self.PER_GROUP - 1:
            wait_count(dve, self.looked, n, self.PER_GROUP, self.PER_GROUP)
            wait_count(dve, self.folded, n, 1, 1)
            self.nc.vector.tensor_tensor(self.largest[:, 0, :], self.largest[:, 0, :], self.largest[:, 1, :], ALU.max).then_inc(self.folded, 1)

    def setup(self, dve):
        self.nc.vector.memset(self.largest[:, 0, :], 0.0).then_inc(self.folded, 1)


def attention_phase(nc, sems, layer, w, sig, masks, cos, sin, gate, x_res, xn_parts, ctx_parts, prefetch, int_range, ident):
    first_group, end_group = layer * NG, (layer + 1) * NG
    with ExitStack() as c:
        m = Chip(nc, c)
        name = f"a{layer}_"
        qT = m.sb(name + "qT", [P, BATCH, HPG, SEQ])
        kT = m.sb(name + "kT", [P, BATCH, SEQ])
        vT = m.sb(name + "vT", [P, HALF])
        v = m.parts(name + "v", [P, NT, D])
        rot = m.sb(name + "rot", [P, 2, HALF])
        qcos = m.sb(name + "qcos", [P, HALF])
        sc = m.sb(name + "sc", [P, 256])
        prob = m.sb(name + "prob", [P, 2, 256])
        probT = m.parts(name + "probT", [P, 2, 256])
        oT = m.parts(name + "oT", [P, 2, HPG, 2, SEQ])
        mx, total, inv = (m.sb(name + n, [P, 4]) for n in ("mx", "total", "inv"))
        proj_bank = [m.bank(f"{name}proj{i}") for i in range(2)]
        s_bank, t_bank, o_bank = (m.bank(name + n) for n in ("s", "t", "o"))
        pv_bank = [m.bank(f"{name}pv{i}") for i in range(2)]
        norm = Norm(nc, sems, m, f"n{layer + 1}_" if layer == 0 else "n3_", x_res, xn_parts, rot, proj_bank, ident)

        def in_layer(g):
            return g.within(first_group, end_group)

        def weights_due(g):
            return g.within(first_group + 1, min(end_group, LAYERS * NG - 1) + 1)

        def wo_due(g):
            return g.within(first_group + 1, end_group)

        def in_prologue(g):
            return g.register is None and g.added == first_group - 1

        def norm_step(g, t):
            return -1 if g.register is not None else (g.added - end_group + 1) * NT + t

        def by_pool(g, t):
            return g.register is None and g.added == end_group - 1 and 1 <= t < NT - 1

        def heads_of(unit):
            kind, h, half = unit
            b = slice(half * (BATCH // 2), (half + 1) * (BATCH // 2))
            return qT[:, b, h, :] if kind == "q" else kT[:, b, :]

        def unit_at(g, t, which):
            if len(PROJ[t]) > which and in_layer(proj_group(g, t)):
                return proj_group(g, t), PROJ[t][which]
            return None

        o_scaled = sems(name + "o_scaled")
        scaled = (qcos, vT)
        block = c.enter_context(nc.Block())

        def run_steps(eng, step):
            def body(g):
                for t in STEPS:
                    step(g if t >= 2 else g + 1, t)

            body(Group(first_group - 1))
            body(Group(first_group))
            with eng.Fori(first_group + 1, end_group - 2) as g:
                body(Group(0, g, first_group + 1))
            body(Group(end_group - 2))
            body(Group(end_group - 1))
            step(Group(end_group), 2)
            step(Group(end_group), 3)

        @block.sync
        def _(sp):
            def step(g, t):
                if t == 2:
                    for h in range(2):
                        if weights_due(g + 2):
                            w.load_wq(sp, g + 2, h, layer)
                elif t == 3 and weights_due(g + 2):
                    w.load_wv(sp, g + 2, layer)
                elif t == 4 and weights_due(g + 2):
                    w.load_wk(sp, g + 2, layer)
                elif t == 0 and weights_due(g + 1):
                    w.load_wq(sp, g + 1, 2, layer)
                elif t == 1 and weights_due(g + 1):
                    w.load_wq(sp, g + 1, 3, layer)
                    w.load_wo(sp, g + 1, layer)
                if int_range:
                    int_range.load(sp, g, t)

            if layer == 0:
                w.load_wq(sp, Group(0), 3, layer)
            run_steps(sp, step)
            if layer == 0:
                sp.wait_ge(sig.rope_done, end_group * NR)
            prefetch(sp)

        @block.tensor
        def _(pe):
            def project(g, t, which):
                if (found := unit_at(g, t, which)) is None:
                    return
                g, unit = found
                kind, h, half = unit
                j = UNITS.index(unit)
                before, gb = (UNITS[j - 2], g) if j >= 2 else (UNITS[j - 2], g + -1)
                if before[0] == "v":
                    wait_count(pe, sig.vT_ready, gb, 2, before[2] + 1)
                elif before[0] == "x":
                    wait_count(pe, sig.v_lo, gb, 2, before[2] + 1)
                else:
                    wait_count(pe, sig.cos_done, gb, NR, ROPES.index(before) + 1)
                out = proj_bank[j % 2]
                if kind == "x":
                    wait_count(pe, sig.vT_ready, g, 2, half + 1)
                    for i in range(NT // 2):
                        last = nc.tensor.transpose(out[:, i * P:(i + 1) * P], vT[:, i * P:(i + 1) * P], ident[:])
                else:
                    if kind == "q":
                        wait_count(pe, w.wq_lo, g, HPG, h + 1)
                        weights, moving = [part[:, h] for part in w.wq], xn_parts
                    elif kind == "k":
                        wait_count(pe, w.wk_lo, g, 1, 1)
                        weights, moving = [part[:] for part in w.wk], ctx_parts
                    else:
                        wait_count(pe, w.wv_lo, g, 1, 1)
                        weights, moving = [part[:] for part in w.wv], ctx_parts
                    for k in range(KC):
                        for n, (a, b) in enumerate(PASSES):
                            last = nc.tensor.matmul(out[:], weights[a][:, k, :], moving[b][:, k, half * HALF:(half + 1) * HALF],
                                                    start=(k == 0 and n == 0), stop=(k == KC - 1 and n == 2))
                last.then_inc(sig.proj_done, 1)

            def scores(g, t):
                if not in_layer(g):
                    return
                wait_count(pe, sig.rope_done, g, NR, NR if t >= NT // 2 else FIRST_HALF_ROPES)
                wait_count(pe, sig.s_read, g, NT, t)
                for pair in range(HPG // 2):
                    for b2 in range(2):
                        b = 2 * t + b2
                        last = nc.tensor.matmul(s_bank[:, (2 * pair + b2) * SEQ:(2 * pair + b2 + 1) * SEQ],
                                                qT[:, b, 2 * pair:2 * pair + 2, :].rearrange("p h s -> p (h s)"), kT[:, b, :],
                                                start=True, stop=True)
                last.then_inc(sig.s_done, 1)

            def transpose_probs(g, t):
                if not in_layer(g):
                    return
                wait_count(pe, sig.prob_ready, g, NT, t + 1)
                wait_count(pe, sig.probT_lo, g, NT, t)
                for pair in range(HPG // 2):
                    last = nc.tensor.transpose(t_bank[:, pair * P:(pair + 1) * P], prob[:, t % 2, pair * P:(pair + 1) * P], ident[:])
                last.then_inc(sig.t_done, 1)

            def probs_values(g, t):
                if not in_layer(g):
                    return
                wait_count(pe, sig.probT_lo, g, NT, t + 1)
                wait_count(pe, sig.v_lo, g, 2, t // (NT // 2) + 1)
                wait_count(pe, sig.oT_lo, g, 2 * NT, 2 * t)
                for b2 in range(2):
                    rows = slice(b2 * SEQ, (b2 + 1) * SEQ)
                    for n, (a, b) in enumerate(PASSES):
                        last = nc.tensor.matmul(pv_bank[b2][:, 0:256], v[a][rows, t, :], probT[b][rows, t % 2, :], start=(n == 0), stop=(n == 2))
                last.then_inc(sig.pv_done, 1)

            def output(g, t):
                if not in_layer(g):
                    return
                wait_count(pe, sig.oT_lo, g, 2 * NT, 2 * t + 2)
                wait_count(pe, w.wo_lo_pool, g, 2, 2)
                wait_count(pe, w.wo_lo_dve, g, 2, 2)
                if by_pool(g, t - 1):
                    pe.wait_ge(o_scaled, t - 1)
                else:
                    wait_count(pe, sig.acc_done, g, NT, t)
                for h in range(HPG):
                    for n, (a, b) in enumerate(PASSES):
                        last = nc.tensor.matmul(o_bank[:], oT[a][:, t % 2, h].rearrange("p b s -> p (b s)"), w.wo[b][:, h, :],
                                                start=(h == 0 and n == 0), stop=(h == HPG - 1 and n == 2))
                last.then_inc(sig.o_done, 1)

            def step(g, t):
                scores(*ahead(g, t))
                transpose_probs(g, t)
                project(g, t, 0)
                output(*back(g, t))
                probs_values(g, t)
                project(g, t, 1)
                n = norm_step(g, t)
                if n == 3:
                    pe.wait_ge(sig.v_lo, 2 * end_group)
                    pe.wait_ge(sig.cos_done, NR * end_group)
                if 3 <= n < NT + 3:
                    norm.tensor_transpose(pe, n - 3)

            run_steps(pe, step)

        @block.scalar
        def _(act):
            def rotate_or_copy(g, t, which):
                if (found := unit_at(g, t, which)) is None:
                    return
                g, unit = found
                kind, _, half = unit
                bank = proj_bank[UNITS.index(unit) % 2]
                wait_count(act, sig.proj_done, g, NU, UNITS.index(unit) + 1)
                if kind == "v":
                    nc.scalar.activation(vT[:], bank[:], ACT.Copy).then_inc(sig.vT_ready, 1)
                elif kind == "x":
                    wait_count(act, sig.pv_done, g + -1, NT, NT // 2 * (half + 1))
                    tiles = slice(NT // 2 * half, NT // 2 * (half + 1))
                    nc.scalar.activation(v[0][:, tiles, :], bank[:].rearrange("p (t d) -> p t d", d=D), ACT.Copy).then_inc(sig.v_hi, 1)
                else:
                    r = ROPES.index(unit)
                    wait_count(act, sig.rope_done, g, NR, r - 1)
                    nc.scalar.activation(rot[0:64, r % 2, :], bank[64:128, :], ACT.Copy).then_inc(sig.rot_ready, 1)
                    nc.scalar.activation(rot[64:128, r % 2, :], bank[0:64, :], ACT.Copy).then_inc(sig.rot_ready, 1)

            def exponentials(g, t):
                if not in_layer(g):
                    return
                wait_count(act, sig.shifted, g, NT, t + 1)
                nc.scalar.activation(prob[:, t % 2, :], sc[:], ACT.Exp).then_inc(sig.exp_ready, 1)

            def probs_high(g, t):
                if not in_layer(g):
                    return
                wait_count(act, sig.t_done, g, NT, t + 1)
                nc.scalar.activation(probT[0][:, t % 2, :], t_bank[:, 0:256], ACT.Copy).then_inc(sig.probT_hi, 1)

            def heads_high(g, t):
                if not in_layer(g):
                    return
                wait_count(act, sig.pv_done, g, NT, t + 1)
                for b2 in range(2):
                    nc.scalar.activation(oT[0][:, t % 2, :, b2, :], by_batch(pv_bank[b2][:, 0:256]), ACT.Copy).then_inc(sig.oT_hi, 1)

            def scale_output(g, t):
                if by_pool(g, t):
                    if t == 1:
                        act.wait_ge(sig.rope_done, NR * end_group)
                        act.wait_ge(sig.v_lo, 2 * end_group)
                    act.wait_ge(sig.o_done, g.added * NT + t + 1)
                    if t >= 3:
                        act.wait_ge(sig.acc_done, g.added * NT + t - 1)
                    nc.scalar.activation(scaled[t % 2][:], o_bank[:], ACT.Copy, scale=gate).then_inc(o_scaled, 1)

            def split_wq(g, h):
                if weights_due(g):
                    wait_count(act, sig.proj_done, g + -1, NU, UNITS.index(("q", h, 1)) + 1)
                    w.high_wq(act, g, h)

            def split_k_or_v(g, kind):
                if weights_due(g):
                    wait_count(act, sig.proj_done, g + -1, NU, UNITS.index((kind, 0, 1)) + 1)
                    (w.high_wk if kind == "k" else w.high_wv)(act, g)

            def split_wo(g):
                if wo_due(g) or g.added == first_group:
                    wait_count(act, sig.o_done, g, NT, 0)
                    w.high_wo(act, g)

            def step(g, t):
                n = norm_step(g, t)
                gb, tb = back(g, t)
                heads_high(gb, tb)
                rotate_or_copy(gb, tb, 1)
                if 4 <= n < NT + 4:
                    norm.scalar_high(act, n - 4)
                probs_high(g, t)
                if 3 <= n < NT + 3:
                    norm.scalar_apply(act, n - 3)
                exponentials(*ahead(g, t))
                rotate_or_copy(g, t, 0)
                scale_output(gb, tb)
                if t in SPLIT_Q:
                    split_wq(g + SPLIT_Q[t][0], SPLIT_Q[t][1])
                if t == 2:
                    split_k_or_v(g + 1, "v")
                if t == 3:
                    split_k_or_v(g + 1, "k")
                if t == 0 and wo_due(g):
                    split_wo(g)
                if in_prologue(g):
                    first_splits(t)

            def first_splits(t):
                if t == 5:
                    split_wo(Group(first_group))
                if layer == 0 and t in (2, 3):
                    w.high_wq(act, Group(0), t)
                elif layer == 0 and t == 4:
                    w.high_wv(act, Group(0))

            if layer == 0:
                w.high_wq(act, Group(0), 1)
                w.high_wk(act, Group(0))
            run_steps(act, step)

        @block.gpsimd
        def _(pool):
            def times_sin(g, t, which):
                if (found := unit_at(g, t, which)) is None or found[1][0] not in "qk":
                    return
                g, unit = found
                r = ROPES.index(unit)
                wait_count(pool, sig.rot_ready, g, 2 * NR, 2 * r + 2)
                nc.gpsimd.tensor_tensor(by_batch(rot[:, r % 2, :]), by_batch(rot[:, r % 2, :]), sin(unit[2]), ALU.mult).then_inc(sig.sin_done, 1)

            def step(g, t):
                gb, tb = back(g, t)
                times_sin(gb, tb, 1)
                times_sin(g, t, 0)
                n = norm_step(g, t)
                if 2 <= n < NT + 2:
                    norm.pool_rstd(pool, n - 2)
                if by_pool(gb, tb):
                    pool.wait_ge(o_scaled, tb)
                    nc.gpsimd.tensor_tensor(x_res[:, tb, :], scaled[tb % 2][:], x_res[:, tb, :], ALU.add).then_inc(sig.acc_done, 1)
                if t in SPLIT_Q and weights_due(g + SPLIT_Q[t][0]):
                    w.low_wq(pool, g + SPLIT_Q[t][0], SPLIT_Q[t][1])
                if t == 2 and weights_due(g + 1):
                    w.low_wv(pool, g + 1)
                if t == 3 and weights_due(g + 1):
                    w.low_wk(pool, g + 1)
                if t == 0 and wo_due(g):
                    w.low_wo_pool(pool, g)
                if in_prologue(g):
                    first_splits(t)

            def first_splits(t):
                if t == 5:
                    w.low_wo_pool(pool, Group(first_group))
                if layer == 0 and t == 2:
                    w.low_wq(pool, Group(0), 2)
                    w.low_wk(pool, Group(0))
                elif layer == 0 and t == 3:
                    w.low_wq(pool, Group(0), 3)
                elif layer == 0 and t == 4:
                    w.low_wv(pool, Group(0))

            norm.pool_setup(pool)
            if layer == 0:
                w.low_wq(pool, Group(0), 1)
            run_steps(pool, step)

        @block.vector
        def _(dve):
            def rotary_or_low(g, t, which):
                if (found := unit_at(g, t, which)) is None:
                    return
                g, unit = found
                kind, _, half = unit
                bank = proj_bank[UNITS.index(unit) % 2]
                if kind == "x":
                    wait_count(dve, sig.v_hi, g, 2, half + 1)
                    tiles = slice(NT // 2 * half, NT // 2 * (half + 1))
                    nc.vector.tensor_tensor(v[1][:, tiles, :], bank[:].rearrange("p (t d) -> p t d", d=D), v[0][:, tiles, :].bitcast(F32),
                                            ALU.subtract).then_inc(sig.v_lo, 1)
                if kind not in "qk":
                    return
                r = ROPES.index(unit)
                wait_count(dve, sig.rot_ready, g, 2 * NR, 2 * r + 2)
                wait_count(dve, sig.rope_done, g, NR, r)
                nc.vector.tensor_tensor(by_batch(qcos[:]), by_batch(bank[:]), cos(half), ALU.mult).then_inc(sig.cos_done, 1)
                wait_count(dve, sig.cos_done, g, NR, r + 1)
                wait_count(dve, sig.sin_done, g, NR, r + 1)
                wait_count(dve, sig.s_done, g + -1, NT, NT // 2 * (half + 1))
                nc.vector.tensor_tensor(heads_of(unit), by_batch(qcos[:]), by_batch(rot[:, r % 2, :]), ALU.add).then_inc(sig.rope_done, 1)

            def softmax(g, t, n):
                low, stats = 4 <= n < NT + 4, 2 <= n < NT + 2
                if stats and not in_layer(g):
                    dve.wait_ge(sig.acc_done, (end_group - 1) * NT + n - 1)
                    norm.vector_stats(dve, n - 2, n - 4)
                    return
                if low and not in_layer(g):
                    norm.vector_low(dve, n - 4)
                if not in_layer(g):
                    return
                b = slice(2 * t, 2 * t + 2)
                both_pairs = [P, 2, 2 * SEQ]
                pairs = sc[:].rearrange("p (a n) -> p a n", a=2)
                bank = s_bank[:, 0:256].rearrange("p (a n) -> p a n", a=2)

                def for_tile(mask):
                    return mask[:, b, :].rearrange("p b k -> p (b k)").unsqueeze(1).to_broadcast(both_pairs)

                wait_count(dve, sig.exp_ready, g, NT, t)
                wait_count(dve, sig.s_done, g, NT, t + 1)
                if len(masks) == 2:
                    nc.vector.scalar_tensor_tensor(out=pairs, in0=bank, scalar=SCALE, in1=for_tile(masks[0]),
                                                   op0=ALU.mult, op1=ALU.mult).then_inc(sig.s_read, 1)
                    wait_count(dve, sig.s_read, g, NT, t + 1)
                    nc.vector.scalar_tensor_tensor(out=pairs, in0=for_tile(masks[1]), scalar=-1e9, in1=pairs,
                                                   op0=ALU.mult, op1=ALU.add).then_inc(sig.s_masked, 1)
                    wait_count(dve, sig.s_masked, g, NT, t + 1)
                else:
                    nc.vector.scalar_tensor_tensor(out=pairs, in0=bank, scalar=SCALE, in1=for_tile(masks[0]),
                                                   op0=ALU.mult, op1=ALU.add).then_inc(sig.s_read, 1)
                    wait_count(dve, sig.s_read, g, NT, t + 1)
                rows = [P, 4, SEQ]
                sc4 = by_batch(sc[:])
                pr4 = by_batch(prob[:, t % 2, :])
                nc.vector.reduce_max(mx[:], sc4, AX_X).then_inc(sig.mx_ready, 1)
                wait_count(dve, sig.mx_ready, g, NT, t + 1)
                nc.vector.tensor_tensor(sc4, sc4, mx[:].unsqueeze(2).to_broadcast(rows), ALU.subtract).then_inc(sig.shifted, 1)
                if low:
                    norm.vector_low(dve, n - 4)
                wait_count(dve, sig.exp_ready, g, NT, t + 1)
                nc.vector.reduce_sum(total[:], pr4, AX_X).then_inc(sig.total_ready, 1)
                if stats:
                    dve.wait_ge(sig.acc_done, (end_group - 1) * NT + n - 1)
                    nc.vector.bn_stats(norm.stats[:, n % 2, :], x_res[:, n - 2, :]).then_inc(norm.stats_done, 1)
                wait_count(dve, sig.total_ready, g, NT, t + 1)
                nc.vector.reciprocal(inv[:], total[:]).then_inc(sig.inv_ready, 1)
                if stats:
                    norm.vector_aggregate(dve, n - 2)
                wait_count(dve, sig.inv_ready, g, NT, t + 1)
                nc.vector.tensor_tensor(pr4, pr4, inv[:].unsqueeze(2).to_broadcast(rows), ALU.mult).then_inc(sig.prob_ready, 1)
                if stats:
                    norm.vector_variance(dve, n - 2)

            def probs_low(g, t):
                if not in_layer(g):
                    return
                wait_count(dve, sig.probT_hi, g, NT, t + 1)
                nc.vector.tensor_tensor(probT[1][:, t % 2, :], t_bank[:, 0:256], probT[0][:, t % 2, :].bitcast(F32), ALU.subtract)\
                  .then_inc(sig.probT_lo, 1)

            def heads_low(g, t):
                if not in_layer(g):
                    return
                for b2 in range(2):
                    wait_count(dve, sig.oT_hi, g, 2 * NT, 2 * t + b2 + 1)
                    nc.vector.tensor_tensor(oT[1][:, t % 2, :, b2, :], by_batch(pv_bank[b2][:, 0:256]),
                                            oT[0][:, t % 2, :, b2, :].bitcast(F32), ALU.subtract).then_inc(sig.oT_lo, 1)

            def accumulate(g, t):
                if not in_layer(g) or by_pool(g, t):
                    return
                wait_count(dve, sig.o_done, g, NT, t + 1)
                nc.vector.scalar_tensor_tensor(out=x_res[:, t, :], in0=o_bank[:], scalar=gate, in1=x_res[:, t, :],
                                               op0=ALU.mult, op1=ALU.add).then_inc(sig.acc_done, 1)

            def step(g, t):
                n = norm_step(g, t)
                gb, tb = back(g, t)
                heads_low(gb, tb)
                rotary_or_low(gb, tb, 1)
                probs_low(g, t)
                softmax(*ahead(g, t), n)
                rotary_or_low(g, t, 0)
                accumulate(gb, tb)
                if t == 0 and wo_due(g):
                    w.low_wo_vector(dve, g)
                if t == 6 and in_prologue(g):
                    w.low_wo_vector(dve, Group(first_group))
                if int_range:
                    int_range.look(dve, g, t)

            if int_range:
                int_range.setup(dve)
            run_steps(dve, step)


def low_rank_phase(nc, sems, a_nat, wr_nat, b_nat, br, prefetched, mask_in, x_mask, x_res, xn_parts, gates, ident):
    RD = RH * RR
    with ExitStack() as c:
        m = Chip(nc, c)
        aT, wrT = m.parts("lr_aT", [P, KC, RD]), m.parts("lr_wrT", [P, KC, RH])
        bT = m.sb("lr_bT", [P, DM])
        spread = m.sb("lr_spread", [RH, RH, RR])
        low, low_scored = m.sb("lr_low", [P, TOK]), m.sb("lr_low_scored", [P, TOK])
        logitT, scoreT = m.sb("lr_logitT", [RH, TOK]), m.sb("lr_scoreT", [RH, TOK])
        logit, shifted, expd, score = (m.sb("lr_" + n, [P, NT, RH]) for n in ("logit", "shifted", "expd", "score"))
        mx, total, inv = (m.sb("lr_" + n, [P, NT]) for n in ("mx", "total", "inv"))
        gate = m.sb("lr_gate", [P, 1])
        ring, scaled = m.sb("lr_ring", [P, 2, DM]), m.sb("lr_scaled", [P, 2, DM])
        tr, low_bank, r_bank, o_bank = ([m.bank(f"lr_{n}{i}") for i in range(2)] for n in ("tr", "low", "r", "o"))
        norm = Norm(nc, sems, m, "n2_", x_res, xn_parts, ring, tr, ident)
        wt_tr, wt_hi, wt_lo, bT_ready, router_done, logitT_ready, low_done, low_ready, rows_tr, chain, scores_tr, scoreT_ready, spread_ready, spread_done = (
            sems("lr_" + n) for n in ("wt_tr", "wt_hi", "wt_lo", "bT", "router", "logitT", "low_done", "low_ready", "rows_tr", "chain",
                                      "scores_tr", "scoreT", "spread", "spread_done"))
        low_scored_ready, o_done, o_scaled, added, gate_ready, mask_loaded = (
            sems("lr_" + n) for n in ("low_scored", "o_done", "o_scaled", "added", "gate", "mask"))
        block = c.enter_context(nc.Block())
        WT = ((tr[0][:, 0:KC * RD], aT), (tr[1][:, 0:KC * RH], wrT))

        def columns(half):
            return slice(half * HALF, (half + 1) * HALF)

        @block.sync
        def _(sp):
            for half in range(2):
                sp.dma_start(x_mask[half * SEQ:(half + 1) * SEQ], mask_in.rearrange("b q k -> q b k")).then_inc(mask_loaded, 16)
            sp.wait_ge(mask_loaded, 32)

        @block.tensor
        def _(pe):
            def products(bank, weights, half):
                for k in range(KC):
                    for n, (a, b) in enumerate(PASSES):
                        last = nc.tensor.matmul(bank, weights[a][:, k, :], xn_parts[b][:, k, columns(half)],
                                                start=(k == 0 and n == 0), stop=(k == KC - 1 and n == 2))
                return last

            pe.wait_ge(prefetched, PREFETCHED_LOW_RANK)
            for k in range(KC):
                last = nc.tensor.transpose(tr[1][:, k * RH:(k + 1) * RH], wr_nat[:, k * P:(k + 1) * P], ident[0:RH, 0:RH])
            last.then_inc(wt_tr, 1)
            for k in range(KC):
                last = nc.tensor.transpose(tr[0][:, k * P:(k + 1) * P], a_nat[:, k * P:(k + 1) * P], ident[:])
            last.then_inc(wt_tr, 1)
            for k in range(KC):
                last = nc.tensor.transpose(o_bank[0][:, k * P:(k + 1) * P], b_nat[:, k * RD:(k + 1) * RD], ident[:])
            last.then_inc(wt_tr, 1)
            pe.wait_ge(wt_lo, 1)
            for half in range(2):
                products(r_bank[half][0:RH, :], wrT, half).then_inc(router_done, 1)
            pe.wait_ge(wt_lo, 2)
            products(low_bank[0][:], aT, 0).then_inc(low_done, 1)
            pe.wait_ge(logitT_ready, 2)
            for t in range(NT):
                last = nc.tensor.transpose(o_bank[1][:, t * RH:(t + 1) * RH], logitT[:, t * P:(t + 1) * P], ident[0:RH, 0:RH])
            last.then_inc(rows_tr, 1)
            products(low_bank[1][:], aT, 1).then_inc(low_done, 1)
            pe.wait_ge(chain, 7)
            for t in range(NT):
                last = nc.tensor.transpose(r_bank[t * P // HALF][0:RH, t * P % HALF:t * P % HALF + P], score[:, t, :], ident[:])
            last.then_inc(scores_tr, 1)
            pe.wait_ge(spread_ready, 1)
            for half in range(2):
                pe.wait_ge(scoreT_ready, half + 1)
                nc.tensor.matmul(tr[half][:], spread[:].rearrange("e h r -> e (h r)"), scoreT[:, columns(half)], start=True, stop=True)\
                  .then_inc(spread_done, 1)
            pe.wait_ge(bT_ready, 1)
            for t in range(NT + 3):
                if t < NT:
                    pe.wait_ge(low_scored_ready, t // (NT // 2) + 1)
                    if t >= 2:
                        pe.wait_ge(o_scaled, t - 1)
                    nc.tensor.matmul(o_bank[t % 2][:], low_scored[:, t * P:(t + 1) * P], bT[:], start=True, stop=True).then_inc(o_done, 1)
                if t >= 3:
                    if t == 3:
                        pe.wait_ge(low_scored_ready, 2)
                    norm.tensor_transpose(pe, t - 3)

        @block.scalar
        def _(act):
            for n in (1, 0):
                bank, weights = WT[n]
                act.wait_ge(wt_tr, 2 - n)
                nc.scalar.activation(weights[0][:].rearrange("p c n -> p (c n)"), bank, ACT.Copy).then_inc(wt_hi, 1)
            act.wait_ge(wt_tr, 3)
            nc.scalar.activation(bT[:], o_bank[0][:], ACT.Copy).then_inc(bT_ready, 1)
            for half in range(2):
                act.wait_ge(router_done, half + 1)
                nc.scalar.activation(logitT[:, columns(half)], r_bank[half][0:RH, :], ACT.Copy).then_inc(logitT_ready, 1)
            act.wait_ge(low_done, 1)
            nc.scalar.activation(low[:, columns(0)], low_bank[0][:], ACT.Copy).then_inc(low_ready, 1)
            act.wait_ge(chain, 3)
            nc.scalar.activation(expd[:], shifted[:], ACT.Exp).then_inc(chain, 1)
            act.wait_ge(low_done, 2)
            nc.scalar.activation(low[:, columns(1)], low_bank[1][:], ACT.Copy).then_inc(low_ready, 1)
            act.wait_ge(scores_tr, 1)
            for half in range(2):
                nc.scalar.activation(scoreT[:, columns(half)], r_bank[half][0:RH, :], ACT.Copy).then_inc(scoreT_ready, 1)
            act.wait_ge(gate_ready, 1)
            for t in range(NT + 3):
                if t < NT:
                    act.wait_ge(o_done, t + 1)
                    if t >= 2:
                        act.wait_ge(added, t - 1)
                    nc.scalar.activation(scaled[:, t % 2, :], o_bank[t % 2][:], ACT.Copy, scale=gate[:, 0:1]).then_inc(o_scaled, 1)
                if 2 <= t < NT + 2:
                    norm.scalar_apply(act, t - 2)
                if t >= 3:
                    norm.scalar_high(act, t - 3)

        @block.gpsimd
        def _(pool):
            norm.pool_setup(pool)
            for t in range(NT + 1):
                if t < NT:
                    pool.wait_ge(o_scaled, t + 1)
                    nc.gpsimd.tensor_tensor(x_res[:, t, :], scaled[:, t % 2, :], x_res[:, t, :], ALU.add).then_inc(added, 1)
                if t >= 1:
                    norm.pool_rstd(pool, t - 1)

        @block.vector
        def _(dve):
            nc.vector.tensor_scalar(gate[:], gates[:, 2:3], float(2 * RH), None, ALU.mult).then_inc(gate_ready, 1)
            nc.vector.tensor_copy(spread[:], ident[0:RH, 0:RH].unsqueeze(2).to_broadcast([RH, RH, RR])).then_inc(spread_ready, 1)
            for done, n in enumerate((1, 0)):
                bank, weights = WT[n]
                dve.wait_ge(wt_hi, done + 1)
                nc.vector.tensor_tensor(weights[1][:].rearrange("p c n -> p (c n)"), bank, weights[0][:].rearrange("p c n -> p (c n)").bitcast(F32),
                                        ALU.subtract).then_inc(wt_lo, 1)
            tiles = [P, NT, RH]
            dve.wait_ge(prefetched, PREFETCHED_LOW_RANK)
            dve.wait_ge(rows_tr, 1)
            nc.vector.tensor_tensor(logit[:], o_bank[1][:, 0:NT * RH].rearrange("p (t h) -> p t h", h=RH), br.unsqueeze(1).to_broadcast(tiles),
                                    ALU.add).then_inc(chain, 1)
            dve.wait_ge(chain, 1)
            nc.vector.reduce_max(mx[:], logit[:], AX_X).then_inc(chain, 1)
            dve.wait_ge(chain, 2)
            nc.vector.tensor_tensor(shifted[:], logit[:], mx[:].unsqueeze(2).to_broadcast(tiles), ALU.subtract).then_inc(chain, 1)
            dve.wait_ge(chain, 4)
            nc.vector.reduce_sum(total[:], expd[:], AX_X).then_inc(chain, 1)
            dve.wait_ge(chain, 5)
            nc.vector.reciprocal(inv[:], total[:]).then_inc(chain, 1)
            dve.wait_ge(chain, 6)
            nc.vector.tensor_tensor(score[:], expd[:], inv[:].unsqueeze(2).to_broadcast(tiles), ALU.mult).then_inc(chain, 1)
            for half in range(2):
                dve.wait_ge(low_ready, half + 1)
                dve.wait_ge(spread_done, half + 1)
                nc.vector.tensor_tensor(low_scored[:, columns(half)], tr[half][:], low[:, columns(half)], ALU.mult).then_inc(low_scored_ready, 1)
            for t in range(NT + 4):
                if t < NT:
                    dve.wait_ge(added, t + 1)
                    norm.vector_stats(dve, t, t - 4)
                else:
                    norm.vector_low(dve, t - 4)


class Plan:

    def __init__(self, passes, down_passes, split):
        self.passes, self.down_passes, self.split = passes, down_passes, split


def ternary_phase(nc, sems, gate_in, up_in, down_in, down_s_in, first_pair, scales_nat, largest, prefetched, x_res,
                  xn_parts, gates, out, ident):
    with ExitStack() as c:
        m = Chip(nc, c)
        nat_i = m.sb("nat_i", [P, 3, 2 * DM], I32)
        nat = m.sb("nat", [P, 3, 2 * DM])
        widest, row_max = m.sb("widest", [P, 1]), m.sb("row_max", [1, 1])
        wide = m.sb("wide", [1, 1], I32)
        w_parts = [[m.sb(f"{w}T_{n}", [P, 2, DM], F32R) for n in ("hi", "lo")] for w in ("gate", "up", "down")]
        hid_parts = [m.sb(f"hid_{n}", [P, 2, TOK], F32R) for n in ("hi", "lo")]
        silu = m.sb("silu", [P, 2, HALF])
        hid = m.sb("hid", [P, 2, HALF])
        acc = m.sb("acc", [P, NT, DM])
        scales = m.sb("ff_scales", [P, 2, FFT])
        pair_scale = m.sb("pair_scale", [P, 2])
        down_s = m.sb("down_s", [P, DM])
        down_sg = m.sb("down_sg", [P, DM])
        tr = [m.bank(f"ff_tr{i}") for i in range(2)]
        g_bank = [m.bank(f"ff_g{i}") for i in range(2)]
        u_bank = [m.bank(f"ff_u{i}") for i in range(2)]
        d_bank = [m.bank(f"ff_d{i}") for i in range(2)]
        loaded = [sems(f"ff_loaded{i}") for i in range(3)]
        scales_tr, scales_ready, down_s_loaded, pair_scale_ready = (
            sems("ff_" + n) for n in ("scales_tr", "scales_ready", "down_s", "pair_scale"))
        cast, tr_done, w_hi, w_lo, prod_done, silu_ready, hid_ready, h_hi, h_lo, d_done, acc_done, acc_zero, down_s_ready, others_added, widest_done, widest_tr, table_loaded, final, final_pool, written = (
            sems("ff_" + n) for n in ("cast", "tr", "w_hi", "w_lo", "prod", "silu", "hid", "h_hi", "h_lo", "d", "acc", "acc_zero", "down_s_ready", "others", "widest",
                                      "widest_tr", "table", "final", "final_pool", "written"))
        gate_v = gate_in.rearrange("(f p) d -> p f d", p=P)
        up_v = up_in.rearrange("(f p) d -> p f d", p=P)
        down_v = down_in.rearrange("(c p) f -> p c f", p=P)

        TR = [(0, 0), (1, 0), (0, 1), (1, 1), (2, 0), (2, 1)]
        UNITS_FF = [(0, 0), (1, 0), (0, 1), (1, 1)]
        BY_POOL = (1, 3, 5)
        WIDE = Plan(PASSES, PASSES, w_lo)
        NARROW = Plan(PASSES[0:2], (PASSES[0], PASSES[2]), w_hi)
        block = c.enter_context(nc.Block())

        class Pair(Group):
            def valid(self):
                return self.register is not None or 0 <= self.added < NFP

        def run_pairs(eng, iteration):
            iteration(Pair(0))
            with eng.Fori(1, NFP - 1) as i:
                iteration(Pair(0, i))
            iteration(Pair(NFP - 1))

        def nxt(i, n=1):
            return Pair(i.added + n, i.register, i.least)

        @block.sync
        def _(sp):
            def load(i):
                if not i.valid():
                    return
                wait_count(sp, cast, i, 3, 0)
                for n, view in enumerate((gate_v, up_v)):
                    if i.register is not None or i.added > 0:
                        sp.dma_start(nat_i[:, n].rearrange("p (f d) -> p f d", f=2), view[:, bass.ds(i.number(2, 0), 2), :])\
                          .then_inc(loaded[n], 16)
                sp.dma_start(nat_i[:, 2].rearrange("p (c f) -> p c f", c=KC), down_v[:, :, bass.ds(i.number(2 * P, 0), 2 * P)]).then_inc(loaded[2], 16)

            load(Pair(0))
            sp.dma_start(down_s[:], down_s_in.unsqueeze(0).to_broadcast([P, DM])).then_inc(down_s_loaded, 16)
            load(Pair(1))
            with sp.Fori(1, NFP - 1) as i:
                load(Pair(1, i))
            for t in range(NT):
                if t in BY_POOL:
                    sp.wait_ge(final_pool, BY_POOL.index(t) + 1)
                else:
                    sp.wait_ge(final, [u for u in range(NT) if u not in BY_POOL].index(t) + 1)
                sp.dma_start(out[t * P:(t + 1) * P, :], x_res[:, t, :]).then_inc(written, 16)
            sp.wait_ge(written, 16 * NT)

        @block.tensor
        def _(pe):
            def transpose(i, n, plan=WIDE):
                if not i.valid():
                    return
                w, f = TR[n]
                wait_count(pe, cast, i, 3, w + 1)
                wait_count(pe, plan.split, i, len(TR), n - 1)
                for k in range(KC):
                    if w < 2:
                        src = nat[:, w, f * DM + k * P:f * DM + (k + 1) * P]
                    else:
                        src = nat[:, w, k * 2 * P + f * P:k * 2 * P + (f + 1) * P]
                    last = nc.tensor.transpose(tr[n % 2][:, k * P:(k + 1) * P], src, ident[:])
                last.then_inc(tr_done, 1)

            def products(i, n, plan):
                f, half = UNITS_FF[n]
                wait_count(pe, plan.split, i, len(TR), 2 * f + 2)
                wait_count(pe, hid_ready, i, 4, n - 1)
                for w, bank in ((0, g_bank), (1, u_bank)):
                    for k in range(KC):
                        for q, (a, b) in enumerate(plan.passes):
                            last = nc.tensor.matmul(bank[n % 2][:], w_parts[w][a][:, f, k * P:(k + 1) * P],
                                                    xn_parts[b][:, k, half * HALF:(half + 1) * HALF],
                                                    start=(k == 0 and q == 0), stop=(k == KC - 1 and q == len(plan.passes) - 1))
                last.then_inc(prod_done, 1)

            def down(i, first_tile, plan):
                if not i.valid():
                    return
                wait_count(pe, plan.split, i, len(TR), 6)
                wait_count(pe, h_lo, i, 4, 2 * (first_tile // (NT // 2)) + 2)
                for t in range(first_tile, first_tile + 2):
                    wait_count(pe, acc_done, i, NT, t - 1)
                    for f in range(2):
                        for q, (a, b) in enumerate(plan.down_passes):
                            last = nc.tensor.matmul(d_bank[t % 2][:], hid_parts[a][:, f, t * P:(t + 1) * P], w_parts[2][b][:, f, :],
                                                    start=(f == 0 and q == 0), stop=(f == 1 and q == len(plan.down_passes) - 1))
                    last.then_inc(d_done, 1)

            def iteration(i, plan):
                products(i, 0, plan)
                down(nxt(i, -1), 4, plan)
                transpose(i, 2, plan)
                transpose(i, 3, plan)
                down(nxt(i, -1), 6, plan)
                transpose(i, 4, plan)
                transpose(i, 5, plan)
                products(i, 1, plan)
                products(i, 2, plan)
                if i.register is None and i.added == NFP - 1:
                    products(i, 3, plan)
                    down(i, 0, plan)
                    down(i, 2, plan)
                else:
                    down(i, 0, plan)
                    transpose(nxt(i), 0, plan)
                    transpose(nxt(i), 1, plan)
                    down(i, 2, plan)
                    products(i, 3, plan)

            def feed_forward(plan):
                run_pairs(pe, lambda i: iteration(i, plan))
                down(Pair(NFP - 1), 4, plan)
                down(Pair(NFP - 1), 6, plan)

            pe.wait_ge(widest_done, 1)
            nc.tensor.transpose(d_bank[1][0:1, 0:P], widest[:], ident[:]).then_inc(widest_tr, 1)
            pe.wait_ge(prefetched, PREFETCHED)
            for n in range(2):
                last = nc.tensor.transpose(d_bank[0][:, n * FFT:(n + 1) * FFT], scales_nat[:, n, :], ident[0:FFT, 0:FFT])
            last.then_inc(scales_tr, 1)
            transpose(Pair(0), 0)
            transpose(Pair(0), 1)
            pe.wait_ge(widest_done, 3)
            is_wide = pe.value_load(wide[:], min_val=0, max_val=1)
            with pe.If(is_wide != 0):
                feed_forward(WIDE)
            with pe.Else():
                feed_forward(NARROW)

        @block.scalar
        def _(act):
            def high_part(i, n):
                if not i.valid():
                    return
                w, f = TR[n]
                wait_count(act, tr_done, i, len(TR), n + 1)
                nc.scalar.activation(w_parts[w][0][:, f, :], tr[n % 2][:], ACT.Copy).then_inc(w_hi, 1)

            def silu_of(i, n):
                f = UNITS_FF[n][0]
                wait_count(act, pair_scale_ready, i, 1, 1)
                wait_count(act, prod_done, i, 4, n + 1)
                nc.scalar.activation(silu[:, n % 2, :], g_bank[n % 2][:], ACT.Silu, scale=pair_scale[:, f:f + 1]).then_inc(silu_ready, 1)

            def hidden_high(i, n):
                f, half = UNITS_FF[n]
                wait_count(act, hid_ready, i, 4, n + 1)
                wait_count(act, d_done, i, NT, NT // 2 * (half + 1) - NT)
                nc.scalar.activation(hid_parts[0][:, f, half * HALF:(half + 1) * HALF], hid[:, n % 2, :], ACT.Copy).then_inc(h_hi, 1)

            def iteration(i):
                nc.scalar.activation(pair_scale[:], scales[:, 0, bass.ds(i.number(2, 0), 2)], ACT.Copy).then_inc(pair_scale_ready, 1)
                silu_of(i, 0)
                if i.register is None and i.added == 0:
                    high_part(i, 2)
                    high_part(i, 3)
                    hidden_high(i, 0)
                else:
                    hidden_high(i, 0)
                    high_part(i, 2)
                    high_part(i, 3)
                high_part(i, 4)
                high_part(i, 5)
                silu_of(i, 1)
                hidden_high(i, 1)
                silu_of(i, 2)
                hidden_high(i, 2)
                if not (i.register is None and i.added == NFP - 1):
                    high_part(nxt(i), 0)
                    high_part(nxt(i), 1)
                silu_of(i, 3)
                hidden_high(i, 3)

            act.wait_ge(scales_tr, 1)
            nc.scalar.activation(scales[:], d_bank[0][:, 0:2 * FFT].rearrange("p (n f) -> p n f", n=2), ACT.Copy).then_inc(scales_ready, 1)
            act.wait_ge(scales_ready, 1)
            high_part(Pair(0), 0)
            high_part(Pair(0), 1)
            nc.scalar.activation(silu[:, 1, 0:1], scales[:, 0, 0:1], ACT.Silu).then_inc(table_loaded, 1)
            act.wait_ge(table_loaded, 1)
            run_pairs(act, iteration)

        @block.gpsimd
        def _(pool):
            nc.gpsimd.memset(acc[:], 0.0).then_inc(acc_zero, 1)
            pool.wait_ge(down_s_ready, 1)
            for t in range(NT):
                pool.wait_ge(acc_done, NT * (NFP - 2) + t + 1)
                nc.gpsimd.tensor_tensor(acc[:, t, :], acc[:, t, :], down_sg[:], ALU.mult).then_inc(others_added, 1)
                pool.wait_ge(others_added, 2 * t + 1)
                nc.gpsimd.tensor_tensor(x_res[:, t, :], acc[:, t, :], x_res[:, t, :], ALU.add).then_inc(others_added, 1)
            for t in BY_POOL:
                pool.wait_ge(others_added, 2 * t + 2)
                pool.wait_ge(acc_done, NT * (NFP - 1) + t + 1)
                nc.gpsimd.tensor_tensor(x_res[:, t, :], acc[:, t, :], x_res[:, t, :], ALU.add).then_inc(final_pool, 1)

        @block.vector
        def _(dve):
            def cast_to_float(i, n):
                wait_count(dve, loaded[n], i, 16, 16 if n == 2 else 0)
                wait_count(dve, tr_done, i, len(TR), (-2, -2, 0)[n])
                first = n < 2 and i.register is None and i.added == 0
                nc.vector.tensor_copy(nat[:, n], first_pair[n] if first else nat_i[:, n]).then_inc(cast, 1)

            def low_of_weights(i, n):
                if not i.valid():
                    return
                w, f = TR[n]
                wait_count(dve, w_hi, i, len(TR), n + 1)
                nc.vector.tensor_tensor(w_parts[w][1][:, f, :], tr[n % 2][:], w_parts[w][0][:, f, :].bitcast(F32), ALU.subtract).then_inc(w_lo, 1)

            def hidden(i, n):
                hidden_product(i, n)
                hidden_low(i, n)

            def hidden_product(i, n):
                f, half = UNITS_FF[n]
                wait_count(dve, silu_ready, i, 4, n + 1)
                wait_count(dve, h_lo, i, 4, n - 1)
                scale = scales[:, 1, bass.ds(i.number(2, f), 1)]
                nc.vector.scalar_tensor_tensor(out=hid[:, n % 2, :], in0=u_bank[n % 2][:], scalar=scale, in1=silu[:, n % 2, :],
                                               op0=ALU.mult, op1=ALU.mult).then_inc(hid_ready, 1)

            def hidden_low(i, n):
                f, half = UNITS_FF[n]
                cols = slice(half * HALF, (half + 1) * HALF)
                wait_count(dve, h_hi, i, 4, n + 1)
                nc.vector.tensor_tensor(hid_parts[1][:, f, cols], hid[:, n % 2, :], hid_parts[0][:, f, cols].bitcast(F32),
                                        ALU.subtract).then_inc(h_lo, 1)

            def accumulate(i, t):
                if not i.valid():
                    return
                wait_count(dve, d_done, i, NT, t + 1)
                if not (i.register is None and i.added == NFP - 1):
                    nc.vector.tensor_tensor(acc[:, t, :], d_bank[t % 2][:], acc[:, t, :], ALU.add).then_inc(acc_done, 1)
                    return
                dve.wait_ge(others_added, 2 * t + 2)
                nc.vector.tensor_tensor(acc[:, t, :], d_bank[t % 2][:], down_sg[:], ALU.mult).then_inc(acc_done, 1)
                dve.wait_ge(acc_done, NT * (NFP - 1) + t + 1)
                if t not in BY_POOL:
                    nc.vector.tensor_tensor(x_res[:, t, :], acc[:, t, :], x_res[:, t, :], ALU.add).then_inc(final, 1)

            def iteration(i, plan):
                last = i.register is None and i.added == NFP - 1

                def low_part(i, n):
                    if plan is WIDE:
                        low_of_weights(i, n)

                hidden_product(i, 0)
                accumulate(nxt(i, -1), 4)
                accumulate(nxt(i, -1), 5)
                hidden_low(i, 0)
                low_part(i, 2)
                low_part(i, 3)
                accumulate(nxt(i, -1), 6)
                accumulate(nxt(i, -1), 7)
                low_part(i, 4)
                low_part(i, 5)
                if not last:
                    for n in range(3):
                        cast_to_float(nxt(i), n)
                hidden(i, 1)
                if last:
                    hidden(i, 2)
                    hidden(i, 3)
                    for t in range(NT // 2):
                        accumulate(i, t)
                    return
                hidden_product(i, 2)
                accumulate(i, 0)
                accumulate(i, 1)
                hidden_low(i, 2)
                low_part(nxt(i), 0)
                low_part(nxt(i), 1)
                accumulate(i, 2)
                accumulate(i, 3)
                hidden(i, 3)

            nc.vector.reduce_max(widest[:], largest[:, 0, :], AX_X).then_inc(widest_done, 1)
            dve.wait_ge(prefetched, PREFETCHED)
            for n in range(2):
                cast_to_float(Pair(0), n)
            dve.wait_ge(widest_tr, 1)
            nc.vector.reduce_max(row_max[:], d_bank[1][0:1, 0:P], AX_X).then_inc(widest_done, 1)
            dve.wait_ge(widest_done, 2)
            nc.vector.tensor_scalar(wide[:], row_max[:], EXACT_IN_HIGH_PART, None, ALU.is_gt).then_inc(widest_done, 1)
            def feed_forward(plan):
                if plan is WIDE:
                    low_of_weights(Pair(0), 0)
                    low_of_weights(Pair(0), 1)
                run_pairs(dve, lambda i: iteration(i, plan))
                for t in range(4, NT):
                    accumulate(Pair(NFP - 1), t)

            cast_to_float(Pair(0), 2)
            dve.wait_ge(down_s_loaded, 16)
            nc.vector.tensor_scalar(down_sg[:], down_s[:], gates[:, 3:4], None, ALU.mult).then_inc(down_s_ready, 1)
            dve.wait_ge(scales_ready, 1)
            dve.wait_ge(acc_zero, 1)
            dve.wait_ge(down_s_ready, 1)
            dve.wait_ge(widest_done, 3)
            is_wide = dve.value_load(wide[:], min_val=0, max_val=1)
            with dve.If(is_wide != 0):
                feed_forward(WIDE)
            with dve.Else():
                feed_forward(NARROW)


def flamingo(nc, a, out):
    with ExitStack() as c:
        m = Chip(nc, c)
        in_use, lasting = [], []

        def sems(name):
            in_use.append(nc.alloc_semaphore(name=name))
            return in_use[-1]

        def lasting_sem(name):
            lasting.append(nc.alloc_semaphore(name=name))
            return lasting[-1]

        def phase_ends():
            nc.clear_and_free_semaphores(in_use)
            in_use.clear()
            nc.all_engine_barrier()

        x_res = m.sb("x_res", [P, NT, DM])
        ctx_parts = m.parts("ctxT", [P, KC, TOK])
        xn_parts = m.parts("xnT", [P, KC, TOK])
        tables = m.sb("tables", [P, 2, TOK])
        rope1 = m.sb("rope1", [P, 2, SEQ])
        ident = m.sb("ident", [P, P])
        gates = m.sb("gates", [P, 4])
        scales_nat = m.sb("scales_nat", [FFT, 2, P])
        largest = m.sb("largest", [P, 2, TernaryRange.PER_GROUP])
        prefetched = lasting_sem("prefetched")
        a_nat, wr_nat = tables[:, 0, 0:DM], tables[0:RH, 0, DM:2 * DM]
        b_nat, br = tables[:, 1, 0:DM], tables[:, 1, DM:DM + RH]
        integers = [tables[:, n, :].bitcast(I32) for n in range(2)]
        gate_in, up_in, down_in = (a[f"L1_ffn_{n}_t"] for n in ("gate", "up", "down"))

        def prefetch_low_rank(sp):
            sp.dma_start(a_nat, a["L0_ffn_A"].rearrange("h r d -> (h r) d")).then_inc(prefetched, 16)
            sp.dma_start(wr_nat, a["L0_ffn_Wr"]).then_inc(prefetched, 16)
            sp.dma_start(br, a["L0_ffn_br"].unsqueeze(0).to_broadcast([P, RH])).then_inc(prefetched, 16)
            b_rows = b_nat.rearrange("p (c h r) -> p c h r", c=KC, h=RH)
            for e in range(RH):
                sp.dma_start(b_rows[:, :, e, :], a["L0_ffn_B"][e].rearrange("(c p) r -> p c r", p=P)).then_inc(prefetched, 16)

        def prefetch_ternary(sp):
            for n, name in enumerate(("gate", "up")):
                sp.dma_start(scales_nat[:, n, :], a[f"L1_ffn_{name}_s"].rearrange("(f p) -> f p", p=P)).then_inc(prefetched, 16)

        def half_of(n):
            return lambda half: tables[:, n, half * HALF:(half + 1) * HALF].rearrange("p (b s) -> p b s", s=SEQ)

        def every_batch(n):
            return lambda half: rope1[:, n, :].unsqueeze(1).to_broadcast([P, BATCH // 2, SEQ])

        with ExitStack() as during_attention:
            m2 = Chip(nc, during_attention)
            x_mask = m2.sb("mask", [P, BATCH, SEQ])
            hidden, shown = (m2.sb(n, [P, BATCH, SEQ], U8) for n in ("hidden", "shown"))
            w = Weights(nc, m2, lasting_sem, [[a[f"L0_xattn_W{n}"] for n in "qkvo"], [a[f"L1_xattn_w{n}"] for n in "qkvo"]])
            sig = AttentionSignals(lasting_sem)
            load_phase(nc, sems, w, a["ctx_4096"].rearrange("b s d -> (b s) d"), a["x"].rearrange("b s d -> (b s) d"),
                       a["pos_BxS2"].rearrange("b s -> (b s)").unsqueeze(0).to_broadcast([P, TOK]), a["tables"], a["table1"],
                       a["g_xattn"].unsqueeze(0).to_broadcast([P, 2]), a["g_ffn"].unsqueeze(0).to_broadcast([P, 2]),
                       a["mask_BxSxS2_ik0"], x_res, ctx_parts, xn_parts, tables, rope1, x_mask, hidden, shown, gates, ident)
            phase_ends()
            attention_phase(nc, sems, 0, w, sig, (shown, hidden), half_of(0), half_of(1), gates[:, 0:1], x_res, xn_parts, ctx_parts,
                            prefetch_low_rank, None, ident)
            phase_ends()
            low_rank_phase(nc, sems, a_nat, wr_nat, b_nat, br, prefetched, a["mask_BxSxS2_ff0"], x_mask, x_res, xn_parts, gates, ident)
            phase_ends()
            int_range = TernaryRange(nc, lasting_sem, NG, integers, largest, gate_in, up_in, down_in)
            attention_phase(nc, sems, 1, w, sig, (x_mask,), every_batch(0), every_batch(1), gates[:, 1:2], x_res, xn_parts, ctx_parts,
                            prefetch_ternary, int_range, ident)
            phase_ends()
        ternary_phase(nc, sems, gate_in, up_in, down_in, a["L1_ffn_down_s"], integers, scales_nat, largest,
                      prefetched, x_res, xn_parts, gates, out, ident)
        in_use.extend(lasting)
        phase_ends()


def rotary_tables():
    import numpy as np

    inv_freq = (1.0 / 10000.0 ** (np.arange(0, D, 2, dtype=np.float32) / np.float32(D))).astype(np.float32)
    angle = np.arange(MAX_POS, dtype=np.float32)[:, None] * inv_freq[None, :]
    cos, sin = np.cos(angle).astype(np.float32), np.sin(angle).astype(np.float32)
    cos, sin = np.concatenate([cos, cos], 1), np.concatenate([-sin, sin], 1)
    both = np.stack([cos, sin], 1)
    chunks = both.reshape(MAX_POS // P, P, 2, D).transpose(1, 0, 2, 3)
    return np.ascontiguousarray(chunks), np.ascontiguousarray(both[:SEQ].transpose(2, 1, 0))


_INS = ['x', 'ctx_4096', 'pos_BxS2', 'mask_BxSxS2_ik0', 'mask_BxSxS2_ff0', 'g_xattn', 'g_ffn', 'L0_xattn_Wq', 'L0_xattn_Wk',
        'L0_xattn_Wv', 'L0_xattn_Wo', 'L0_ffn_A', 'L0_ffn_B', 'L0_ffn_Wr', 'L0_ffn_br', 'L1_xattn_wq', 'L1_xattn_wk', 'L1_xattn_wv',
        'L1_xattn_wo', 'L1_ffn_gate_t', 'L1_ffn_up_t', 'L1_ffn_down_t', 'L1_ffn_gate_s', 'L1_ffn_up_s', 'L1_ffn_down_s']


def kernel(**inputs):
    import numpy as _np
    import concourse.bacc as _bacc
    from concourse import mybir as _mybir
    from concourse.bass_utils import run_bass_kernel_spmd as _run

    nc = _bacc.Bacc("TRN2", target_bir_lowering=False, num_devices=1)
    arrays = {name: _np.ascontiguousarray(inputs[name]) for name in _INS}
    arrays["tables"], arrays["table1"] = rotary_tables()
    aps = {name: nc.dram_tensor(f"in_{name}", x.shape, _mybir.dt.from_np(x.dtype), kind="ExternalInput").ap() for name, x in arrays.items()}
    out = nc.dram_tensor("out", (TOK, DM), _mybir.dt.float32, kind="ExternalOutput").ap()
    flamingo(nc, aps, out)
    r = _run(nc, [{f"in_{name}": x for name, x in arrays.items()}], core_ids=[0])
    return r.results[0]["out"].reshape(BATCH, SEQ, DM)
```
